# Optimizing a Trainium2 kernel written in Bass

```python
import numpy as np
import jax
import jax.numpy as jnp

def _softmax(x, axis=-1):
    return jax.nn.softmax(x, axis=axis)

def _gelu(x):
    return jax.nn.gelu(x, approximate=True)

def _silu(x):
    return jax.nn.silu(x)

def _sigmoid(x):
    return jax.nn.sigmoid(x)

def _layernorm(x, axis=-1, eps=1e-05):
    m = jnp.mean(x, axis=axis, keepdims=True)
    v = jnp.var(x, axis=axis, keepdims=True)
    return (x - m) / jnp.sqrt(v + eps)

def _scatter_add(tgt, idx, src, axis=0):
    return tgt.at[idx].add(src)

def _segment_sum(src, seg, n):
    return jax.ops.segment_sum(src, seg, n)
kernel_name = 'mk_gnn_resnorm_d2_gnn_r32_fd6e8e'

def setup_inputs(seed: int=0):
    np.random.seed(seed)
    _w = jnp.asarray

    def _rec_inputs():
        import jax
        import jax.numpy as jnp
        _gk = jax.random.key(seed)
        x = -0.0005121 + 1.001 * jax.random.normal(jax.random.fold_in(_gk, 1), (3125, 64), jnp.float32)
        src = jax.random.randint(jax.random.fold_in(_gk, 2), (100000,), 0, 3125, jnp.int32)
        dst = jax.random.randint(jax.random.fold_in(_gk, 3), (100000,), 0, 3125, jnp.int32)
        _o = jnp.argsort(dst, stable=True)
        src = src[_o]
        dst = dst[_o]
        return (x, src, dst)
    x, src, dst = _rec_inputs()

    def _L0_gnn_setup():
        import jax, jax.numpy as jnp
        import numpy as np
        NEG_SLOPE = 0.2

        def gatv2_layer(x, src, dst, Wl, Wr, att, bias, n_nodes, heads):
            N, Din = x.shape
            Dh = Wl.shape[1] // heads
            xl = (x @ Wl).reshape(N, heads, Dh)
            xr = (x @ Wr).reshape(N, heads, Dh)
            e = jax.nn.leaky_relu(xl[src] + xr[dst], NEG_SLOPE)
            logits = jnp.einsum('ehd,hd->eh', e, att)
            m = jax.ops.segment_max(logits, dst, num_segments=n_nodes)
            a = jnp.exp(logits - m[dst])
            denom = jax.ops.segment_sum(a, dst, num_segments=n_nodes)
            alpha = a / denom[dst]
            out = jax.ops.segment_sum(alpha[:, :, None] * xl[src], dst, num_segments=n_nodes)
            return out.mean(axis=1) + bias
        key = jax.random.key(seed)
        ks = jax.random.split(key, 12)
        N, E, D, H1, H2 = (50000, 25000, 64, 8, 4)
        x = jax.random.normal(ks[0], (N, D), dtype=jnp.float32)
        edge_index = jax.random.randint(ks[1], (2, E), 0, N, dtype=jnp.int64)
        s = 1.0 / np.sqrt(D)
        W1l = jax.random.normal(ks[2], (D, H1 * D), dtype=jnp.float32) * s
        W1r = jax.random.normal(ks[3], (D, H1 * D), dtype=jnp.float32) * s
        att1 = jax.random.normal(ks[4], (H1, D), dtype=jnp.float32) * s
        b1 = jnp.zeros((D,), dtype=jnp.float32)
        W2l = jax.random.normal(ks[5], (D, H2 * D), dtype=jnp.float32) * s
        W2r = jax.random.normal(ks[6], (D, H2 * D), dtype=jnp.float32) * s
        att2 = jax.random.normal(ks[7], (H2, D), dtype=jnp.float32) * s
        b2 = jnp.zeros((D,), dtype=jnp.float32)
        return {'x': x, 'edge_index': edge_index, 'W1l': W1l, 'W1r': W1r, 'att1': att1, 'b1': b1, 'W2l': W2l, 'W2r': W2r, 'att2': att2, 'b2': b2}
    _L0_gnn_all = _L0_gnn_setup()
    _L0_gnn_in = {k: v for k, v in _L0_gnn_all.items() if k in ('W1l', 'W1r', 'att1', 'b1', 'W2l', 'W2r', 'att2', 'b2')}
    del _L0_gnn_all

    def _L1_gnn_setup():
        import jax, jax.numpy as jnp
        import numpy as np
        N = 3125
        E = 50000
        IN, HID, OUT = (64, 256, 64)
        key = jax.random.key(seed)
        ks = jax.random.split(key, 8)
        x = jax.random.normal(ks[0], (N, IN), dtype=jnp.float32)
        edge_index = jax.random.randint(ks[1], (2, E), 0, N, dtype=jnp.int64)

        def lin(k, fan_in, fan_out):
            bound = 1.0 / np.sqrt(fan_in)
            kw, kb = jax.random.split(k)
            W = jax.random.uniform(kw, (fan_in, fan_out), minval=-bound, maxval=bound, dtype=jnp.float32)
            b = jax.random.uniform(kb, (fan_out,), minval=-bound, maxval=bound, dtype=jnp.float32)
            return (W, b)
        W1, b1 = lin(ks[2], IN, HID)
        W2, b2 = lin(ks[3], HID, HID)
        W3, b3 = lin(ks[4], HID, OUT)
        return {'x': x, 'edge_index': edge_index, 'W1': W1, 'b1': b1, 'W2': W2, 'b2': b2, 'W3': W3, 'b3': b3}
    _L1_gnn_all = _L1_gnn_setup()
    _L1_gnn_in = {k: v for k, v in _L1_gnn_all.items() if k in ('W1', 'b1', 'W2', 'b2', 'W3', 'b3')}
    del _L1_gnn_all
    return {'x': x, 'src': src, 'dst': dst, 'L0_gnn_W1l': _L0_gnn_in['W1l'], 'L0_gnn_W1r': _L0_gnn_in['W1r'], 'L0_gnn_att1': _L0_gnn_in['att1'], 'L0_gnn_b1': _L0_gnn_in['b1'], 'L0_gnn_W2l': _L0_gnn_in['W2l'], 'L0_gnn_W2r': _L0_gnn_in['W2r'], 'L0_gnn_att2': _L0_gnn_in['att2'], 'L0_gnn_b2': _L0_gnn_in['b2'], 'L1_gnn_W1': _L1_gnn_in['W1'], 'L1_gnn_b1': _L1_gnn_in['b1'], 'L1_gnn_W2': _L1_gnn_in['W2'], 'L1_gnn_b2': _L1_gnn_in['b2'], 'L1_gnn_W3': _L1_gnn_in['W3'], 'L1_gnn_b3': _L1_gnn_in['b3']}

def reference(x, src, dst, L0_gnn_W1l, L0_gnn_W1r, L0_gnn_att1, L0_gnn_b1, L0_gnn_W2l, L0_gnn_W2r, L0_gnn_att2, L0_gnn_b2, L1_gnn_W1, L1_gnn_b1, L1_gnn_W2, L1_gnn_b2, L1_gnn_W3, L1_gnn_b3):
    import jax
    import jax.numpy as jnp

    def _L0_gnn_ref(x, edge_index, W1l, W1r, att1, b1, W2l, W2r, att2, b2):
        import jax, jax.numpy as jnp
        import numpy as np
        NEG_SLOPE = 0.2

        def gatv2_layer(x, src, dst, Wl, Wr, att, bias, n_nodes, heads):
            N, Din = x.shape
            Dh = Wl.shape[1] // heads
            xl = (x @ Wl).reshape(N, heads, Dh)
            xr = (x @ Wr).reshape(N, heads, Dh)
            e = jax.nn.leaky_relu(xl[src] + xr[dst], NEG_SLOPE)
            logits = jnp.einsum('ehd,hd->eh', e, att)
            m = jax.ops.segment_max(logits, dst, num_segments=n_nodes)
            a = jnp.exp(logits - m[dst])
            denom = jax.ops.segment_sum(a, dst, num_segments=n_nodes)
            alpha = a / denom[dst]
            out = jax.ops.segment_sum(alpha[:, :, None] * xl[src], dst, num_segments=n_nodes)
            return out.mean(axis=1) + bias
        N = x.shape[0]
        loops = jnp.arange(N, dtype=edge_index.dtype)
        src = jnp.concatenate([edge_index[0], loops])
        dst = jnp.concatenate([edge_index[1], loops])
        h = gatv2_layer(x, src, dst, W1l, W1r, att1, b1, N, 8)
        h = jax.nn.relu(h)
        h = gatv2_layer(h, src, dst, W2l, W2r, att2, b2, N, 4)
        return h

    def _L1_gnn_ref(x, edge_index, W1, b1, W2, b2, W3, b3):
        import jax, jax.numpy as jnp
        import numpy as np
        N = 3125
        E = 50000
        IN, HID, OUT = (64, 256, 64)
        src, dst = (edge_index[0], edge_index[1])
        agg = jax.ops.segment_sum(x[src], dst, num_segments=x.shape[0])
        h = x + agg
        h = jax.nn.relu(h @ W1 + b1)
        h = jax.nn.relu(h @ W2 + b2)
        return h @ W3 + b3
    edge_index = jnp.stack([src, dst])
    x = _layernorm(x + _L0_gnn_ref(x, edge_index, L0_gnn_W1l, L0_gnn_W1r, L0_gnn_att1, L0_gnn_b1, L0_gnn_W2l, L0_gnn_W2r, L0_gnn_att2, L0_gnn_b2), axis=-1)
    x = _layernorm(x + _L1_gnn_ref(x, edge_index, L1_gnn_W1, L1_gnn_b1, L1_gnn_W2, L1_gnn_b2, L1_gnn_W3, L1_gnn_b3), axis=-1)
    return x

_drawn_inputs = setup_inputs


def setup_inputs(seed=0):
    import zlib

    import numpy as np

    out = dict(_drawn_inputs(seed))
    spreads = {'L0_gnn_b1': (0.0, 0.1), 'L0_gnn_b2': (0.0, 0.1)}
    factors = {'L0_gnn_W1r': 64.0,
     'L0_gnn_W2r': 64.0,
     'L0_gnn_att2': 64.0,
     'L1_gnn_b1': 5.012,
     'L1_gnn_b2': 4.003}
    for name, (base, spread) in spreads.items():
        noise = np.random.default_rng([zlib.crc32(name.encode()), seed]).standard_normal(out[name].shape)
        drawn = base * np.exp(spread * noise) if base else spread * noise
        out[name] = jnp.asarray(drawn.astype(out[name].dtype))
    for name, factor in factors.items():
        out[name] = (out[name] * factor).astype(out[name].dtype)
    return out
```

```python
from contextlib import ExitStack

import concourse.bass as bass
from concourse import mybir

F32 = mybir.dt.float32
I32 = mybir.dt.int32
ALU = mybir.AluOpType
ACT = mybir.ActivationFunctionType
AX = mybir.AxisListType

N, D, E = 3125, 64, 100000
HID = 256
SLOPE = 0.2
EPS = 1e-5
T = 125
G = E // T
WN = 32
NW = -(-N // WN)
Q = 4
R = 3
U = -(-(G + NW - 1) // (Q * R)) * R
UT = U * Q
SLOTS = UT * T
QT = Q * T
NT = N // T
BLK = 100
NB = UT // BLK
CH = 120
BIG = 1.5e38
XW = D + 1
PAD = NW * WN
assert UT % BLK == 0 and N % T == 0 and E % T == 0 and U % R == 0


class Program:

    def __init__(self, ctx):
        self.ctx, self.sems = ctx, {}


class Layer:

    def __init__(self, nm, H, Wl, Wr, att, bias, x_node, next_table, next_node, logit_d, v_d, mx_d, norm):
        self.nm, self.H, self.Wl, self.Wr, self.att, self.bias = nm, H, Wl, Wr, att, bias
        self.x_node, self.next_table, self.next_node = x_node, next_table, next_node
        self.logit_d, self.v_d, self.mx_d, self.norm = logit_d, v_d, mx_d, norm


class Link:

    def __init__(self, eng, sem):
        self.eng, self.sem, self.n = eng, sem, 0

    def __call__(self, ins):
        self.n += 1
        ins.then_inc(self.sem, 1)
        self.eng.wait_ge(self.sem, self.n)


class Dma:

    def __init__(self, eng, sem):
        self.eng, self.sem, self.n = eng, sem, 0

    def start(self, out, in_, elements=False):
        self.n += 16
        self.eng.dma_start(out, in_, allow_slow_non_contiguous=elements).then_inc(self.sem, 16)

    def wait(self):
        self.eng.wait_ge(self.sem, self.n)


def loop3(eng, body):
    body(0, True, False)
    with eng.Fori(1, U // R - 1) as i:
        body(i, False, False)
    body(U // R - 1, False, True)


def sbuf(nc, ctx, name, shape, dt=F32):
    return ctx.enter_context(nc.sbuf_tensor(name, shape, dt))


def psum(nc, ctx, name, shape=(128, 512)):
    return ctx.enter_context(nc.psum_tensor(name, list(shape), F32))


def semaphore(nc, k, name):
    if name not in k.sems:
        k.sems[name] = k.ctx.enter_context(nc.semaphore(name))
    return k.sems[name]


def build_staircase(nc, k, a, ctx0):
    k.ident = sbuf(nc, ctx0, "ident", [128, 128])
    k.node_in_window = sbuf(nc, ctx0, "node_in_window", [T, WN])
    k.dst_local = sbuf(nc, ctx0, "dst_local", [T, UT])
    k.src_idx = sbuf(nc, ctx0, "src_idx", [T, UT], I32)
    k.win_idx = sbuf(nc, ctx0, "win_idx", [BLK, NB], I32)
    k.same = sbuf(nc, ctx0, "same", [128, UT])
    k.row_idx = sbuf(nc, ctx0, "row_idx", [T, NT], I32)
    k.row2_idx = sbuf(nc, ctx0, "row2_idx", [T, NT], I32)
    k.pcol = sbuf(nc, ctx0, "pcol", [128, 1])

    with ExitStack() as ctx:
        dg = sbuf(nc, ctx, "dg", [BLK, G // BLK, T], I32)
        gnum_i = sbuf(nc, ctx, "gnum_i", [BLK, G // BLK], I32)
        ucol_i = sbuf(nc, ctx, "ucol_i", [BLK, NB], I32)
        pcol_i = sbuf(nc, ctx, "pcol_i", [128, 1], I32)
        niw_i = sbuf(nc, ctx, "niw_i", [T, WN], I32)
        lastw_i = sbuf(nc, ctx, "lastw_i", [BLK, G // BLK], I32)
        gnum = sbuf(nc, ctx, "gnum", [BLK, G // BLK])
        key = sbuf(nc, ctx, "key", [BLK, G // BLK])
        ucol = sbuf(nc, ctx, "ucol", [BLK, NB])
        key_all = sbuf(nc, ctx, "key_all", [BLK, G])
        cmp = sbuf(nc, ctx, "cmp", [128, UT])
        gcnt = sbuf(nc, ctx, "gcnt", [BLK, NB])
        gidx = sbuf(nc, ctx, "gidx", [BLK, NB], I32)
        wcol = sbuf(nc, ctx, "wcol", [BLK, NB])
        w32 = sbuf(nc, ctx, "w32", [BLK, NB])
        wrow = sbuf(nc, ctx, "wrow", [128, UT])
        win_f = sbuf(nc, ctx, "win_f", [BLK, NB])
        wcnt = sbuf(nc, ctx, "wcnt", [NW, 1])
        wl32 = sbuf(nc, ctx, "wl32", [NW, 1])
        rowf = sbuf(nc, ctx, "rowf", [NW, WN])
        rowi = sbuf(nc, ctx, "rowi", [NW, WN], I32)
        row2f = sbuf(nc, ctx, "row2f", [NW, WN])
        row2i = sbuf(nc, ctx, "row2i", [NW, WN], I32)
        srcu = sbuf(nc, ctx, "srcu", [BLK, NB * T], I32)
        dstu = sbuf(nc, ctx, "dstu", [BLK, NB * T], I32)
        srcf = sbuf(nc, ctx, "srcf", [BLK, NB * T])
        dstf = sbuf(nc, ctx, "dstf", [BLK, NB * T])
        dl = sbuf(nc, ctx, "dl", [BLK, NB * T])
        ge0 = sbuf(nc, ctx, "ge0", [BLK, NB * T])
        keyu = sbuf(nc, ctx, "keyu", [BLK, NB * T])
        edge_keys = sbuf(nc, ctx, "edge_keys", [1, 2])
        ps = [psum(nc, ctx, f"ps_setup{i}") for i in range(4)]
        s = {n: semaphore(nc, k, "st_" + n) for n in (
            "load", "iota", "ident0", "ident", "dve", "dve2", "dve3", "gather", "store", "transposed", "pad")}

        with nc.Block() as block:
            @block.sync
            def _(sp):
                sp.dma_start(dg[:], a["dst"].rearrange("(p k e) -> p k e", k=G // BLK, e=T)).then_inc(s["load"], 16)
                sp.wait_ge(s["dve"], 4)
                st = Dma(sp, s["store"])
                st.start(k.key_d.rearrange("(p k) -> p k", k=G // BLK), key[:])
                st.wait()
                st.start(key_all[:], bass.AP(k.key_d.tensor, 0, [[0, BLK], [1, G]]))
                st.wait()

            @block.gpsimd
            def _(pool):
                pool.iota(gnum_i[:], [[1, G // BLK]], base=0, channel_multiplier=G // BLK).then_inc(s["iota"], 1)
                pool.iota(ucol_i[:], [[BLK, NB]], base=0, channel_multiplier=1).then_inc(s["iota"], 1)
                pool.iota(pcol_i[:], [[0, 1]], base=0, channel_multiplier=1).then_inc(s["iota"], 1)
                pool.iota(niw_i[:], [[1, WN]], base=0, channel_multiplier=0).then_inc(s["iota"], 1)
                pool.memset(k.ident[:], 0.0).then_inc(s["ident0"], 1)
                pool.memset(edge_keys[:], -5.0).then_inc(s["pad"], 1)
                pool.wait_ge(s["ident0"], 1)
                pool.affine_select(out=k.ident[:], in_=k.ident[:], compare_op=ALU.not_equal, fill=1.0,
                                   base=0, pattern=[[-1, 128]], channel_multiplier=1).then_inc(s["ident"], 1)

            @block.vector
            def _(dve):
                link = Link(dve, s["dve"])
                dve.wait_ge(s["load"], 16)
                dve.wait_ge(s["iota"], 4)
                link(dve.tensor_scalar(lastw_i[:], dg[:, :, T - 1], 5, None, ALU.arith_shift_right))
                link(dve.tensor_copy(key[:], lastw_i[:]))
                link(dve.tensor_copy(gnum[:], gnum_i[:]))
                link(dve.tensor_tensor(key[:], key[:], gnum[:], ALU.add))
                link(dve.tensor_copy(ucol[:], ucol_i[:]))
                link(dve.tensor_copy(k.pcol[:], pcol_i[:]))
                link(dve.tensor_copy(k.node_in_window[:], niw_i[:]))

        with nc.Block() as block:
            @block.vector
            def _(dve):
                link = Link(dve, s["dve2"])
                for b in range(NB):
                    link(dve.tensor_scalar(cmp[0:BLK, 0:G], key_all[:], ucol[:, b:b + 1], None, ALU.is_lt))
                    link(dve.tensor_reduce(gcnt[:, b:b + 1], cmp[0:BLK, 0:G], AX.X, ALU.add))
                link(dve.tensor_scalar(gcnt[:], gcnt[:], float(G - 1), None, ALU.min))
                link(dve.tensor_copy(gidx[:], gcnt[:]))
                link(dve.tensor_tensor(wcol[:], ucol[:], gcnt[:], ALU.subtract))
                link(dve.tensor_scalar(w32[:], wcol[:], float(WN), None, ALU.mult))

            @block.gpsimd
            def _(pool):
                pool.wait_ge(s["dve2"], 2 * NB + 2)
                for b in range(NB):
                    pool.indirect_dma_start(srcu[:, b * T:(b + 1) * T], None, a["src"].rearrange("(g e) -> g e", e=T),
                                            bass.IndirectOffsetOnAxis(gidx[:, b:b + 1], 0)).then_inc(s["gather"], 16)
                    pool.indirect_dma_start(dstu[:, b * T:(b + 1) * T], None, a["dst"].rearrange("(g e) -> g e", e=T),
                                            bass.IndirectOffsetOnAxis(gidx[:, b:b + 1], 0)).then_inc(s["gather"], 16)
                pool.wait_ge(s["gather"], 32 * NB)

            @block.sync
            def _(sp):
                st = Dma(sp, s["store"])
                st.n = 32
                sp.wait_ge(s["dve2"], 2 * NB + 3)
                st.start(k.w_d.rearrange("(b p) -> p b", p=BLK), wcol[:], elements=True)
                st.wait()
                st.start(wrow[:], bass.AP(k.w_d.tensor, 0, [[0, 128], [1, UT]]))
                st.wait()

        with nc.Block() as block:
            @block.vector
            def _(dve):
                link = Link(dve, s["dve3"])
                link(dve.tensor_copy(srcf[:], srcu[:]))
                link(dve.tensor_copy(dstf[:], dstu[:]))
                for b in range(NB):
                    c = slice(b * T, (b + 1) * T)
                    link(dve.tensor_scalar(dl[:, c], dstf[:, c], w32[:, b:b + 1], None, ALU.subtract))
                link(dve.tensor_scalar(ge0[:], dl[:], 0.0, None, ALU.is_ge))
                link(dve.scalar_tensor_tensor(out=ge0[:], in0=dl[:], scalar=float(WN), in1=ge0[:],
                                              op0=ALU.is_lt, op1=ALU.mult))
                link(dve.scalar_tensor_tensor(out=keyu[:], in0=dstf[:], scalar=1.0, in1=ge0[:],
                                              op0=ALU.add, op1=ALU.mult))
                link(dve.tensor_scalar(keyu[:], keyu[:], -1.0, None, ALU.add))
                link(dve.tensor_scalar(win_f[:], wcol[:], float(NW - 1), None, ALU.min))
                link(dve.tensor_copy(k.win_idx[:], win_f[:]))
                link(dve.memset(k.same[:, 0:1], 0.0))
                link(dve.tensor_tensor(k.same[:, 1:UT], wrow[:, 1:UT], wrow[:, 0:UT - 1], ALU.is_equal))
                link(dve.tensor_scalar(cmp[0:NW, :], wrow[0:NW, :], k.pcol[0:NW, :], None, ALU.is_le))
                link(dve.tensor_reduce(wcnt[:], cmp[0:NW, :], AX.X, ALU.add))
                link(dve.tensor_scalar(wcnt[:], wcnt[:], -1.0, None, ALU.add))
                link(dve.tensor_scalar(wl32[:], wcnt[:], float(WN), None, ALU.mult))
                link(dve.tensor_scalar(rowf[:], k.node_in_window[0:NW, :], wl32[:], None, ALU.add))
                link(dve.tensor_copy(rowi[:], rowf[:]))
                link(dve.tensor_scalar(row2f[:], k.node_in_window[0:NW, :], float(UT), wcnt[:], ALU.mult, ALU.add))
                link(dve.tensor_copy(row2i[:], row2f[:]))
                dve.wait_ge(s["transposed"], 2 * NB)
                link(dve.tensor_copy(k.src_idx[:, 0:5 * BLK], ps[0][0:T, 0:5 * BLK]))
                link(dve.tensor_copy(k.src_idx[:, 5 * BLK:UT], ps[1][0:T, 0:4 * BLK]))
                link(dve.tensor_copy(k.dst_local[:, 0:5 * BLK], ps[2][0:T, 0:5 * BLK]))
                link(dve.tensor_copy(k.dst_local[:, 5 * BLK:UT], ps[3][0:T, 0:4 * BLK]))

            @block.tensor
            def _(pe):
                pe.wait_ge(s["dve3"], NB + 2)
                for b in range(NB):
                    c = slice((b % 5) * BLK, (b % 5 + 1) * BLK)
                    pe.transpose(ps[b // 5][0:T, c], srcf[:, b * T:(b + 1) * T],
                                 k.ident[0:BLK, 0:BLK]).then_inc(s["transposed"], 1)
                    pe.transpose(ps[2 + b // 5][0:T, c], dl[:, b * T:(b + 1) * T],
                                 k.ident[0:BLK, 0:BLK]).then_inc(s["transposed"], 1)

            @block.sync
            def _(sp):
                st = Dma(sp, s["store"])
                st.n = 64
                sp.wait_ge(s["dve3"], NB + 6)
                for b in range(NB):
                    st.start(k.keys_d[1 + b * BLK * T:1 + (b + 1) * BLK * T].rearrange("(p e) -> p e", e=T),
                             keyu[:, b * T:(b + 1) * T])
                st.start(k.keys_d[0:1].unsqueeze(0), edge_keys[:, 0:1])
                st.start(k.keys_d[SLOTS + 1:SLOTS + 2].unsqueeze(0), edge_keys[:, 1:2])
                sp.wait_ge(s["dve3"], NB + 18)
                st.start(k.row_d.rearrange("(w n) -> w n", n=WN), rowi[:])
                st.start(k.row2_d.rearrange("(w n) -> w n", n=WN), row2i[:])
                st.wait()
                st.start(k.row_idx[:], k.row_d[0:N].rearrange("(p t) -> p t", t=NT))
                st.start(k.row2_idx[:], k.row2_d[0:N].rearrange("(p t) -> p t", t=NT))
                st.wait()


def prepare_layer(nc, k, ctx, lay):
    H = lay.H
    C = H * D // 128
    FR = 128 // H
    lay.C, lay.FR = C, FR
    lay.w_abs = sbuf(nc, ctx, lay.nm + "w_abs", [128, C * 128])
    lay.w_lin = sbuf(nc, ctx, lay.nm + "w_lin", [128, H])
    lay.sign = sbuf(nc, ctx, lay.nm + "sign", [128, C])
    lay.sign_sum = sbuf(nc, ctx, lay.nm + "sign_sum", [128, H])
    lay.self_logit = sbuf(nc, ctx, lay.nm + "self_logit", [T, NT, H])
    lay.XR = XW + H
    lay.table = nc.dram_tensor(lay.nm + "table_d", [N, lay.XR], F32, kind="Internal").ap()
    lay.xpad_d = nc.dram_tensor(lay.nm + "xpad_d", [PAD, D], F32, kind="Internal").ap()
    with ExitStack() as tmp:
        rows = sbuf(nc, tmp, lay.nm + "rows", [T, NT, lay.XR])
        zero = sbuf(nc, tmp, lay.nm + "zero", [PAD - N, D])
        win = [sbuf(nc, tmp, f"{lay.nm}win{i}", [BLK, WN * D]) for i in range(3)]
        w_raw = sbuf(nc, tmp, lay.nm + "w_raw", [128, H * D])
        att_row = sbuf(nc, tmp, lay.nm + "att_row", [128, H * D])
        att_abs = sbuf(nc, tmp, lay.nm + "att_abs", [128, H * D])
        w_att = sbuf(nc, tmp, lay.nm + "w_att", [128, H * D])
        sign_row = sbuf(nc, tmp, lay.nm + "sign_row", [128, H * D])
        att_col = sbuf(nc, tmp, lay.nm + "att_col", [128, C])
        head0_i = sbuf(nc, tmp, lay.nm + "head0_i", [128, H], I32)
        head0 = sbuf(nc, tmp, lay.nm + "head0", [128, H])
        in_head = sbuf(nc, tmp, lay.nm + "in_head", [128, H])
        xx = sbuf(nc, tmp, lay.nm + "xx", [T, NT, 2 * D])
        xxT = sbuf(nc, tmp, lay.nm + "xxT", [128, NT * T])
        rel = sbuf(nc, tmp, lay.nm + "rel", [T, 2, H * D])
        ps_t = [psum(nc, tmp, f"{lay.nm}ps_t{i}") for i in range(2)]
        ps_z = [psum(nc, tmp, f"{lay.nm}ps_z{i}") for i in range(2)]
        ps_l = psum(nc, tmp, lay.nm + "ps_l")
        s = {n: semaphore(nc, k, "p_" + n) for n in (
            "load", "dve", "iota", "xT", "xT_copied", "z", "relu", "used", "lin", "zero", "xpad", "table", "rows")}
        win_in = [semaphore(nc, k, f"{lay.nm}win_in{i}") for i in range(3)]
        win_out = [semaphore(nc, k, f"p_win_out{i}") for i in range(3)]
        with nc.Block() as block:
            @block.sync
            def _(sp):
                ld = Dma(sp, s["load"])
                ld.start(w_raw[0:D, :], lay.Wl)
                ld.start(w_raw[D:128, :], lay.Wr)
                ld.start(att_row[:], bass.AP(lay.att.tensor, 0, [[0, 128], [1, H * D]]))
                for h in range(H):
                    ld.start(att_col[h * FR:(h + 1) * FR, :], lay.att[h, :].rearrange("(c r) -> r c", r=FR), elements=True)
                sp.wait_ge(s["zero"], 1)
                sp.dma_start(lay.xpad_d[0:N, :].rearrange("(p t) d -> p t d", t=NT),
                             lay.x_node[:]).then_inc(s["xpad"], 16)
                sp.dma_start(lay.xpad_d[N:PAD, :], zero[:]).then_inc(s["xpad"], 16)
                ld.wait()
                sp.wait_ge(s["xpad"], 32)

            @block.gpsimd
            def _(pool):
                pool.memset(zero[:], 0.0).then_inc(s["zero"], 1)
                pool.iota(head0_i[:], [[-FR, H]], base=0, channel_multiplier=1).then_inc(s["iota"], 1)

            @block.vector
            def _(dve):
                link = Link(dve, s["dve"])
                link(dve.tensor_copy(xx[:, :, 0:D], lay.x_node[:, :, :]))
                link(dve.tensor_copy(xx[:, :, D:2 * D], lay.x_node[:, :, :]))
                dve.wait_ge(s["load"], 16 * (3 + H))
                link(dve.tensor_scalar(att_abs[:], att_row[:], -1.0, None, ALU.mult))
                link(dve.tensor_tensor(att_abs[:], att_abs[:], att_row[:], ALU.max))
                for c in range(C):
                    f = slice(c * FR, (c + 1) * FR)
                    link(dve.tensor_tensor(lay.w_abs[:, c * 128:(c + 1) * 128].rearrange("p (h r) -> p h r", h=H),
                                           w_raw[:].rearrange("p (h d) -> p h d", h=H)[:, :, f],
                                           att_abs[:].rearrange("p (h d) -> p h d", h=H)[:, :, f], ALU.mult))
                link(dve.tensor_tensor(w_att[:], w_raw[:], att_row[:], ALU.mult))
                link(dve.tensor_reduce(lay.w_lin[:], w_att[:].rearrange("p (h d) -> p h d", h=H), AX.X, ALU.add))
                link(dve.tensor_scalar(lay.w_lin[:], lay.w_lin[:], SLOPE, None, ALU.mult))
                for c in range(C):
                    f = slice(c * FR, (c + 1) * FR)
                    link(dve.tensor_scalar(sign_row[:, c * 128:(c + 1) * 128].rearrange("p (h r) -> p h r", h=H),
                                           att_row[:].rearrange("p (h d) -> p h d", h=H)[:, :, f], 0.0, 2.0,
                                           ALU.is_ge, ALU.mult))
                link(dve.tensor_scalar(sign_row[:], sign_row[:], -1.0, None, ALU.add))
                link(dve.tensor_scalar(att_col[:], att_col[:], 0.0, 2.0, ALU.is_ge, ALU.mult))
                link(dve.tensor_scalar(lay.sign[:], att_col[:], -1.0, None, ALU.add))
                dve.wait_ge(s["iota"], 1)
                link(dve.tensor_copy(head0[:], head0_i[:]))
                link(dve.tensor_scalar(in_head[:], head0[:], 0.0, None, ALU.is_ge))
                link(dve.scalar_tensor_tensor(out=in_head[:], in0=head0[:], scalar=float(FR), in1=in_head[:],
                                              op0=ALU.is_lt, op1=ALU.mult))
                link(dve.tensor_scalar(lay.sign_sum[:], in_head[:], lay.sign[:, 0:1], None, ALU.mult))
                link(dve.tensor_scalar(lay.sign[:, 1:C], lay.sign[:, 1:C], lay.sign[:, 0:1], None, ALU.mult))

        with nc.Block() as block:
            @block.gpsimd
            def _(pool):
                for b in range(NB):
                    if b >= 3:
                        pool.wait_ge(win_out[b % 3], 16 * (b // 3))
                    pool.indirect_dma_start(win[b % 3][:], None, lay.xpad_d.rearrange("(w n) d -> w (n d)", n=WN),
                                            bass.IndirectOffsetOnAxis(k.win_idx[:, b:b + 1], 0)).then_inc(win_in[b % 3], 16)

            @block.sync
            def _(sp):
                for b in range(NB):
                    sp.wait_ge(win_in[b % 3], 16 * (b // 3 + 1))
                    sp.dma_start(k.xw_d[b * BLK:(b + 1) * BLK, :], win[b % 3][:]).then_inc(win_out[b % 3], 16)
                sp.wait_ge(s["rows"], 3)
                sp.dma_start(lay.table.rearrange("(p t) f -> p t f", t=NT), rows[:]).then_inc(s["table"], 16)
                for i in range(3):
                    sp.wait_ge(win_out[i], 16 * len(range(i, NB, 3)))
                sp.wait_ge(s["table"], 16)

            @block.tensor
            def _(pe):
                for t in range(NT):
                    if t >= 2:
                        pe.wait_ge(s["xT_copied"], t - 1)
                    pe.transpose(ps_t[t % 2][:, 0:T], xx[:, t, :], k.ident[0:T, 0:T]).then_inc(s["xT"], 1)
                    pe.wait_ge(s["xT_copied"], t + 1)
                    if t >= 2:
                        pe.wait_ge(s["relu"], t - 1)
                    pe.matmul(ps_z[t % 2][0:T, 0:H * D], xxT[:, t * T:(t + 1) * T], lay.w_abs[:],
                              start=True, stop=True).then_inc(s["z"], 1)
                    pe.matmul(ps_l[0:T, t * H:(t + 1) * H], xxT[0:D, t * T:(t + 1) * T], lay.w_lin[0:D, :],
                              start=True, stop=True).then_inc(s["lin"], 1)

            @block.scalar
            def _(act):
                for t in range(NT):
                    act.wait_ge(s["z"], t + 1)
                    if t >= 2:
                        act.wait_ge(s["used"], 2 * t - 2)
                    act.activation(rel[:, t % 2, :], ps_z[t % 2][0:T, 0:H * D], ACT.Relu,
                                   scale=1.0 - SLOPE).then_inc(s["relu"], 1)

            @block.vector
            def _(dve):
                used = 0

                def reduce(t):
                    dve.wait_ge(s["relu"], t + 1)
                    dve.tensor_tensor(rel[:, t % 2, :], rel[:, t % 2, :], sign_row[0:T, :],
                                      ALU.mult).then_inc(s["used"], 1)
                    dve.wait_ge(s["used"], 2 * t + 1)
                    dve.tensor_reduce(lay.self_logit[:, t, :],
                                      rel[:, t % 2, :].rearrange("p (c h r) -> p h c r", c=C, h=H),
                                      AX.XY, ALU.add).then_inc(s["used"], 1)

                for t in range(NT):
                    dve.wait_ge(s["xT"], t + 1)
                    dve.tensor_copy(xxT[:, t * T:(t + 1) * T], ps_t[t % 2][:, 0:T]).then_inc(s["xT_copied"], 1)
                    if t >= 1:
                        reduce(t - 1)
                reduce(NT - 1)
                dve.wait_ge(s["lin"], NT)
                dve.wait_ge(s["used"], 2 * NT)
                dve.tensor_tensor(lay.self_logit[:].rearrange("p t h -> p (t h)"),
                                  lay.self_logit[:].rearrange("p t h -> p (t h)"),
                                  ps_l[0:T, 0:NT * H], ALU.add).then_inc(s["used"], 1)
                dve.tensor_copy(rows[:, :, 0:D], lay.x_node[:]).then_inc(s["rows"], 1)
                dve.memset(rows[:, :, D:XW], 1.0).then_inc(s["rows"], 1)
                dve.tensor_copy(rows[:, :, XW:lay.XR],
                                ps_l[0:T, 0:NT * H].rearrange("p (t h) -> p t h", h=H)).then_inc(s["rows"], 1)


def edge_logits(nc, k, lay):
    H, C = lay.H, lay.C
    NE = 6
    with ExitStack() as ctx:
        ph, nm = "a_", lay.nm + "a_"
        idx = [sbuf(nc, ctx, f"{nm}idx{r}", [T, Q], I32) for r in range(R)]
        xs = [sbuf(nc, ctx, f"{nm}xs{r}", [T, Q, lay.XR]) for r in range(R)]
        xw = [sbuf(nc, ctx, f"{nm}xw{r}", [128, D]) for r in range(R)]
        oh = [sbuf(nc, ctx, f"{nm}oh{r}", [T, Q, WN]) for r in range(R)]
        ohT = [sbuf(nc, ctx, f"{nm}ohT{r}", [128, Q, T]) for r in range(R)]
        xT = [sbuf(nc, ctx, f"{nm}xT{r}", [128, QT]) for r in range(R)]
        rl = [sbuf(nc, ctx, f"{nm}rl{r}", [128, QT]) for r in range(NE)]
        f = [sbuf(nc, ctx, f"{nm}f{r}", [128, QT]) for r in range(R)]
        lg = [sbuf(nc, ctx, f"{nm}lg{r}", [H, QT]) for r in range(R)]
        ps_oh = psum(nc, ctx, nm + "ps_oh")
        ps_x = [psum(nc, ctx, f"{nm}ps_x{r}") for r in range(R)]
        ps_z = [psum(nc, ctx, f"{nm}ps_z{r}") for r in range(R)]
        ps_l = psum(nc, ctx, nm + "ps_l")
        s = {n: semaphore(nc, k, ph + n) for n in (
            "zeros", "idx_staged", "pool_step", "act_step", "src_read", "lin_read", "oh_ready", "oh_turned", "ohT_ready", "x_ready",
            "xT_ready", "z_ready", "relu_done", "combined", "logit_ready", "logit_copied")}
        gath = [semaphore(nc, k, f"{nm}gath{r}") for r in range(R)]
        spill = [semaphore(nc, k, f"{ph}spill{r}") for r in range(R)]
        lgst = [semaphore(nc, k, f"{ph}lgst{r}") for r in range(R)]
        xwld = [semaphore(nc, k, f"{ph}xwld{r}") for r in range(R)]
        GB = 16 * Q

        with nc.Block() as block:
            @block.gpsimd
            def _(pool):
                def body(i, first, last):
                    for r in range(R):
                        u = i * R + r
                        if not first:
                            pool.wait_ge(s["src_read"], u - R + 1)
                            pool.sem_inc(s["pool_step"], 1)
                            pool.wait_ge(s["lin_read"], u - R + 1)
                            pool.sem_inc(s["pool_step"], 1)
                            pool.wait_ge(spill[r], 16 * i)
                            pool.sem_inc(s["pool_step"], 1)
                        pool.wait_ge(s["idx_staged"], u + 1)
                        pool.sem_inc(s["pool_step"], 1)
                        for j in range(Q):
                            pool.indirect_dma_start(xs[r][:, j, :], None, lay.table,
                                                    bass.IndirectOffsetOnAxis(idx[r][:, j:j + 1], 0)).then_inc(gath[r], 16)
                loop3(pool, body)

            @block.sync
            def _(sp):
                def load_windows(u, r):
                    sp.dma_start(xw[r][:], k.xw_d[bass.ds(u * Q, Q), :].rearrange("w (n d) -> (w n) d", d=D)).then_inc(xwld[r], 16)

                def store_logits(u, r):
                    sp.wait_ge(s["logit_copied"], u + 1)
                    sp.dma_start(lay.logit_d[:, bass.ds(u * QT, QT)], lg[r][:]).then_inc(lgst[r], 16)

                load_windows(0, 0)
                load_windows(1, 1)

                def body(i, first, last):
                    for r in range(R):
                        u = i * R + r
                        if not (last and r >= R - 2):
                            if not (first and r == 0):
                                sp.wait_ge(s["x_ready"], u)
                            load_windows(u + 2, (r + 2) % R)
                        sp.wait_ge(gath[r], GB * (i + 1))
                        sp.dma_start(lay.xs_d[bass.ds(u, 1), :, :].rearrange("u p f -> (u p) f"),
                                     xs[r][:].rearrange("p j f -> p (j f)")).then_inc(spill[r], 16)
                        if not (first and r < 2):
                            store_logits(u - 2, (r + R - 2) % R)
                    if last:
                        store_logits(U - 2, R - 2)
                        store_logits(U - 1, R - 1)
                loop3(sp, body)
                for r in range(R):
                    sp.wait_ge(spill[r], 16 * (U // R))
                    sp.wait_ge(lgst[r], 16 * (U // R))

            @block.tensor
            def _(pe):
                def turn(u, r, uses, free):
                    pe.wait_ge(s["oh_ready"], u + 1)
                    if free:
                        pe.wait_ge(s["xT_ready"], u - R + 1)
                    if free is not None:
                        pe.wait_ge(s["ohT_ready"], u)
                    pe.wait_ge(gath[r], GB * uses)
                    pe.transpose(ps_oh[:, 0:T], oh[r][:].rearrange("p j n -> p (j n)"),
                                 k.ident[0:T, 0:T]).then_inc(s["oh_turned"], 1)
                    for j in range(Q):
                        ins = pe.transpose(ps_x[r][0:D, j * T:(j + 1) * T], xs[r][:, j, 0:D], k.ident[0:T, 0:T])
                    ins.then_inc(s["src_read"], 1)

                def spread(u, r, uses):
                    pe.wait_ge(s["ohT_ready"], u + 1)
                    pe.wait_ge(xwld[r], 16 * uses)
                    pe.matmul(ps_x[r][D:128, 0:QT], xw[r][:], ohT[r][:].rearrange("p j e -> p (j e)"),
                              start=True, stop=True).then_inc(s["x_ready"], 1)

                def project(i, r, first, cs):
                    u = i * R + r
                    for c in cs:
                        b = (C * r + c) % R
                        if c == 0:
                            pe.wait_ge(s["xT_ready"], u + 1)
                        if not (first and C * r + c < R):
                            pe.wait_ge(s["relu_done"], C * u + c - R + 1)
                        pe.matmul(ps_z[b][:, 0:QT], lay.w_abs[:, c * 128:(c + 1) * 128], xT[r][:],
                                  start=True, stop=True).then_inc(s["z_ready"], 1)

                def reduce(u, r, free):
                    if free:
                        pe.wait_ge(s["logit_copied"], u)
                    pe.wait_ge(s["combined"], (C - 1) * (u + 1))
                    pe.matmul(ps_l[0:H, 0:QT], lay.sign_sum[:], f[r][:], start=True,
                              stop=True).then_inc(s["logit_ready"], 1)

                turn(0, 0, 1, None)
                spread(0, 0, 1)

                def body(i, first, last):
                    for r in range(R):
                        u = i * R + r
                        n = (r + 1) % R
                        more = not (last and r == R - 1)
                        if more:
                            turn(u + 1, n, i + 1 + (n == 0), not (first and n != 0))
                        project(i, r, first, range(0, C // 2))
                        if more:
                            spread(u + 1, n, i + 1 + (n == 0))
                        project(i, r, first, range(C // 2, C))
                        if not (first and r == 0):
                            reduce(u - 1, (r + R - 1) % R, not (first and r == 1))
                loop3(pe, body)
                reduce(U - 1, R - 1, True)

            @block.scalar
            def _(act):
                def copy_logit(u, r, i, free):
                    act.wait_ge(s["logit_ready"], u + 1)
                    if free:
                        act.wait_ge(lgst[r], 16 * i)
                    act.activation(lg[r][:], ps_l[0:H, 0:QT], ACT.Copy).then_inc(s["logit_copied"], 1)

                def stage(u, r):
                    act.activation(idx[r][:], k.src_idx[:, bass.ds(u * Q, Q)], ACT.Copy).then_inc(s["idx_staged"], 1)

                for r in range(R):
                    stage(r, r)

                def body(i, first, second, last=False):
                    for r in range(R):
                        u = i * R + r
                        act.wait_ge(gath[r], GB * (i + 1))
                        act.sem_inc(s["act_step"], 1)
                        if not last:
                            stage(u + R, r)
                        act.activation(lay.lin_edge[:, bass.ds(u * Q, Q), :], xs[r][:, :, XW:lay.XR],
                                       ACT.Copy).then_inc(s["lin_read"], 1)
                        for c in range(C):
                            m = C * r + c
                            act.wait_ge(s["z_ready"], C * u + c + 1)
                            back = m - NE
                            br, bc = back // C, back % C
                            if not (first and back < 0):
                                act.wait_ge(s["combined"], (C - 1) * (i * R + br) + max(bc, 1))
                            act.activation(rl[m % NE][:], ps_z[m % R][:, 0:QT], ACT.Relu,
                                           scale=1.0 - SLOPE).then_inc(s["relu_done"], 1)
                        if not (first and r == 0):
                            copy_logit(u - 1, (r + R - 1) % R, i - (r == 0), not (first or second and r == 0))
                body(0, True, False)
                body(1, False, True)
                with act.Fori(2, U // R - 1) as i:
                    body(i, False, False)
                body(U // R - 1, False, False, True)
                copy_logit(U - 1, R - 1, U // R - 1, True)

            @block.vector
            def _(dve):
                def one_hot(u, r, free):
                    if free:
                        dve.wait_ge(s["oh_turned"], u - R + 1)
                    dve.tensor_tensor(oh[r][:], k.dst_local[:, bass.ds(u * Q, Q)].unsqueeze(2).to_broadcast([T, Q, WN]),
                                      k.node_in_window[:].unsqueeze(1).to_broadcast([T, Q, WN]),
                                      ALU.is_equal).then_inc(s["oh_ready"], 1)

                def copy_ohT(u, r, free):
                    dve.wait_ge(s["oh_turned"], u + 1)
                    if free:
                        dve.wait_ge(s["x_ready"], u - R + 1)
                    for j in range(Q):
                        p = slice(WN * j, WN * j + WN)
                        ins = dve.tensor_copy(ohT[r][p, j, :], ps_oh[p, 0:T])
                    ins.then_inc(s["ohT_ready"], 1)

                def copy_xT(u, r, free):
                    dve.wait_ge(s["x_ready"], u + 1)
                    if free:
                        dve.wait_ge(s["z_ready"], C * (u - R + 1))
                    dve.tensor_copy(xT[r][:], ps_x[r][:, 0:QT]).then_inc(s["xT_ready"], 1)

                def combine(i, r, first, c):
                    u = i * R + r
                    dve.wait_ge(s["relu_done"], C * u + c + 1)
                    if c == 1 and not first:
                        dve.wait_ge(s["logit_ready"], u - R + 1)
                    if c > 1:
                        dve.wait_ge(s["combined"], (C - 1) * u + c - 1)
                    dve.scalar_tensor_tensor(out=f[r][:], in0=rl[(C * r + c) % NE][:], scalar=lay.sign[:, c:c + 1],
                                             in1=rl[(C * r) % NE][:] if c == 1 else f[r][:],
                                             op0=ALU.mult, op1=ALU.add).then_inc(s["combined"], 1)

                for r in range(R):
                    dve.memset(ohT[r][:], 0.0).then_inc(s["zeros"], 1)
                dve.wait_ge(s["zeros"], R)
                one_hot(0, 0, False)
                one_hot(1, 1, False)
                copy_ohT(0, 0, False)
                copy_xT(0, 0, False)

                def body(i, first, last):
                    for r in range(R):
                        u = i * R + r
                        if not (last and r >= R - 2):
                            one_hot(u + 2, (r + 2) % R, not (first and r + 2 < R))
                        more = not (last and r == R - 1)
                        free = not (first and r + 1 < R)
                        if more:
                            copy_ohT(u + 1, (r + 1) % R, free)
                        combine(i, r, first, 1)
                        if more:
                            copy_xT(u + 1, (r + 1) % R, free)
                        for c in range(2, C):
                            combine(i, r, first, c)
                loop3(dve, body)


def edge_softmax(nc, k, lay):
    H = lay.H
    NC = CH // H
    F = SLOTS // NC
    TPC = F // T
    lay.stat_d = nc.dram_tensor(lay.nm + "stat_d", [NC, H, 4], F32, kind="Internal").ap()
    lay.carry_d = nc.dram_tensor(lay.nm + "carry_d", [NC, H, 2], F32, kind="Internal").ap()
    with ExitStack() as tmp:
        ph, nm = "s_", lay.nm + "s_"
        keys = sbuf(nc, tmp, nm + "keys", [CH, F + 2])
        lim = sbuf(nc, tmp, nm + "lim", [CH, F + 1])
        lg = sbuf(nc, tmp, nm + "lg", [CH, F])
        fw = sbuf(nc, tmp, nm + "fw", [CH, F])
        bw = keys
        stat = sbuf(nc, tmp, nm + "stat", [CH, 4])
        stat_h = sbuf(nc, tmp, nm + "stat_h", [H, NC, 4])
        run = sbuf(nc, tmp, nm + "run", [H, 2, NC])
        carry_h = sbuf(nc, tmp, nm + "carry_h", [H, NC, 2])
        carry = sbuf(nc, tmp, nm + "carry", [CH, 2])
        ps = [psum(nc, tmp, f"{nm}ps{i}") for i in range(4)]
        s = {n: semaphore(nc, k, ph + n) for n in (
            "load", "bounce", "dve", "exp", "lin_laid", "lin_turned", "lin_added", "turned", "copied")}
        lin = lay.m_edge[:].rearrange("p s h -> p (s h)").rearrange("p (t v) -> p t v", v=CH)
        GRP = 4
        LG = -(-TPC // GRP)
        with nc.Block() as block:
            @block.sync
            def _(sp):
                ld = Dma(sp, s["load"])
                for c in range(NC):
                    ld.start(keys[c * H:(c + 1) * H, :], bass.AP(k.keys_d.tensor, c * F, [[0, H], [1, F + 2]]))
                for c in range(NC):
                    ld.start(lg[c * H:(c + 1) * H, :], lay.logit_d[:, c * F:(c + 1) * F])
                bo = Dma(sp, s["bounce"])
                sp.wait_ge(s["dve"], 8)
                bo.start(lay.stat_d.rearrange("c h v -> (c h) v"), stat[:])
                bo.wait()
                bo.start(stat_h[:], lay.stat_d.rearrange("c h v -> h c v"))
                bo.wait()
                sp.wait_ge(s["dve"], 14)
                bo.start(lay.carry_d.rearrange("c h v -> h c v"), carry_h[:])
                bo.wait()
                bo.start(carry[:], lay.carry_d.rearrange("c h v -> (c h) v"))
                bo.wait()

            @block.vector
            def _(dve):
                link = Link(dve, s["dve"])
                dve.tensor_copy(lin.rearrange("p t (c h) -> p t c h", h=H),
                                lay.lin_edge[:].rearrange("p (c t) h -> p t c h", c=NC)).then_inc(s["lin_laid"], 1)
                dve.wait_ge(s["load"], 32 * NC)
                link(dve.tensor_tensor(lim[:], keys[:, 0:F + 1], keys[:, 1:F + 2], ALU.is_equal))
                link(dve.tensor_scalar(lim[:], lim[:], 2 * BIG, -BIG, ALU.mult, ALU.add))
                for g in range(LG):
                    c = slice(g * GRP * T, min((g + 1) * GRP, TPC) * T)
                    dve.wait_ge(s["lin_turned"], g + 1)
                    dve.tensor_tensor(lg[:, c], lg[:, c], ps[g % 4][0:CH, 0:c.stop - c.start],
                                      ALU.add).then_inc(s["lin_added"], 1)
                dve.wait_ge(s["lin_added"], LG)
                link(dve.tensor_tensor_scan(fw[:], lim[:, 0:F], lg[:], -BIG, ALU.min, ALU.max))
                link(dve.tensor_tensor_scan(bw[:, 0:F][:, ::-1], lim[:, 1:F + 1][:, ::-1], lg[:, ::-1], -BIG,
                                            ALU.min, ALU.max))
                link(dve.tensor_copy(stat[:, 0:1], fw[:, F - 1:F]))
                link(dve.tensor_reduce(stat[:, 1:2], lim[:, 0:F], AX.X, ALU.min))
                link(dve.tensor_copy(stat[:, 2:3], bw[:, 0:1]))
                link(dve.tensor_reduce(stat[:, 3:4], lim[:, 1:F + 1], AX.X, ALU.min))
                dve.wait_ge(s["bounce"], 32)
                link(dve.tensor_tensor_scan(run[:, 0, :], stat_h[:, :, 1], stat_h[:, :, 0], -BIG, ALU.min, ALU.max))
                link(dve.tensor_tensor_scan(run[:, 1, ::-1], stat_h[:, ::-1, 3], stat_h[:, ::-1, 2], -BIG,
                                            ALU.min, ALU.max))
                link(dve.memset(carry_h[:, 0, 0:1], -BIG))
                link(dve.memset(carry_h[:, NC - 1, 1:2], -BIG))
                link(dve.tensor_copy(carry_h[:, 1:NC, 0], run[:, 0, 0:NC - 1]))
                link(dve.tensor_copy(carry_h[:, 0:NC - 1, 1], run[:, 1, 1:NC]))
                dve.wait_ge(s["bounce"], 64)
                link(dve.tensor_tensor_scan(fw[:], lim[:, 0:F], lg[:], carry[:, 0:1], ALU.min, ALU.max))
                link(dve.tensor_tensor_scan(bw[:, 0:F][:, ::-1], lim[:, 1:F + 1][:, ::-1], lg[:, ::-1],
                                            carry[:, 1:2], ALU.min, ALU.max))
                link(dve.tensor_tensor(fw[:], fw[:], bw[:, 0:F], ALU.max))
                link(dve.tensor_tensor(lg[:], lg[:], fw[:], ALU.subtract))
                link(dve.scalar_tensor_tensor(out=bw[:, 0:F], in0=lim[:, 1:F + 1], scalar=0.0, in1=fw[:],
                                              op0=ALU.is_lt, op1=ALU.mult))
                for n in range(2 * LG):
                    which, g = n % 2, n // 2
                    t0, cnt = g * GRP, min(GRP, TPC - g * GRP)
                    out = (lay.m_edge if which == 0 else lay.a_edge)[:].rearrange("p (c t) h -> p t c h", c=NC)
                    dve.wait_ge(s["turned"], n + 1)
                    for q in range(cnt):
                        ins = dve.tensor_copy(out[:, t0 + q, :, :],
                                              ps[n % 4][0:T, q * CH:(q + 1) * CH].rearrange("p (c h) -> p c h", h=H))
                    ins.then_inc(s["copied"], 1)

            @block.scalar
            def _(act):
                act.wait_ge(s["dve"], 18)
                act.activation(lg[:], lg[:], ACT.Exp).then_inc(s["exp"], 1)

            @block.tensor
            def _(pe):
                pe.wait_ge(s["lin_laid"], 1)
                for g in range(LG):
                    if g >= 4:
                        pe.wait_ge(s["lin_added"], g - 3)
                    for q in range(min(GRP, TPC - g * GRP)):
                        ins = pe.transpose(ps[g % 4][0:CH, q * T:(q + 1) * T], lin[:, g * GRP + q, :],
                                           k.ident[0:T, 0:T])
                    ins.then_inc(s["lin_turned"], 1)
                for n in range(2 * LG):
                    which, g = n % 2, n // 2
                    src = bw if which == 0 else lg
                    if n == 0:
                        pe.wait_ge(s["dve"], 19)
                    if n == 1:
                        pe.wait_ge(s["exp"], 1)
                    if n >= 4:
                        pe.wait_ge(s["copied"], n - 3)
                    for q in range(min(GRP, TPC - g * GRP)):
                        t = g * GRP + q
                        ins = pe.transpose(ps[n % 4][0:T, q * CH:(q + 1) * CH], src[:, t * T:(t + 1) * T],
                                           k.ident[0:CH, 0:CH])
                    ins.then_inc(s["turned"], 1)


def edge_sums(nc, k, lay):
    H = lay.H
    HV = WN * H // 128
    with ExitStack() as ctx:
        ph, nm = "b_", lay.nm + "b_"
        xs = [sbuf(nc, ctx, f"{nm}xs{r}", [T, Q, lay.XR]) for r in range(R)]
        oh = [sbuf(nc, ctx, f"{nm}oh{r}", [T, Q, WN]) for r in range(R)]
        p = [sbuf(nc, ctx, f"{nm}p{r}", [T, Q, WN * H]) for r in range(R)]
        acc = [sbuf(nc, ctx, f"{nm}acc{r}", [128, Q, HV * XW]) for r in range(R)]
        mx = sbuf(nc, ctx, nm + "mx", [WN, H, UT])
        mx_run = sbuf(nc, ctx, nm + "mx_run", [WN, UT, H])
        ps_v = [psum(nc, ctx, f"{nm}ps_v{j}") for j in range(Q)]
        ps_m = [psum(nc, ctx, f"{nm}ps_m{r}") for r in range(R)]
        s = {n: semaphore(nc, k, ph + n) for n in (
            "zero", "oh_ready", "p_ready", "v_ready", "m_ready", "m_copied", "chain", "act_step", "mx_run", "mx_st")}
        load = [semaphore(nc, k, f"{ph}load{r}") for r in range(R)]
        store = [semaphore(nc, k, f"{ph}store{r}") for r in range(R)]

        with nc.Block() as block:
            @block.sync
            def _(sp):
                def body(i, first, last):
                    for r in range(R):
                        u = i * R + r
                        if not first:
                            sp.wait_ge(s["v_ready"], Q * (u - R + 1))
                        sp.dma_start(xs[r][:].rearrange("p j f -> p (j f)"),
                                     lay.xs_d[bass.ds(u, 1), :, :].rearrange("u p f -> (u p) f")).then_inc(load[r], 16)
                loop3(sp, body)
                sp.wait_ge(s["mx_run"], H)
                sp.dma_start(lay.mx_d.rearrange("(n u) h -> n (u h)", u=UT),
                             mx_run[:].rearrange("n u h -> n (u h)")).then_inc(s["mx_st"], 16)
                sp.wait_ge(s["mx_st"], 16)

            @block.vector
            def _(dve):
                dve.memset(acc[R - 1][:, Q - 1, :], 0.0).then_inc(s["zero"], 1)

                def one_hot(u, r):
                    dve.tensor_tensor(oh[r][:], k.dst_local[:, bass.ds(u * Q, Q)].unsqueeze(2).to_broadcast([T, Q, WN]),
                                      k.node_in_window[:].unsqueeze(1).to_broadcast([T, Q, WN]),
                                      ALU.is_equal).then_inc(s["oh_ready"], 1)

                def weigh(u, r, j):
                    if j == 0:
                        dve.wait_ge(s["oh_ready"], u + 1)
                    dve.tensor_tensor(p[r][:, j, :].rearrange("p (n h) -> p n h", h=H),
                                      oh[r][:, j, :].unsqueeze(2).to_broadcast([T, WN, H]),
                                      lay.a_edge[:, bass.ds(u * Q + j, 1), :].to_broadcast([T, WN, H]),
                                      ALU.mult).then_inc(s["p_ready"], 1)

                def run(u, r, j, start):
                    dve.wait_ge(s["v_ready"], Q * u + j + 1)
                    if start:
                        dve.wait_ge(s["zero"], 1)
                    else:
                        dve.wait_ge(s["chain"], Q * u + j)
                    prev = acc[r][:, j - 1, :] if j else acc[(r + R - 1) % R][:, Q - 1, :]
                    dve.scalar_tensor_tensor(out=acc[r][:, j, :], in0=prev, scalar=k.same[:, bass.ds(u * Q + j, 1)],
                                             in1=ps_v[j][:, 0:HV * XW], op0=ALU.mult,
                                             op1=ALU.add).then_inc(s["chain"], 1)

                one_hot(0, 0)
                for j in range(Q):
                    weigh(0, 0, j)
                one_hot(1, 1)

                def body(i, first, last):
                    for r in range(R):
                        u = i * R + r
                        if not first:
                            dve.wait_ge(store[r], 16 * i)
                        for j in range(Q):
                            run(u, r, j, first and r == 0 and j == 0)
                            if j == Q - 1 and not (last and r >= R - 2):
                                one_hot(u + 2, (r + 2) % R)
                            if not (last and r == R - 1):
                                weigh(u + 1, (r + 1) % R, j)
                loop3(dve, body)
                dve.wait_ge(s["m_copied"], U)
                for h in range(H):
                    dve.tensor_tensor_scan(mx_run[:, :, h], k.same[0:WN, :], mx[:, h, :], 0.0,
                                           ALU.mult, ALU.add).then_inc(s["mx_run"], 1)

            @block.tensor
            def _(pe):
                def body(i, first, last):
                    for r in range(R):
                        u = i * R + r
                        if not first:
                            pe.wait_ge(s["m_copied"], u - R + 1)
                        pe.wait_ge(s["oh_ready"], u + 1)
                        pe.matmul(ps_m[r][:, 0:Q * H], oh[r][:].rearrange("p j n -> p (j n)"),
                                  lay.m_edge[:, bass.ds(u * Q, Q), :].rearrange("p j h -> p (j h)"),
                                  start=True, stop=True).then_inc(s["m_ready"], 1)
                        pe.wait_ge(load[r], 16 * (i + 1))
                        for j in range(Q):
                            pe.wait_ge(s["p_ready"], Q * u + j + 1)
                            if not (first and r == 0):
                                pe.wait_ge(s["chain"], Q * (u - 1) + j + 1)
                            for v in range(HV):
                                ins = pe.matmul(ps_v[j][:, v * XW:(v + 1) * XW], p[r][:, j, v * 128:(v + 1) * 128],
                                                xs[r][:, j, 0:XW], start=True, stop=True)
                            ins.then_inc(s["v_ready"], 1)
                loop3(pe, body)

            @block.scalar
            def _(act):
                def body(i, first, last):
                    for r in range(R):
                        u = i * R + r
                        act.wait_ge(s["m_ready"], u + 1)
                        act.sem_inc(s["act_step"], 1)
                        for j in range(Q):
                            ins = act.activation(mx[:, :, bass.ds(u * Q + j, 1)].rearrange("n h u -> n (h u)"),
                                                 ps_m[r][WN * j:WN * j + WN, j * H:(j + 1) * H], ACT.Copy)
                        ins.then_inc(s["m_copied"], 1)
                        act.wait_ge(s["chain"], Q * u + Q)
                        act.dma_start(bass.AP(lay.v_d.tensor, u * (Q * WN * H * XW),
                                              [[XW, 128], [WN * H * XW, Q], [128 * XW, HV], [1, XW]]),
                                      acc[r][:].rearrange("p j (v f) -> p j v f", v=HV)).then_inc(store[r], 16)
                loop3(act, body)
                for r in range(R):
                    act.wait_ge(store[r], 16 * (U // R))


def merge_nodes(nc, k, lay, finish):
    H = lay.H
    CK = H // 2
    TG = 5
    with ExitStack() as tmp:
        ph, nm = "n_", lay.nm + "n_"
        v = sbuf(nc, tmp, nm + "v", [T, NT, H * XW])
        m = sbuf(nc, tmp, nm + "m", [T, NT, H])
        den = sbuf(nc, tmp, nm + "den", [T, NT, H])
        me = sbuf(nc, tmp, nm + "me", [T, NT, H])
        be = sbuf(nc, tmp, nm + "be", [T, NT, H])
        ga = sbuf(nc, tmp, nm + "ga", [T, NT, H])
        agg = sbuf(nc, tmp, nm + "agg", [T, NT, H, D])
        selfx = sbuf(nc, tmp, nm + "selfx", [T, TG, H, D])
        aggT = [sbuf(nc, tmp, f"{nm}aggT{i}", [128, CK * T]) for i in range(2)]
        wl = sbuf(nc, tmp, nm + "wl", [128, CK, D])
        bias = sbuf(nc, tmp, nm + "bias", [T, D])
        o = sbuf(nc, tmp, nm + "o", [T, NT, D])
        ps_t = [psum(nc, tmp, f"{nm}ps_t{i}") for i in range(2)]
        ps_o = [psum(nc, tmp, f"{nm}ps_o{i}") for i in range(2)]
        s = {n: semaphore(nc, k, ph + n) for n in (
            "load", "dve", "exp", "agg", "turned", "copied", "proj", "out", "fin", "finb", "store")}
        s["gather"] = semaphore(nc, k, nm + "gather")
        with nc.Block() as block:
            @block.gpsimd
            def _(pool):
                for t in range(NT):
                    pool.indirect_dma_start(v[:, t, :], None, lay.v_d,
                                            bass.IndirectOffsetOnAxis(k.row_idx[:, t:t + 1], 0)).then_inc(s["gather"], 16)
                    pool.indirect_dma_start(m[:, t, :], None, lay.mx_d,
                                            bass.IndirectOffsetOnAxis(k.row2_idx[:, t:t + 1], 0)).then_inc(s["gather"], 16)
                pool.wait_ge(s["gather"], 32 * NT)

            @block.sync
            def _(sp):
                ld = Dma(sp, s["load"])
                wsrc = lay.Wl.rearrange("d (c b f) -> b d c f", b=2, f=D)
                for b in range(2):
                    ld.start(wl[b * D:(b + 1) * D, :, :], wsrc[b])
                ld.start(bias[:], bass.AP(lay.bias.tensor, 0, [[0, T], [1, D]]))
                ld.wait()

            @block.vector
            def _(dve):
                link = Link(dve, s["dve"])
                flat = lambda x: x[:].rearrange("p t h -> p (t h)")
                one = v[:].rearrange("p t (h f) -> p (t h) f", f=XW)
                sums = one[:, :, D]
                dve.wait_ge(s["gather"], 32 * NT)
                link(dve.tensor_scalar(flat(me), sums, 0.5, -2 * BIG, ALU.is_lt, ALU.mult))
                link(dve.tensor_tensor(flat(me), flat(me), flat(m), ALU.add))
                link(dve.tensor_tensor(flat(m), flat(me), flat(lay.self_logit), ALU.max))
                link(dve.tensor_tensor(flat(be), flat(me), flat(m), ALU.subtract))
                link(dve.tensor_tensor(flat(ga), flat(lay.self_logit), flat(m), ALU.subtract))
                dve.wait_ge(s["exp"], 2)
                link(dve.tensor_tensor(flat(den), sums, flat(be), ALU.mult))
                link(dve.tensor_tensor(flat(den), flat(den), flat(ga), ALU.add))
                link(dve.reciprocal(flat(den), flat(den)))
                link(dve.tensor_tensor(flat(be), flat(be), flat(den), ALU.mult))
                link(dve.tensor_tensor(flat(ga), flat(ga), flat(den), ALU.mult))
                n0 = link.n
                for g in range(NT // TG):
                    t = slice(g * TG, (g + 1) * TG)
                    th = slice(g * TG * H, (g + 1) * TG * H)
                    ag = agg[:].rearrange("p t h f -> p (t h) f")[:, th, :]
                    link(dve.tensor_tensor(selfx[:], lay.x_node[:, t, :].unsqueeze(2).to_broadcast([T, TG, H, D]),
                                           ga[:, t, :].unsqueeze(3).to_broadcast([T, TG, H, D]), ALU.mult))
                    link(dve.tensor_tensor(ag, one[:, th, 0:D],
                                           flat(be)[:, th].unsqueeze(2).to_broadcast([T, TG * H, D]), ALU.mult))
                    dve.tensor_tensor(ag, ag, selfx[:].rearrange("p t h f -> p (t h) f"), ALU.add).then_inc(s["agg"], 1)
                    dve.wait_ge(s["agg"], g + 1)
                dve.wait_ge(s["load"], 48)
                for t in range(NT):
                    dve.wait_ge(s["proj"], t + 1)
                    dve.scalar_tensor_tensor(out=o[:, t, :], in0=ps_o[t % 2][0:T, 0:D], scalar=1.0 / H, in1=bias[:],
                                             op0=ALU.mult, op1=ALU.add).then_inc(s["out"], 1)

            @block.scalar
            def _(act):
                act.wait_ge(s["dve"], 4)
                act.activation(be[:], be[:], ACT.Exp).then_inc(s["exp"], 1)
                act.wait_ge(s["dve"], 5)
                act.activation(ga[:], ga[:], ACT.Exp).then_inc(s["exp"], 1)
                for t in range(NT):
                    act.wait_ge(s["turned"], t + 1)
                    if t >= 2:
                        act.wait_ge(s["proj"], t - 1)
                    act.activation(aggT[t % 2][:], ps_t[t % 2][:, 0:CK * T], ACT.Copy).then_inc(s["copied"], 1)

            @block.tensor
            def _(pe):
                pe.wait_ge(s["load"], 48)

                def turn(t):
                    pe.wait_ge(s["agg"], t // TG + 1)
                    if t >= 2:
                        pe.wait_ge(s["copied"], t - 1)
                    for c in range(CK):
                        ins = pe.transpose(ps_t[t % 2][:, c * T:(c + 1) * T],
                                           agg[:, t, 2 * c:2 * c + 2, :].rearrange("p h f -> p (h f)"), k.ident[0:T, 0:T])
                    ins.then_inc(s["turned"], 1)

                turn(0)
                for t in range(NT):
                    if t + 1 < NT:
                        turn(t + 1)
                    pe.wait_ge(s["copied"], t + 1)
                    if t >= 2:
                        pe.wait_ge(s["out"], t - 1)
                    for c in range(CK):
                        ins = pe.matmul(ps_o[t % 2][0:T, 0:D], aggT[t % 2][:, c * T:(c + 1) * T], wl[:, c, :],
                                        start=(c == 0), stop=(c == CK - 1))
                    ins.then_inc(s["proj"], 1)

        with nc.Block() as block:
            @block.vector
            def _(dve):
                finish(dve, Link(dve, s["fin"]), s["finb"], o)

            @block.scalar
            def _(act):
                if lay.norm:
                    act.wait_ge(s["fin"], 6)
                    act.activation(lay.std[:], lay.var[:], ACT.Sqrt).then_inc(s["finb"], 1)

            @block.sync
            def _(sp):
                sp.wait_ge(s["fin"], lay.fin_steps)
                sp.dma_start(lay.next_table.rearrange("(p t) d -> p t d", t=NT), lay.next_node[:]).then_inc(s["store"], 16)
                sp.wait_ge(s["store"], 16)


def layer_norm(dve, link, std_ready, x, y, sq, mean, var, std, out):
    bc = lambda v: v[:].unsqueeze(2).to_broadcast([T, NT, D])
    link(dve.tensor_tensor(out[:], x[:], y[:], ALU.add))
    link(dve.tensor_reduce(mean[:], out[:], AX.X, ALU.add))
    link(dve.tensor_scalar(mean[:], mean[:], 1.0 / D, None, ALU.mult))
    link(dve.tensor_tensor(out[:], out[:], bc(mean), ALU.subtract))
    dve.tensor_tensor(sq[:], out[:], out[:], ALU.mult).then_inc(std_ready, 1)
    dve.wait_ge(std_ready, 1)
    link(dve.tensor_reduce(var[:], sq[:], AX.X, ALU.add))
    link(dve.tensor_scalar(var[:], var[:], 1.0 / D, EPS, ALU.mult, ALU.add))
    dve.wait_ge(std_ready, 2)
    link(dve.reciprocal(std[:], std[:]))
    link(dve.tensor_tensor(out[:], out[:], bc(std), ALU.mult))


def neighbour_sums(nc, k, table):
    with ExitStack() as ctx:
        nm = "g_"
        idx = [sbuf(nc, ctx, f"{nm}idx{r}", [T, Q], I32) for r in range(R)]
        xs = [sbuf(nc, ctx, f"{nm}xs{r}", [T, Q, D]) for r in range(R)]
        oh = [sbuf(nc, ctx, f"{nm}oh{r}", [T, Q, WN]) for r in range(R)]
        acc = [sbuf(nc, ctx, f"{nm}acc{r}", [WN, Q, D]) for r in range(R)]
        ps = [psum(nc, ctx, f"{nm}ps{r}") for r in range(R)]
        s = {n: semaphore(nc, k, nm + n) for n in (
            "idx_staged", "pool_step", "act_step", "zero", "oh_ready", "sum_ready", "chain")}
        gath = [semaphore(nc, k, f"{nm}gath{r}") for r in range(R)]
        store = [semaphore(nc, k, f"{nm}store{r}") for r in range(R)]
        with nc.Block() as block:
            @block.scalar
            def _(act):
                def stage(u, r):
                    act.activation(idx[r][:], k.src_idx[:, bass.ds(u * Q, Q)], ACT.Copy).then_inc(s["idx_staged"], 1)

                for r in range(R):
                    stage(r, r)

                def body(i, first, last):
                    for r in range(R):
                        if not last:
                            act.wait_ge(gath[r], 16 * Q * (i + 1))
                            act.sem_inc(s["act_step"], 1)
                            stage(i * R + r + R, r)
                loop3(act, body)

            @block.gpsimd
            def _(pool):
                def body(i, first, last):
                    for r in range(R):
                        u = i * R + r
                        if not first:
                            pool.wait_ge(s["sum_ready"], u - R + 1)
                            pool.sem_inc(s["pool_step"], 1)
                        pool.wait_ge(s["idx_staged"], u + 1)
                        pool.sem_inc(s["pool_step"], 1)
                        for j in range(Q):
                            pool.indirect_dma_start(xs[r][:, j, :], None, table,
                                                    bass.IndirectOffsetOnAxis(idx[r][:, j:j + 1], 0)).then_inc(gath[r], 16)
                loop3(pool, body)

            @block.vector
            def _(dve):
                dve.memset(acc[R - 1][:, Q - 1, :], 0.0).then_inc(s["zero"], 1)

                def one_hot(u, r, free):
                    if free:
                        dve.wait_ge(s["sum_ready"], u - R + 1)
                    dve.tensor_tensor(oh[r][:], k.dst_local[:, bass.ds(u * Q, Q)].unsqueeze(2).to_broadcast([T, Q, WN]),
                                      k.node_in_window[:].unsqueeze(1).to_broadcast([T, Q, WN]),
                                      ALU.is_equal).then_inc(s["oh_ready"], 1)

                one_hot(0, 0, False)

                def body(i, first, last):
                    for r in range(R):
                        u = i * R + r
                        if not (last and r == R - 1):
                            one_hot(u + 1, (r + 1) % R, not (first and r + 1 < R))
                        dve.wait_ge(s["sum_ready"], u + 1)
                        if not first:
                            dve.wait_ge(store[r], 16 * i)
                        for j in range(Q):
                            if first and r == 0 and j == 0:
                                dve.wait_ge(s["zero"], 1)
                            else:
                                dve.wait_ge(s["chain"], Q * u + j)
                            prev = acc[r][:, j - 1, :] if j else acc[(r + R - 1) % R][:, Q - 1, :]
                            dve.scalar_tensor_tensor(out=acc[r][:, j, :], in0=prev,
                                                     scalar=k.same[0:WN, bass.ds(u * Q + j, 1)],
                                                     in1=ps[r][0:WN, j * D:(j + 1) * D], op0=ALU.mult,
                                                     op1=ALU.add).then_inc(s["chain"], 1)
                loop3(dve, body)

            @block.tensor
            def _(pe):
                def body(i, first, last):
                    for r in range(R):
                        u = i * R + r
                        pe.wait_ge(s["oh_ready"], u + 1)
                        pe.wait_ge(gath[r], 16 * Q * (i + 1))
                        if not first:
                            pe.wait_ge(s["chain"], Q * (u - R + 1))
                        for j in range(Q):
                            ins = pe.matmul(ps[r][0:WN, j * D:(j + 1) * D], oh[r][:, j, :], xs[r][:, j, :],
                                            start=True, stop=True)
                        ins.then_inc(s["sum_ready"], 1)
                loop3(pe, body)

            @block.sync
            def _(sp):
                def body(i, first, last):
                    for r in range(R):
                        u = i * R + r
                        sp.wait_ge(s["chain"], Q * u + Q)
                        sp.dma_start(bass.AP(k.sum_d.tensor, u * (Q * WN * D), [[D, WN], [WN * D, Q], [1, D]]),
                                     acc[r][:]).then_inc(store[r], 16)
                loop3(sp, body)
                for r in range(R):
                    sp.wait_ge(store[r], 16 * (U // R))


def dense_layers(nc, k, a, out, x_node):
    KC = HID // 128
    BW = 500
    with ExitStack() as tmp:
        nm = "d_"
        agg = sbuf(nc, tmp, nm + "agg", [T, NT, D])
        hT = sbuf(nc, tmp, nm + "hT", [D, N])
        h1 = sbuf(nc, tmp, nm + "h1", [128, KC, N])
        h2 = sbuf(nc, tmp, nm + "h2", [128, KC, N])
        w1 = sbuf(nc, tmp, nm + "w1", [D, HID])
        w2 = sbuf(nc, tmp, nm + "w2", [128, KC, HID])
        w3 = sbuf(nc, tmp, nm + "w3", [128, KC, D])
        b1 = sbuf(nc, tmp, nm + "b1", [128, KC])
        b2 = sbuf(nc, tmp, nm + "b2", [128, KC])
        b3 = sbuf(nc, tmp, nm + "b3", [T, D])
        o = sbuf(nc, tmp, nm + "o", [T, NT, D])
        y = sbuf(nc, tmp, nm + "y", [T, NT, D])
        sq = sbuf(nc, tmp, nm + "sq", [T, NT, D])
        mean, var, std = (sbuf(nc, tmp, nm + n, [T, NT]) for n in ("mean", "var", "std"))
        ps = [psum(nc, tmp, f"{nm}ps{i}") for i in range(4)]
        ps_o = [psum(nc, tmp, f"{nm}ps_o{i}") for i in range(2)]
        s = {n: semaphore(nc, k, nm + n) for n in (
            "load", "gather", "dve", "turned", "copied", "mm1", "mm2", "mm3", "h1", "h2", "out", "fin", "finb", "store")}
        blocks = [(n0, min(BW, N - n0)) for n0 in range(0, N, BW)]
        NBK = len(blocks)
        with nc.Block() as block:
            @block.gpsimd
            def _(pool):
                for t in range(NT):
                    pool.indirect_dma_start(agg[:, t, :], None, k.sum_d,
                                            bass.IndirectOffsetOnAxis(k.row_idx[:, t:t + 1], 0)).then_inc(s["gather"], 16)
                pool.wait_ge(s["gather"], 16 * NT)

            @block.sync
            def _(sp):
                ld = Dma(sp, s["load"])
                ld.start(w1[:], a["L1_gnn_W1"])
                ld.start(w2[:], a["L1_gnn_W2"].rearrange("(c p) f -> p c f", p=128))
                ld.start(w3[:], a["L1_gnn_W3"].rearrange("(c p) f -> p c f", p=128))
                ld.start(b1[:], a["L1_gnn_b1"].rearrange("(c p) -> p c", p=128), elements=True)
                ld.start(b2[:], a["L1_gnn_b2"].rearrange("(c p) -> p c", p=128), elements=True)
                ld.start(b3[:], bass.AP(a["L1_gnn_b3"].tensor, 0, [[0, T], [1, D]]))
                ld.wait()
                sp.wait_ge(s["fin"], 8)
                sp.dma_start(out.rearrange("(p t) d -> p t d", t=NT), y[:]).then_inc(s["store"], 16)
                sp.wait_ge(s["store"], 16)

            @block.vector
            def _(dve):
                dve.wait_ge(s["gather"], 16 * NT)
                dve.tensor_tensor(agg[:], agg[:], x_node[:], ALU.add).then_inc(s["dve"], 1)
                for t in range(NT):
                    dve.wait_ge(s["turned"], t + 1)
                    dve.tensor_copy(hT[:, t * T:(t + 1) * T], ps[t % 4][0:D, 0:T]).then_inc(s["copied"], 1)
                dve.wait_ge(s["load"], 96)
                for t in range(NT):
                    dve.wait_ge(s["mm3"], t + 1)
                    dve.tensor_tensor(o[:, t, :], ps_o[t % 2][0:T, 0:D], b3[:], ALU.add).then_inc(s["out"], 1)
                dve.wait_ge(s["out"], NT)
                layer_norm(dve, Link(dve, s["fin"]), s["finb"], x_node, o, sq, mean, var, std, y)

            @block.tensor
            def _(pe):
                pe.wait_ge(s["dve"], 1)
                for t in range(NT):
                    if t >= 4:
                        pe.wait_ge(s["copied"], t - 3)
                    pe.transpose(ps[t % 4][0:D, 0:T], agg[:, t, :], k.ident[0:T, 0:T]).then_inc(s["turned"], 1)
                pe.wait_ge(s["copied"], NT)
                pe.wait_ge(s["load"], 96)
                n = 0
                for n0, w in blocks:
                    for c in range(KC):
                        if n >= 4:
                            pe.wait_ge(s["h1"], n - 3)
                        pe.matmul(ps[n % 4][:, 0:w], w1[:, c * 128:(c + 1) * 128], hT[:, n0:n0 + w],
                                  start=True, stop=True).then_inc(s["mm1"], 1)
                        n += 1
                pe.wait_ge(s["h1"], KC * NBK)
                n = 0
                for n0, w in blocks:
                    for c in range(KC):
                        if n >= 4:
                            pe.wait_ge(s["h2"], n - 3)
                        for kc in range(KC):
                            ins = pe.matmul(ps[n % 4][:, 0:w], w2[:, kc, c * 128:(c + 1) * 128], h1[:, kc, n0:n0 + w],
                                            start=(kc == 0), stop=(kc == KC - 1))
                        ins.then_inc(s["mm2"], 1)
                        n += 1
                pe.wait_ge(s["h2"], KC * NBK)
                for t in range(NT):
                    if t >= 2:
                        pe.wait_ge(s["out"], t - 1)
                    for kc in range(KC):
                        ins = pe.matmul(ps_o[t % 2][0:T, 0:D], h2[:, kc, t * T:(t + 1) * T], w3[:, kc, :],
                                        start=(kc == 0), stop=(kc == KC - 1))
                    ins.then_inc(s["mm3"], 1)

            @block.scalar
            def _(act):
                act.wait_ge(s["load"], 96)
                for ready, done, h, bias in ((s["mm1"], s["h1"], h1, b1), (s["mm2"], s["h2"], h2, b2)):
                    n = 0
                    for n0, w in blocks:
                        for c in range(KC):
                            act.wait_ge(ready, n + 1)
                            act.activation(h[:, c, n0:n0 + w], ps[n % 4][:, 0:w], ACT.Relu,
                                           bias=bias[:, c:c + 1]).then_inc(done, 1)
                            n += 1
                act.wait_ge(s["fin"], 6)
                act.activation(std[:], var[:], ACT.Sqrt).then_inc(s["finb"], 1)


def build(nc, a, out):
    ctx = ExitStack()
    k = Program(ctx)

    def dram(name, shape, dt=F32):
        return nc.dram_tensor(name, shape, dt, kind="Internal").ap()

    with ctx:
        k.key_d = dram("key_d", [G])
        k.w_d = dram("w_d", [UT])
        k.keys_d = dram("keys_d", [SLOTS + 2])
        k.row_d = dram("row_d", [NW * WN], I32)
        k.row2_d = dram("row2_d", [NW * WN], I32)
        k.xw_d = dram("xw_d", [UT, WN * D])
        k.sum_d = dram("sum_d", [UT * WN, D])
        build_staircase(nc, k, a, ctx)

        x0 = sbuf(nc, ctx, "x0", [T, NT, D])
        x1 = sbuf(nc, ctx, "x1", [T, NT, D])
        load_x = semaphore(nc, k, "load_x")
        with nc.Block() as block:
            @block.sync
            def _(sp):
                sp.dma_start(x0[:], a["x"].rearrange("(p t) d -> p t d", t=NT)).then_inc(load_x, 16)
                sp.wait_ge(load_x, 16)

        x1_d = dram("x1_d", [N, D])
        nodes = [x0, x1, x1]
        for n, H in enumerate((a["L0_gnn_att1"].shape[0], a["L0_gnn_att2"].shape[0])):
            nm = f"L{n + 1}_"
            lay = Layer(nm=nm, H=H, Wl=a[f"L0_gnn_W{n + 1}l"], Wr=a[f"L0_gnn_W{n + 1}r"],
                                  att=a[f"L0_gnn_att{n + 1}"], bias=a[f"L0_gnn_b{n + 1}"],
                                  x_node=nodes[n], next_table=x1_d, next_node=nodes[n + 1],
                                  logit_d=dram(nm + "logit_d", [H, SLOTS]), norm=n == 1,
                                  v_d=dram(nm + "v_d", [UT * WN, H * XW]), mx_d=dram(nm + "mx_d", [WN * UT, H]))
            if n == 0:
                before = set(k.sems)
            else:
                with nc.Block() as block:
                    @block.gpsimd
                    def _(pool):
                        for name in sorted(n for n in set(k.sems) - before if not n.startswith("L1_")):
                            pool.sem_clear(k.sems[name])
            with ExitStack() as lctx:
                if lay.norm:
                    lay.sq = sbuf(nc, lctx, nm + "sq", [T, NT, D])
                    lay.mean, lay.var, lay.std = (sbuf(nc, lctx, nm + v, [T, NT]) for v in ("mean", "var", "std"))
                    lay.fin_steps = 8

                    def finish(dve, link, finb, o, lay=lay):
                        layer_norm(dve, link, finb, x0, o, lay.sq, lay.mean, lay.var, lay.std, lay.next_node)
                else:
                    lay.fin_steps = 1

                    def finish(dve, link, finb, o, lay=lay):
                        link(dve.tensor_scalar(lay.next_node[:], o[:], 0.0, None, ALU.max))
                prepare_layer(nc, k, lctx, lay)
                lay.xs_d = dram(nm + "xs_d", [U, T, Q * lay.XR])
                with ExitStack() as ectx:
                    lay.a_edge = sbuf(nc, ectx, nm + "a_edge", [T, UT, H])
                    lay.m_edge = sbuf(nc, ectx, nm + "m_edge", [T, UT, H])
                    lay.lin_edge = lay.a_edge
                    edge_logits(nc, k, lay)
                    edge_softmax(nc, k, lay)
                    edge_sums(nc, k, lay)
                merge_nodes(nc, k, lay, finish)
        neighbour_sums(nc, k, x1_d)
        dense_layers(nc, k, a, out, x1)


_INS = ["x", "src", "dst", "L0_gnn_W1l", "L0_gnn_W1r", "L0_gnn_att1", "L0_gnn_b1", "L0_gnn_W2l", "L0_gnn_W2r",
        "L0_gnn_att2", "L0_gnn_b2", "L1_gnn_W1", "L1_gnn_b1", "L1_gnn_W2", "L1_gnn_b2", "L1_gnn_W3", "L1_gnn_b3"]


def kernel(**inputs):
    import numpy as np
    import concourse.bacc as bacc
    from concourse import mybir as _mybir
    from concourse.bass_utils import run_bass_kernel_spmd

    nc = bacc.Bacc("TRN2", target_bir_lowering=False, num_devices=1)
    arrays, args = {}, {}
    for name in _INS:
        arr = np.ascontiguousarray(inputs[name])
        arrays[f"in_{name}_dram"] = arr
        args[name] = nc.dram_tensor(f"in_{name}_dram", arr.shape, _mybir.dt.from_np(arr.dtype),
                                    kind="ExternalInput").ap()
    out = nc.dram_tensor("out_dram", (N, D), _mybir.dt.float32, kind="ExternalOutput").ap()
    build(nc, args, out)
    r = run_bass_kernel_spmd(nc, [arrays], core_ids=[0])
    return r.results[0]["out_dram"]
```

```python
from contextlib import ExitStack

import concourse.bass as bass
from concourse import mybir

F32 = mybir.dt.float32
I32 = mybir.dt.int32
ALU = mybir.AluOpType
ACT = mybir.ActivationFunctionType
AX = mybir.AxisListType

N, D, E = 3125, 64, 100000
HID = 256
SLOPE = 0.2
EPS = 1e-5
T = 125
G = E // T
WN = 32
NW = -(-N // WN)
Q = 4
R = 3
U = -(-(G + NW - 1) // (Q * R)) * R
UT = U * Q
SLOTS = UT * T
QT = Q * T
NT = N // T
BLK = 100
NB = UT // BLK
GQ, GR = 4, 4
GU = G // GQ
KT = G // BLK
CH = 120
BIG = 1.5e38
XW = D + 1
PAD = NW * WN
assert UT % BLK == 0 and N % T == 0 and E % T == 0 and U % R == 0 and G % BLK == 0 and GU % GR == 0


class Program:

    def __init__(self, ctx):
        self.ctx, self.sems = ctx, {}


class Layer:

    def __init__(self, nm, H, Wl, Wr, att, bias, x_node, next_table, next_node, logit_d, v_d, max_d, norm):
        self.nm, self.H, self.Wl, self.Wr, self.att, self.bias = nm, H, Wl, Wr, att, bias
        self.x_node, self.next_table, self.next_node = x_node, next_table, next_node
        self.logit_d, self.v_d, self.max_d, self.norm = logit_d, v_d, max_d, norm


class Link:

    def __init__(self, eng, sem):
        self.eng, self.sem, self.n = eng, sem, 0

    def __call__(self, ins):
        self.n += 1
        ins.then_inc(self.sem, 1)
        self.eng.wait_ge(self.sem, self.n)


class Dma:

    def __init__(self, eng, sem):
        self.eng, self.sem, self.n = eng, sem, 0

    def start(self, out, in_, elements=False):
        self.n += 16
        self.eng.dma_start(out, in_, allow_slow_non_contiguous=elements).then_inc(self.sem, 16)

    def wait(self):
        self.eng.wait_ge(self.sem, self.n)


def peeled(eng, count, body):
    body(0, True, False)
    with eng.Fori(1, count - 1) as i:
        body(i, False, False)
    body(count - 1, False, True)


def loop3(eng, body):
    peeled(eng, U // R, body)


def sbuf(nc, ctx, name, shape, dt=F32):
    return ctx.enter_context(nc.sbuf_tensor(name, shape, dt))


def psum(nc, ctx, name, shape=(128, 512)):
    return ctx.enter_context(nc.psum_tensor(name, list(shape), F32))


def semaphore(nc, k, name):
    if name not in k.sems:
        k.sems[name] = k.ctx.enter_context(nc.semaphore(name))
    return k.sems[name]


def build_staircase(nc, k, a, ctx0):
    k.ident = sbuf(nc, ctx0, "ident", [128, 128])
    k.node_in_window = sbuf(nc, ctx0, "node_in_window", [T, WN])
    k.dst_local = sbuf(nc, ctx0, "dst_local", [T, UT])
    k.src_idx = sbuf(nc, ctx0, "src_idx", [T, UT], I32)
    k.win_idx = sbuf(nc, ctx0, "win_idx", [BLK, NB], I32)
    k.same = sbuf(nc, ctx0, "same", [128, UT])
    k.row_idx = sbuf(nc, ctx0, "row_idx", [T, NT], I32)
    k.max_idx = sbuf(nc, ctx0, "max_idx", [T, NT], I32)
    k.edge_idx = sbuf(nc, ctx0, "edge_idx", [T, NT], I32)
    k.src_tile = sbuf(nc, ctx0, "src_tile", [T, G], I32)
    k.pcol = sbuf(nc, ctx0, "pcol", [128, 1])

    with ExitStack() as ctx:
        dg = sbuf(nc, ctx, "dg", [BLK, G // BLK, T], I32)
        gnum_i = sbuf(nc, ctx, "gnum_i", [BLK, G // BLK], I32)
        ucol_i = sbuf(nc, ctx, "ucol_i", [BLK, NB], I32)
        pcol_i = sbuf(nc, ctx, "pcol_i", [128, 1], I32)
        niw_i = sbuf(nc, ctx, "niw_i", [T, WN], I32)
        lastw_i = sbuf(nc, ctx, "lastw_i", [BLK, G // BLK], I32)
        gnum = sbuf(nc, ctx, "gnum", [BLK, G // BLK])
        key = sbuf(nc, ctx, "key", [BLK, G // BLK])
        ucol = sbuf(nc, ctx, "ucol", [BLK, NB])
        key_all = sbuf(nc, ctx, "key_all", [BLK, G])
        cmp = sbuf(nc, ctx, "cmp", [128, UT])
        gcnt = sbuf(nc, ctx, "gcnt", [BLK, NB])
        gidx = sbuf(nc, ctx, "gidx", [BLK, NB], I32)
        wcol = sbuf(nc, ctx, "wcol", [BLK, NB])
        w32 = sbuf(nc, ctx, "w32", [BLK, NB])
        wrow = sbuf(nc, ctx, "wrow", [128, UT])
        win_f = sbuf(nc, ctx, "win_f", [BLK, NB])
        wcnt = sbuf(nc, ctx, "wcnt", [NW, 1])
        wl32 = sbuf(nc, ctx, "wl32", [NW, 1])
        rowf = sbuf(nc, ctx, "rowf", [NW, WN])
        rowi = sbuf(nc, ctx, "rowi", [NW, WN], I32)
        sg = sbuf(nc, ctx, "sg", [BLK, KT, T], I32)
        sgf = sbuf(nc, ctx, "sgf", [BLK, KT, T])
        dgf = sbuf(nc, ctx, "dgf", [BLK, KT * T])
        dprev_i = sbuf(nc, ctx, "dprev_i", [BLK, 1], I32)
        dprev = sbuf(nc, ctx, "dprev", [BLK, 1])
        same_edge = sbuf(nc, ctx, "same_edge", [BLK, KT * T])
        lastd = sbuf(nc, ctx, "lastd", [BLK, KT])
        last_all = sbuf(nc, ctx, "last_all", [T, G])
        node_i = sbuf(nc, ctx, "node_i", [T, NT], I32)
        nodew_i = sbuf(nc, ctx, "nodew_i", [T, NT], I32)
        node_half = sbuf(nc, ctx, "node_half", [T, NT])
        node_win = sbuf(nc, ctx, "node_win", [T, NT])
        side = sbuf(nc, ctx, "side", [T, G])
        side2 = sbuf(nc, ctx, "side2", [T, T])
        tiles_upto = sbuf(nc, ctx, "tiles_upto", [T, NT])
        tile_i = sbuf(nc, ctx, "tile_i", [T, NT], I32)
        dst_of = sbuf(nc, ctx, "dst_of", [T, NT, T], I32)
        edges_upto = sbuf(nc, ctx, "edges_upto", [T, NT])
        none = sbuf(nc, ctx, "none", [T, NT])
        place = sbuf(nc, ctx, "place", [T, NT])
        idxf = sbuf(nc, ctx, "idxf", [T, NT])
        srcu = sbuf(nc, ctx, "srcu", [BLK, NB * T], I32)
        dstu = sbuf(nc, ctx, "dstu", [BLK, NB * T], I32)
        srcf = sbuf(nc, ctx, "srcf", [BLK, NB * T])
        dstf = sbuf(nc, ctx, "dstf", [BLK, NB * T])
        dl = sbuf(nc, ctx, "dl", [BLK, NB * T])
        ge0 = sbuf(nc, ctx, "ge0", [BLK, NB * T])
        keyu = sbuf(nc, ctx, "keyu", [BLK, NB * T])
        keyp = sbuf(nc, ctx, "keyp", [BLK, NB * T])
        no_key = sbuf(nc, ctx, "no_key", [1, 1])
        no_more = sbuf(nc, ctx, "no_more", [1, 1])
        ps = [psum(nc, ctx, f"ps_setup{i}") for i in range(6)]
        s = {n: semaphore(nc, k, "st_" + n) for n in (
            "load", "iota", "ident0", "ident", "dve", "dve2", "dve3", "gather", "store", "transposed", "pad",
            "load2", "sides", "last", "upto2", "node", "keys", "lim")}
        s["gather2"] = semaphore(nc, k, "st_gather2")

        with nc.Block() as block:
            @block.sync
            def _(sp):
                sp.dma_start(dg[:], a["dst"].rearrange("(p k e) -> p k e", k=KT, e=T)).then_inc(s["load"], 16)
                ld = Dma(sp, s["load2"])
                ld.start(sg[:], a["src"].rearrange("(p k e) -> p k e", k=KT, e=T))
                sp.wait_ge(s["pad"], 3)
                ld.start(dprev_i[1:BLK, :], bass.AP(a["dst"].tensor, KT * T - 1, [[KT * T, BLK - 1], [1, 1]]), elements=True)
                ld.wait()
                sp.wait_ge(s["dve"], 4)
                st = Dma(sp, s["store"])
                st.start(k.key_d.rearrange("(p k) -> p k", k=G // BLK), key[:])
                st.wait()
                st.start(key_all[:], bass.AP(k.key_d.tensor, 0, [[0, BLK], [1, G]]))
                sp.wait_ge(s["dve"], 8)
                la = Dma(sp, s["last"])
                la.start(k.last_d.rearrange("(p k) -> p k", k=KT), lastd[:])
                la.wait()
                la.start(last_all[:], bass.AP(k.last_d.tensor, 0, [[0, T], [1, G]]))
                sp.wait_ge(s["dve"], 15)
                la.start(k.same_d.rearrange("(p e) -> p e", p=BLK), same_edge[:])
                st.wait()
                la.wait()

            @block.gpsimd
            def _(pool):
                pool.iota(gnum_i[:], [[1, G // BLK]], base=0, channel_multiplier=G // BLK).then_inc(s["iota"], 1)
                pool.iota(ucol_i[:], [[BLK, NB]], base=0, channel_multiplier=1).then_inc(s["iota"], 1)
                pool.iota(pcol_i[:], [[0, 1]], base=0, channel_multiplier=1).then_inc(s["iota"], 1)
                pool.iota(niw_i[:], [[1, WN]], base=0, channel_multiplier=0).then_inc(s["iota"], 1)
                pool.memset(k.ident[:], 0.0).then_inc(s["ident0"], 1)
                pool.memset(no_key[:], -5.0).then_inc(s["pad"], 1)
                pool.memset(no_more[:], -BIG).then_inc(s["pad"], 1)
                pool.memset(dprev_i[:], -1).then_inc(s["pad"], 1)
                pool.iota(node_i[:], [[1, NT]], base=0, channel_multiplier=NT).then_inc(s["iota"], 1)
                pool.wait_ge(s["ident0"], 1)
                pool.affine_select(out=k.ident[:], in_=k.ident[:], compare_op=ALU.not_equal, fill=1.0,
                                   base=0, pattern=[[-1, 128]], channel_multiplier=1).then_inc(s["ident"], 1)

            @block.vector
            def _(dve):
                link = Link(dve, s["dve"])
                dve.wait_ge(s["load"], 16)
                dve.wait_ge(s["iota"], 5)
                link(dve.tensor_scalar(lastw_i[:], dg[:, :, T - 1], 5, None, ALU.arith_shift_right))
                link(dve.tensor_copy(key[:], lastw_i[:]))
                link(dve.tensor_copy(gnum[:], gnum_i[:]))
                link(dve.tensor_tensor(key[:], key[:], gnum[:], ALU.add))
                link(dve.tensor_copy(ucol[:], ucol_i[:]))
                link(dve.tensor_copy(k.pcol[:], pcol_i[:]))
                link(dve.tensor_copy(k.node_in_window[:], niw_i[:]))
                link(dve.tensor_copy(lastd[:], dg[:, :, T - 1]))
                link(dve.tensor_scalar(nodew_i[:], node_i[:], 5, None, ALU.arith_shift_right))
                link(dve.tensor_copy(node_win[:], nodew_i[:]))
                link(dve.tensor_scalar(node_half[:], node_i[:], 0.5, None, ALU.add))
                dve.wait_ge(s["load2"], 32)
                link(dve.tensor_copy(dgf[:], dg[:].rearrange("p k e -> p (k e)")))
                link(dve.tensor_copy(dprev[:], dprev_i[:]))
                link(dve.tensor_tensor(same_edge[:, 1:KT * T], dgf[:, 1:KT * T], dgf[:, 0:KT * T - 1], ALU.is_equal))
                link(dve.tensor_tensor(same_edge[:, 0:1], dgf[:, 0:1], dprev[:], ALU.is_equal))
                link(dve.tensor_copy(sgf[:], sg[:]))

        with nc.Block() as block:
            @block.vector
            def _(dve):
                link = Link(dve, s["dve2"])
                for b in range(NB):
                    link(dve.tensor_scalar(cmp[0:BLK, 0:G], key_all[:], ucol[:, b:b + 1], None, ALU.is_lt))
                    link(dve.tensor_reduce(gcnt[:, b:b + 1], cmp[0:BLK, 0:G], AX.X, ALU.add))
                link(dve.tensor_scalar(gcnt[:], gcnt[:], float(G - 1), None, ALU.min))
                link(dve.tensor_copy(gidx[:], gcnt[:]))
                link(dve.tensor_tensor(wcol[:], ucol[:], gcnt[:], ALU.subtract))
                link(dve.tensor_scalar(w32[:], wcol[:], float(WN), None, ALU.mult))

            @block.gpsimd
            def _(pool):
                pool.wait_ge(s["dve2"], 2 * NB + 2)
                for b in range(NB):
                    pool.indirect_dma_start(srcu[:, b * T:(b + 1) * T], None, a["src"].rearrange("(g e) -> g e", e=T),
                                            bass.IndirectOffsetOnAxis(gidx[:, b:b + 1], 0)).then_inc(s["gather"], 16)
                    pool.indirect_dma_start(dstu[:, b * T:(b + 1) * T], None, a["dst"].rearrange("(g e) -> g e", e=T),
                                            bass.IndirectOffsetOnAxis(gidx[:, b:b + 1], 0)).then_inc(s["gather"], 16)
                pool.wait_ge(s["gather"], 32 * NB)

            @block.sync
            def _(sp):
                st = Dma(sp, s["store"])
                st.n = 32
                sp.wait_ge(s["dve2"], 2 * NB + 3)
                st.start(k.w_d.rearrange("(b p) -> p b", p=BLK), wcol[:], elements=True)
                st.wait()
                st.start(wrow[:], bass.AP(k.w_d.tensor, 0, [[0, 128], [1, UT]]))
                st.wait()

            @block.scalar
            def _(act):
                for t in range(NT):
                    if t:
                        act.wait_ge(s["sides"], t)
                    act.activation(side[:], last_all[:], ACT.Sign, bias=node_half[:, t:t + 1], scale=-1.0,
                                   accum_out=tiles_upto[:, t:t + 1]).then_inc(s["sides"], 1)
                act.wait_ge(s["sides"], NT)

        with nc.Block() as block:
            @block.vector
            def _(dve):
                node = Link(dve, s["node"])
                node(dve.tensor_scalar(tiles_upto[:], tiles_upto[:], 0.5, G / 2, ALU.mult, ALU.add))
                node(dve.tensor_scalar(tiles_upto[:], tiles_upto[:], float(G - 1), None, ALU.min))
                node(dve.tensor_copy(tile_i[:], tiles_upto[:]))
                link = Link(dve, s["dve3"])
                link(dve.tensor_copy(srcf[:], srcu[:]))
                link(dve.tensor_copy(dstf[:], dstu[:]))
                for b in range(NB):
                    c = slice(b * T, (b + 1) * T)
                    link(dve.tensor_scalar(dl[:, c], dstf[:, c], w32[:, b:b + 1], None, ALU.subtract))
                link(dve.tensor_scalar(ge0[:], dl[:], 0.0, None, ALU.is_ge))
                link(dve.scalar_tensor_tensor(out=ge0[:], in0=dl[:], scalar=float(WN), in1=ge0[:],
                                              op0=ALU.is_lt, op1=ALU.mult))
                link(dve.scalar_tensor_tensor(out=keyu[:], in0=dstf[:], scalar=1.0, in1=ge0[:],
                                              op0=ALU.add, op1=ALU.mult))
                link(dve.tensor_scalar(keyu[:], keyu[:], -1.0, None, ALU.add))
                link(dve.tensor_scalar(win_f[:], wcol[:], float(NW - 1), None, ALU.min))
                link(dve.tensor_copy(k.win_idx[:], win_f[:]))
                link(dve.memset(k.same[:, 0:1], 0.0))
                link(dve.tensor_tensor(k.same[:, 1:UT], wrow[:, 1:UT], wrow[:, 0:UT - 1], ALU.is_equal))
                link(dve.tensor_scalar(cmp[0:NW, :], wrow[0:NW, :], k.pcol[0:NW, :], None, ALU.is_le))
                link(dve.tensor_reduce(wcnt[:], cmp[0:NW, :], AX.X, ALU.add))
                link(dve.tensor_scalar(wcnt[:], wcnt[:], -1.0, None, ALU.add))
                link(dve.tensor_scalar(wl32[:], wcnt[:], float(WN), None, ALU.mult))
                link(dve.tensor_scalar(rowf[:], k.node_in_window[0:NW, :], wl32[:], None, ALU.add))
                link(dve.tensor_copy(rowi[:], rowf[:]))
                dve.wait_ge(s["transposed"], 2 * NB + KT)
                link(dve.tensor_copy(k.src_idx[:, 0:5 * BLK], ps[0][0:T, 0:5 * BLK]))
                link(dve.tensor_copy(k.src_idx[:, 5 * BLK:UT], ps[1][0:T, 0:4 * BLK]))
                link(dve.tensor_copy(k.dst_local[:, 0:5 * BLK], ps[2][0:T, 0:5 * BLK]))
                link(dve.tensor_copy(k.dst_local[:, 5 * BLK:UT], ps[3][0:T, 0:4 * BLK]))
                for half in range(2):
                    link(dve.tensor_copy(k.src_tile[:].rearrange("e (p k) -> e k p", k=KT)[:, half * KT // 2:(half + 1) * KT // 2, :],
                                         ps[4 + half][0:T, 0:KT // 2 * BLK].rearrange("e (k p) -> e k p", p=BLK)))
                dve.wait_ge(s["keys"], 16 * (2 * NB + 1))
                dve.tensor_tensor(keyp[:], keyp[:], keyu[:], ALU.is_equal).then_inc(s["lim"], 1)
                dve.wait_ge(s["lim"], 1)
                dve.tensor_scalar(keyp[:], keyp[:], 2 * BIG, -BIG, ALU.mult, ALU.add).then_inc(s["lim"], 1)
                dve.wait_ge(s["upto2"], NT)
                node(dve.tensor_scalar(edges_upto[:], edges_upto[:], 0.5, T / 2, ALU.mult, ALU.add))
                node(dve.tensor_scalar(none[:], edges_upto[:], 0.5, None, ALU.is_lt))
                node(dve.scalar_tensor_tensor(out=place[:], in0=none[:], scalar=float(T), in1=edges_upto[:],
                                              op0=ALU.mult, op1=ALU.add))
                node(dve.tensor_scalar(place[:], place[:], -1.0, None, ALU.add))
                node(dve.tensor_tensor(tiles_upto[:], tiles_upto[:], none[:], ALU.subtract))
                node(dve.tensor_scalar(tiles_upto[:], tiles_upto[:], 0.0, None, ALU.max))
                node(dve.scalar_tensor_tensor(out=idxf[:], in0=place[:], scalar=float(G), in1=tiles_upto[:],
                                              op0=ALU.mult, op1=ALU.add))
                node(dve.tensor_copy(k.edge_idx[:], idxf[:]))
                node(dve.tensor_tensor(tiles_upto[:], tiles_upto[:], node_win[:], ALU.add))
                node(dve.scalar_tensor_tensor(out=idxf[:], in0=place[:], scalar=float(UT), in1=tiles_upto[:],
                                              op0=ALU.mult, op1=ALU.add))
                node(dve.tensor_copy(k.max_idx[:], idxf[:]))

            @block.gpsimd
            def _(pool):
                pool.wait_ge(s["node"], 3)
                for t in range(NT):
                    pool.indirect_dma_start(dst_of[:, t, :], None, a["dst"].rearrange("(g e) -> g e", e=T),
                                            bass.IndirectOffsetOnAxis(tile_i[:, t:t + 1], 0)).then_inc(s["gather2"], 16)
                pool.wait_ge(s["gather2"], 16 * NT)

            @block.scalar
            def _(act):
                act.wait_ge(s["gather2"], 16 * NT)
                for t in range(NT):
                    if t:
                        act.wait_ge(s["upto2"], t)
                    act.activation(side2[:], dst_of[:, t, :], ACT.Sign, bias=node_half[:, t:t + 1], scale=-1.0,
                                   accum_out=edges_upto[:, t:t + 1]).then_inc(s["upto2"], 1)

            @block.tensor
            def _(pe):
                pe.wait_ge(s["dve3"], NB + 2)
                for b in range(NB):
                    c = slice((b % 5) * BLK, (b % 5 + 1) * BLK)
                    pe.transpose(ps[b // 5][0:T, c], srcf[:, b * T:(b + 1) * T],
                                 k.ident[0:BLK, 0:BLK]).then_inc(s["transposed"], 1)
                    pe.transpose(ps[2 + b // 5][0:T, c], dl[:, b * T:(b + 1) * T],
                                 k.ident[0:BLK, 0:BLK]).then_inc(s["transposed"], 1)
                for c in range(KT):
                    h = KT // 2
                    pe.transpose(ps[4 + c // h][0:T, (c % h) * BLK:(c % h + 1) * BLK], sgf[:, c, :],
                                 k.ident[0:BLK, 0:BLK]).then_inc(s["transposed"], 1)

            @block.sync
            def _(sp):
                st = Dma(sp, s["store"])
                st.n = 64
                sp.wait_ge(s["dve3"], NB + 6)
                slots = lambda row, b, off: row[off + b * BLK * T:off + (b + 1) * BLK * T].rearrange("(p e) -> p e", e=T)
                ks = Dma(sp, s["keys"])
                ks.start(k.keys_d[0:1].unsqueeze(0), no_key[:])
                for b in range(NB):
                    ks.start(slots(k.keys_d, b, 1), keyu[:, b * T:(b + 1) * T])
                ks.wait()
                for b in range(NB):
                    ks.start(keyp[:, b * T:(b + 1) * T], slots(k.keys_d, b, 0))
                sp.wait_ge(s["dve3"], NB + 16)
                st.start(k.row_d.rearrange("(w n) -> w n", n=WN), rowi[:])
                st.wait()
                st.start(k.row_idx[:], k.row_d[0:N].rearrange("(p t) -> p t", t=NT))
                ks.wait()
                sp.wait_ge(s["lim"], 2)
                for b in range(NB):
                    st.start(slots(k.lim_d, b, 0), keyp[:, b * T:(b + 1) * T])
                st.start(k.lim_d[SLOTS:SLOTS + 1].unsqueeze(0), no_more[:])
                st.wait()


def prepare_layer(nc, k, ctx, lay):
    H = lay.H
    C = H * D // 128
    FR = 128 // H
    lay.C, lay.FR = C, FR
    lay.w_abs = sbuf(nc, ctx, lay.nm + "w_abs", [128, C * 128])
    lay.w_lin = sbuf(nc, ctx, lay.nm + "w_lin", [128, H])
    lay.sign = sbuf(nc, ctx, lay.nm + "sign", [128, C])
    lay.sign_sum = sbuf(nc, ctx, lay.nm + "sign_sum", [128, 128 // Q])
    lay.self_logit = sbuf(nc, ctx, lay.nm + "self_logit", [T, NT, H])
    lay.XR = XW + H
    lay.table = nc.dram_tensor(lay.nm + "table_d", [N, lay.XR], F32, kind="Internal").ap()
    lay.xpad_d = nc.dram_tensor(lay.nm + "xpad_d", [PAD, D], F32, kind="Internal").ap()
    with ExitStack() as tmp:
        rows = sbuf(nc, tmp, lay.nm + "rows", [T, NT, lay.XR])
        zero = sbuf(nc, tmp, lay.nm + "zero", [PAD - N, D])
        win = [sbuf(nc, tmp, f"{lay.nm}win{i}", [BLK, WN * D]) for i in range(3)]
        w_raw = sbuf(nc, tmp, lay.nm + "w_raw", [128, H * D])
        att_row = sbuf(nc, tmp, lay.nm + "att_row", [128, H * D])
        att_abs = sbuf(nc, tmp, lay.nm + "att_abs", [128, H * D])
        w_att = sbuf(nc, tmp, lay.nm + "w_att", [128, H * D])
        sign_row = sbuf(nc, tmp, lay.nm + "sign_row", [128, H * D])
        att_col = sbuf(nc, tmp, lay.nm + "att_col", [128, C])
        head0_i = sbuf(nc, tmp, lay.nm + "head0_i", [128, H], I32)
        head0 = sbuf(nc, tmp, lay.nm + "head0", [128, H])
        in_head = sbuf(nc, tmp, lay.nm + "in_head", [128, H])
        xx = sbuf(nc, tmp, lay.nm + "xx", [T, NT, 2 * D])
        xxT = sbuf(nc, tmp, lay.nm + "xxT", [128, NT * T])
        rel = sbuf(nc, tmp, lay.nm + "rel", [T, 2, H * D])
        ps_t = [psum(nc, tmp, f"{lay.nm}ps_t{i}") for i in range(2)]
        ps_z = [psum(nc, tmp, f"{lay.nm}ps_z{i}") for i in range(2)]
        ps_l = psum(nc, tmp, lay.nm + "ps_l")
        s = {n: semaphore(nc, k, "p_" + n) for n in (
            "load", "dve", "iota", "xT", "xT_copied", "z", "relu", "used", "lin", "zero", "xpad", "table", "rows")}
        win_in = [semaphore(nc, k, f"{lay.nm}win_in{i}") for i in range(3)]
        win_out = [semaphore(nc, k, f"p_win_out{i}") for i in range(3)]
        with nc.Block() as block:
            @block.sync
            def _(sp):
                ld = Dma(sp, s["load"])
                ld.start(w_raw[0:D, :], lay.Wl)
                ld.start(w_raw[D:128, :], lay.Wr)
                ld.start(att_row[:], bass.AP(lay.att.tensor, 0, [[0, 128], [1, H * D]]))
                for h in range(H):
                    ld.start(att_col[h * FR:(h + 1) * FR, :], lay.att[h, :].rearrange("(c r) -> r c", r=FR), elements=True)
                sp.wait_ge(s["zero"], 1)
                sp.dma_start(lay.xpad_d[0:N, :].rearrange("(p t) d -> p t d", t=NT),
                             lay.x_node[:]).then_inc(s["xpad"], 16)
                sp.dma_start(lay.xpad_d[N:PAD, :], zero[:]).then_inc(s["xpad"], 16)
                ld.wait()
                sp.wait_ge(s["xpad"], 32)

            @block.gpsimd
            def _(pool):
                pool.memset(zero[:], 0.0).then_inc(s["zero"], 1)
                pool.iota(head0_i[:], [[-FR, H]], base=0, channel_multiplier=1).then_inc(s["iota"], 1)

            @block.vector
            def _(dve):
                link = Link(dve, s["dve"])
                link(dve.tensor_copy(xx[:, :, 0:D], lay.x_node[:, :, :]))
                link(dve.tensor_copy(xx[:, :, D:2 * D], lay.x_node[:, :, :]))
                dve.wait_ge(s["load"], 16 * (3 + H))
                link(dve.tensor_scalar(att_abs[:], att_row[:], -1.0, None, ALU.mult))
                link(dve.tensor_tensor(att_abs[:], att_abs[:], att_row[:], ALU.max))
                for c in range(C):
                    f = slice(c * FR, (c + 1) * FR)
                    link(dve.tensor_tensor(lay.w_abs[:, c * 128:(c + 1) * 128].rearrange("p (h r) -> p h r", h=H),
                                           w_raw[:].rearrange("p (h d) -> p h d", h=H)[:, :, f],
                                           att_abs[:].rearrange("p (h d) -> p h d", h=H)[:, :, f], ALU.mult))
                link(dve.tensor_tensor(w_att[:], w_raw[:], att_row[:], ALU.mult))
                link(dve.tensor_reduce(lay.w_lin[:], w_att[:].rearrange("p (h d) -> p h d", h=H), AX.X, ALU.add))
                link(dve.tensor_scalar(lay.w_lin[:], lay.w_lin[:], SLOPE, None, ALU.mult))
                for c in range(C):
                    f = slice(c * FR, (c + 1) * FR)
                    link(dve.tensor_scalar(sign_row[:, c * 128:(c + 1) * 128].rearrange("p (h r) -> p h r", h=H),
                                           att_row[:].rearrange("p (h d) -> p h d", h=H)[:, :, f], 0.0, 2.0,
                                           ALU.is_ge, ALU.mult))
                link(dve.tensor_scalar(sign_row[:], sign_row[:], -1.0, None, ALU.add))
                link(dve.tensor_scalar(att_col[:], att_col[:], 0.0, 2.0, ALU.is_ge, ALU.mult))
                link(dve.tensor_scalar(lay.sign[:], att_col[:], -1.0, None, ALU.add))
                dve.wait_ge(s["iota"], 1)
                link(dve.tensor_copy(head0[:], head0_i[:]))
                link(dve.tensor_scalar(in_head[:], head0[:], 0.0, None, ALU.is_ge))
                link(dve.scalar_tensor_tensor(out=in_head[:], in0=head0[:], scalar=float(FR), in1=in_head[:],
                                              op0=ALU.is_lt, op1=ALU.mult))
                link(dve.memset(lay.sign_sum[:], 0.0))
                link(dve.tensor_scalar(lay.sign_sum[:, 0:H], in_head[:], lay.sign[:, 0:1], None, ALU.mult))
                link(dve.tensor_scalar(lay.sign[:, 1:C], lay.sign[:, 1:C], lay.sign[:, 0:1], None, ALU.mult))

        with nc.Block() as block:
            @block.gpsimd
            def _(pool):
                for b in range(NB):
                    if b >= 3:
                        pool.wait_ge(win_out[b % 3], 16 * (b // 3))
                    pool.indirect_dma_start(win[b % 3][:], None, lay.xpad_d.rearrange("(w n) d -> w (n d)", n=WN),
                                            bass.IndirectOffsetOnAxis(k.win_idx[:, b:b + 1], 0)).then_inc(win_in[b % 3], 16)

            @block.sync
            def _(sp):
                for b in range(NB):
                    sp.wait_ge(win_in[b % 3], 16 * (b // 3 + 1))
                    sp.dma_start(k.xw_d[b * BLK:(b + 1) * BLK, :], win[b % 3][:]).then_inc(win_out[b % 3], 16)
                sp.wait_ge(s["rows"], 3)
                sp.dma_start(lay.table.rearrange("(p t) f -> p t f", t=NT), rows[:]).then_inc(s["table"], 16)
                for i in range(3):
                    sp.wait_ge(win_out[i], 16 * len(range(i, NB, 3)))
                sp.wait_ge(s["table"], 16)

            @block.tensor
            def _(pe):
                def turn(t):
                    if t >= 2:
                        pe.wait_ge(s["xT_copied"], t - 1)
                    pe.transpose(ps_t[t % 2][:, 0:T], xx[:, t, :], k.ident[0:T, 0:T]).then_inc(s["xT"], 1)

                turn(0)
                for t in range(NT):
                    if t + 1 < NT:
                        turn(t + 1)
                    pe.wait_ge(s["xT_copied"], t + 1)
                    if t >= 2:
                        pe.wait_ge(s["relu"], t - 1)
                    pe.matmul(ps_z[t % 2][0:T, 0:H * D], xxT[:, t * T:(t + 1) * T], lay.w_abs[:],
                              start=True, stop=True).then_inc(s["z"], 1)
                    pe.matmul(ps_l[0:T, t * H:(t + 1) * H], xxT[0:D, t * T:(t + 1) * T], lay.w_lin[0:D, :],
                              start=True, stop=True).then_inc(s["lin"], 1)

            @block.scalar
            def _(act):
                for t in range(NT):
                    act.wait_ge(s["z"], t + 1)
                    if t >= 2:
                        act.wait_ge(s["used"], 2 * t - 2)
                    act.activation(rel[:, t % 2, :], ps_z[t % 2][0:T, 0:H * D], ACT.Relu,
                                   scale=1.0 - SLOPE).then_inc(s["relu"], 1)

            @block.vector
            def _(dve):
                used = 0

                def reduce(t):
                    dve.wait_ge(s["relu"], t + 1)
                    dve.tensor_tensor(rel[:, t % 2, :], rel[:, t % 2, :], sign_row[0:T, :],
                                      ALU.mult).then_inc(s["used"], 1)
                    dve.wait_ge(s["used"], 2 * t + 1)
                    dve.tensor_reduce(lay.self_logit[:, t, :],
                                      rel[:, t % 2, :].rearrange("p (c h r) -> p h c r", c=C, h=H),
                                      AX.XY, ALU.add).then_inc(s["used"], 1)

                for t in range(NT):
                    dve.wait_ge(s["xT"], t + 1)
                    dve.tensor_copy(xxT[:, t * T:(t + 1) * T], ps_t[t % 2][:, 0:T]).then_inc(s["xT_copied"], 1)
                    if t >= 2:
                        reduce(t - 2)
                reduce(NT - 2)
                reduce(NT - 1)
                dve.wait_ge(s["lin"], NT)
                dve.wait_ge(s["used"], 2 * NT)
                dve.tensor_tensor(lay.self_logit[:].rearrange("p t h -> p (t h)"),
                                  lay.self_logit[:].rearrange("p t h -> p (t h)"),
                                  ps_l[0:T, 0:NT * H], ALU.add).then_inc(s["used"], 1)
                dve.tensor_copy(rows[:, :, 0:D], lay.x_node[:]).then_inc(s["rows"], 1)
                dve.memset(rows[:, :, D:XW], 1.0).then_inc(s["rows"], 1)
                dve.tensor_copy(rows[:, :, XW:lay.XR],
                                ps_l[0:T, 0:NT * H].rearrange("p (t h) -> p t h", h=H)).then_inc(s["rows"], 1)


def edge_logits(nc, k, lay):
    H, C = lay.H, lay.C
    NE = 6
    with ExitStack() as ctx:
        ph, nm = "a_", lay.nm + "a_"
        idx = [sbuf(nc, ctx, f"{nm}idx{r}", [T, Q], I32) for r in range(R)]
        xs = [sbuf(nc, ctx, f"{nm}xs{r}", [T, Q, lay.XR]) for r in range(R)]
        xw = [sbuf(nc, ctx, f"{nm}xw{r}", [128, D]) for r in range(R)]
        oh = [sbuf(nc, ctx, f"{nm}oh{r}", [T, Q, WN]) for r in range(R)]
        ohT = [sbuf(nc, ctx, f"{nm}ohT{r}", [128, Q, T]) for r in range(R)]
        xT = [sbuf(nc, ctx, f"{nm}xT{r}", [128, QT]) for r in range(R)]
        rl = [sbuf(nc, ctx, f"{nm}rl{r}", [128, QT]) for r in range(NE)]
        f = [sbuf(nc, ctx, f"{nm}f{r}", [128, QT]) for r in range(R)]
        lg = [sbuf(nc, ctx, f"{nm}lg{r}", [128, T]) for r in range(R)]
        ps_oh = psum(nc, ctx, nm + "ps_oh")
        ps_x = [psum(nc, ctx, f"{nm}ps_x{r}") for r in range(R)]
        ps_z = [psum(nc, ctx, f"{nm}ps_z{r}") for r in range(R)]
        ps_l = psum(nc, ctx, nm + "ps_l")
        s = {n: semaphore(nc, k, ph + n) for n in (
            "zeros", "idx_staged", "pool_step", "act_step", "src_read", "lin_read", "oh_ready", "oh_turned", "ohT_ready", "x_ready",
            "xT_ready", "z_ready", "relu_done", "combined", "logit_ready", "logit_copied")}
        gath = [semaphore(nc, k, f"{nm}gath{r}") for r in range(R)]
        spill = [semaphore(nc, k, f"{ph}spill{r}") for r in range(R)]
        lgst = [semaphore(nc, k, f"{ph}lgst{r}") for r in range(R)]
        xwld = [semaphore(nc, k, f"{ph}xwld{r}") for r in range(R)]
        GB = 16 * Q
        LR = 128 // Q

        with nc.Block() as block:
            @block.gpsimd
            def _(pool):
                def body(i, first, last):
                    for r in range(R):
                        u = i * R + r
                        if not first:
                            pool.wait_ge(s["src_read"], u - R + 1)
                            pool.sem_inc(s["pool_step"], 1)
                            pool.wait_ge(s["lin_read"], u - R + 1)
                            pool.sem_inc(s["pool_step"], 1)
                            pool.wait_ge(spill[r], 16 * i)
                            pool.sem_inc(s["pool_step"], 1)
                        pool.wait_ge(s["idx_staged"], u + 1)
                        pool.sem_inc(s["pool_step"], 1)
                        for j in range(Q):
                            pool.indirect_dma_start(xs[r][:, j, :], None, lay.table,
                                                    bass.IndirectOffsetOnAxis(idx[r][:, j:j + 1], 0)).then_inc(gath[r], 16)
                loop3(pool, body)

            @block.sync
            def _(sp):
                def load_windows(u, r):
                    sp.dma_start(xw[r][:], k.xw_d[bass.ds(u * Q, Q), :].rearrange("w (n d) -> (w n) d", d=D)).then_inc(xwld[r], 16)

                def store_logits(u, r):
                    sp.wait_ge(s["logit_copied"], u + 1)
                    for j in range(Q):
                        sp.dma_start(lay.logit_d[:, bass.ds(u * QT + j * T, T)],
                                     lg[r][LR * j:LR * j + H, :]).then_inc(lgst[r], 16)

                load_windows(0, 0)
                load_windows(1, 1)

                def body(i, first, last):
                    for r in range(R):
                        u = i * R + r
                        if not (last and r >= R - 2):
                            if not (first and r == 0):
                                sp.wait_ge(s["x_ready"], u)
                            load_windows(u + 2, (r + 2) % R)
                        sp.wait_ge(gath[r], GB * (i + 1))
                        sp.dma_start(lay.xs_d[bass.ds(u, 1), :, :].rearrange("u p f -> (u p) f"),
                                     xs[r][:].rearrange("p j f -> p (j f)")).then_inc(spill[r], 16)
                        if not (first and r < 2):
                            store_logits(u - 2, (r + R - 2) % R)
                    if last:
                        store_logits(U - 2, R - 2)
                        store_logits(U - 1, R - 1)
                loop3(sp, body)
                for r in range(R):
                    sp.wait_ge(spill[r], 16 * (U // R))
                    sp.wait_ge(lgst[r], GB * (U // R))

            @block.tensor
            def _(pe):
                def turn(u, r, uses, free):
                    pe.wait_ge(s["oh_ready"], u + 1)
                    if free:
                        pe.wait_ge(s["xT_ready"], u - R + 1)
                    if free is not None:
                        pe.wait_ge(s["ohT_ready"], u)
                    pe.wait_ge(gath[r], GB * uses)
                    pe.transpose(ps_oh[:, 0:T], oh[r][:].rearrange("p j n -> p (j n)"),
                                 k.ident[0:T, 0:T]).then_inc(s["oh_turned"], 1)
                    for j in range(Q):
                        ins = pe.transpose(ps_x[r][0:D, j * T:(j + 1) * T], xs[r][:, j, 0:D], k.ident[0:T, 0:T])
                    ins.then_inc(s["src_read"], 1)

                def spread(u, r, uses):
                    pe.wait_ge(s["ohT_ready"], u + 1)
                    pe.wait_ge(xwld[r], 16 * uses)
                    pe.matmul(ps_x[r][D:128, 0:QT], xw[r][:], ohT[r][:].rearrange("p j e -> p (j e)"),
                              start=True, stop=True).then_inc(s["x_ready"], 1)

                def project(i, r, first, cs):
                    u = i * R + r
                    for c in cs:
                        b = (C * r + c) % R
                        if c == 0:
                            pe.wait_ge(s["xT_ready"], u + 1)
                        if not (first and C * r + c < R):
                            pe.wait_ge(s["relu_done"], C * u + c - R + 1)
                        pe.matmul(ps_z[b][:, 0:QT], lay.w_abs[:, c * 128:(c + 1) * 128], xT[r][:],
                                  start=True, stop=True).then_inc(s["z_ready"], 1)

                def reduce(u, r, free):
                    if free:
                        pe.wait_ge(s["logit_copied"], u)
                    pe.wait_ge(s["combined"], (C - 1) * (u + 1))
                    for j in range(Q):
                        ins = pe.matmul(ps_l[LR * j:LR * j + LR, 0:T], lay.sign_sum[:], f[r][:, j * T:(j + 1) * T],
                                        start=True, stop=True)
                    ins.then_inc(s["logit_ready"], 1)

                turn(0, 0, 1, None)
                spread(0, 0, 1)

                def body(i, first, last):
                    for r in range(R):
                        u = i * R + r
                        n = (r + 1) % R
                        more = not (last and r == R - 1)
                        if more:
                            turn(u + 1, n, i + 1 + (n == 0), not (first and n != 0))
                        project(i, r, first, range(0, C - 1))
                        if more:
                            spread(u + 1, n, i + 1 + (n == 0))
                        project(i, r, first, range(C - 1, C))
                        if not (first and r == 0):
                            reduce(u - 1, (r + R - 1) % R, not (first and r == 1))
                loop3(pe, body)
                reduce(U - 1, R - 1, True)

            @block.scalar
            def _(act):
                def copy_logit(u, r, i, free):
                    act.wait_ge(s["logit_ready"], u + 1)
                    if free:
                        act.wait_ge(lgst[r], GB * i)
                    act.activation(lg[r][:], ps_l[:, 0:T], ACT.Copy).then_inc(s["logit_copied"], 1)

                def stage(u, r):
                    act.activation(idx[r][:], k.src_idx[:, bass.ds(u * Q, Q)], ACT.Copy).then_inc(s["idx_staged"], 1)

                for r in range(R):
                    stage(r, r)

                def body(i, first, second, last=False):
                    for r in range(R):
                        u = i * R + r
                        act.wait_ge(gath[r], GB * (i + 1))
                        act.sem_inc(s["act_step"], 1)
                        if not last:
                            stage(u + R, r)
                        act.activation(lay.lin_edge[:, bass.ds(u * Q, Q), :], xs[r][:, :, XW:lay.XR],
                                       ACT.Copy).then_inc(s["lin_read"], 1)
                        for c in range(C):
                            m = C * r + c
                            act.wait_ge(s["z_ready"], C * u + c + 1)
                            back = m - NE
                            br, bc = back // C, back % C
                            if not (first and back < 0):
                                act.wait_ge(s["combined"], (C - 1) * (i * R + br) + max(bc, 1))
                            act.activation(rl[m % NE][:], ps_z[m % R][:, 0:QT], ACT.Relu,
                                           scale=1.0 - SLOPE).then_inc(s["relu_done"], 1)
                        if not (first and r == 0):
                            copy_logit(u - 1, (r + R - 1) % R, i - (r == 0), not (first or second and r == 0))
                body(0, True, False)
                body(1, False, True)
                with act.Fori(2, U // R - 1) as i:
                    body(i, False, False)
                body(U // R - 1, False, False, True)
                copy_logit(U - 1, R - 1, U // R - 1, True)

            @block.vector
            def _(dve):
                def one_hot(u, r, free):
                    if free:
                        dve.wait_ge(s["oh_turned"], u - R + 1)
                    dve.tensor_tensor(oh[r][:], k.dst_local[:, bass.ds(u * Q, Q)].unsqueeze(2).to_broadcast([T, Q, WN]),
                                      k.node_in_window[:].unsqueeze(1).to_broadcast([T, Q, WN]),
                                      ALU.is_equal).then_inc(s["oh_ready"], 1)

                def copy_ohT(u, r, free):
                    dve.wait_ge(s["oh_turned"], u + 1)
                    if free:
                        dve.wait_ge(s["x_ready"], u - R + 1)
                    for j in range(Q):
                        p = slice(WN * j, WN * j + WN)
                        ins = dve.tensor_copy(ohT[r][p, j, :], ps_oh[p, 0:T])
                    ins.then_inc(s["ohT_ready"], 1)

                def copy_xT(u, r, free):
                    dve.wait_ge(s["x_ready"], u + 1)
                    if free:
                        dve.wait_ge(s["z_ready"], C * (u - R + 1))
                    dve.tensor_copy(xT[r][:], ps_x[r][:, 0:QT]).then_inc(s["xT_ready"], 1)

                def combine(i, r, first, c):
                    u = i * R + r
                    dve.wait_ge(s["relu_done"], C * u + c + 1)
                    if c == 1 and not first:
                        dve.wait_ge(s["logit_ready"], u - R + 1)
                    if c > 1:
                        dve.wait_ge(s["combined"], (C - 1) * u + c - 1)
                    dve.scalar_tensor_tensor(out=f[r][:], in0=rl[(C * r + c) % NE][:], scalar=lay.sign[:, c:c + 1],
                                             in1=rl[(C * r) % NE][:] if c == 1 else f[r][:],
                                             op0=ALU.mult, op1=ALU.add).then_inc(s["combined"], 1)

                for r in range(R):
                    dve.memset(ohT[r][:], 0.0).then_inc(s["zeros"], 1)
                dve.wait_ge(s["zeros"], R)
                one_hot(0, 0, False)
                one_hot(1, 1, False)
                copy_ohT(0, 0, False)
                copy_xT(0, 0, False)

                def body(i, first, last):
                    for r in range(R):
                        u = i * R + r
                        more = not (last and r == R - 1)
                        free = not (first and r + 1 < R)
                        if more:
                            copy_ohT(u + 1, (r + 1) % R, free)
                        if not (last and r >= R - 2):
                            one_hot(u + 2, (r + 2) % R, not (first and r + 2 < R))
                        combine(i, r, first, 1)
                        if more:
                            copy_xT(u + 1, (r + 1) % R, free)
                        for c in range(2, C):
                            combine(i, r, first, c)
                loop3(dve, body)


def edge_softmax(nc, k, lay):
    H = lay.H
    NC = CH // H
    F = SLOTS // NC
    TPC = F // T
    lay.stat_d = nc.dram_tensor(lay.nm + "stat_d", [NC, H, 4], F32, kind="Internal").ap()
    lay.carry_d = nc.dram_tensor(lay.nm + "carry_d", [NC, H, 2], F32, kind="Internal").ap()
    with ExitStack() as tmp:
        ph, nm = "s_", lay.nm + "s_"
        lim = sbuf(nc, tmp, nm + "lim", [CH, F + 1])
        lg = sbuf(nc, tmp, nm + "lg", [CH, F])
        fw = sbuf(nc, tmp, nm + "fw", [CH, F])
        bw = sbuf(nc, tmp, nm + "bw", [CH, F])
        stat = sbuf(nc, tmp, nm + "stat", [CH, 4])
        stat_h = sbuf(nc, tmp, nm + "stat_h", [H, NC, 4])
        run = sbuf(nc, tmp, nm + "run", [H, 2, NC])
        carry_h = sbuf(nc, tmp, nm + "carry_h", [H, NC, 2])
        carry = sbuf(nc, tmp, nm + "carry", [CH, 2])
        ps = [psum(nc, tmp, f"{nm}ps{i}") for i in range(4)]
        s = {n: semaphore(nc, k, ph + n) for n in (
            "load", "load_lg", "bounce", "dve", "exp", "lin_laid", "lin_turned", "lin_added", "less", "turned", "max_copied", "exp_copied")}
        lin = lay.m_edge[:].rearrange("p s h -> p (s h)").rearrange("p (t v) -> p t v", v=CH)
        GRP = 4
        LG = -(-TPC // GRP)
        NX = 4

        def place(edge, g):
            return edge[:].rearrange("p (c t) h -> p t c h", c=NC)[:, g * GRP:min((g + 1) * GRP, TPC), :, :]

        def bank(n, g):
            return ps[n % 4][0:T, 0:min(GRP, TPC - g * GRP) * CH].rearrange("p (q c h) -> p q c h", c=NC, h=H)

        with nc.Block() as block:
            @block.sync
            def _(sp):
                ld = Dma(sp, s["load"])
                for c in range(NC):
                    ld.start(lim[c * H:(c + 1) * H, :], bass.AP(k.lim_d.tensor, c * F, [[0, H], [1, F + 1]]))
                ld = Dma(sp, s["load_lg"])
                for c in range(NC):
                    ld.start(lg[c * H:(c + 1) * H, :], lay.logit_d[:, c * F:(c + 1) * F])
                bo = Dma(sp, s["bounce"])
                sp.wait_ge(s["dve"], 7)
                bo.start(lay.stat_d.rearrange("c h v -> (c h) v"), stat[:])
                bo.wait()
                bo.start(stat_h[:], lay.stat_d.rearrange("c h v -> h c v"))
                bo.wait()
                sp.wait_ge(s["dve"], 13)
                bo.start(lay.carry_d.rearrange("c h v -> h c v"), carry_h[:])
                bo.wait()
                bo.start(carry[:], lay.carry_d.rearrange("c h v -> (c h) v"))
                bo.wait()

            @block.vector
            def _(dve):
                link = Link(dve, s["dve"])
                dve.wait_ge(s["load"], 16 * NC)
                link(dve.tensor_reduce(stat[:, 3:4], lim[:, 1:F], AX.X, ALU.min))
                link(dve.tensor_tensor(stat[:, 1:2], stat[:, 3:4], lim[:, 0:1], ALU.min))
                link(dve.tensor_tensor(stat[:, 3:4], stat[:, 3:4], lim[:, F:F + 1], ALU.min))
                dve.wait_ge(s["load_lg"], 16 * NC)
                for g in range(LG):
                    c = slice(g * GRP * T, min((g + 1) * GRP, TPC) * T)
                    dve.wait_ge(s["lin_turned"], g + 1)
                    dve.tensor_tensor(lg[:, c], lg[:, c], ps[g % 4][0:CH, 0:c.stop - c.start],
                                      ALU.add).then_inc(s["lin_added"], 1)
                dve.wait_ge(s["lin_added"], LG)
                link(dve.tensor_tensor_scan(fw[:], lim[:, 0:F], lg[:], -BIG, ALU.min, ALU.max))
                link(dve.tensor_tensor_scan(bw[:, ::-1], lim[:, 1:F + 1][:, ::-1], lg[:, ::-1], -BIG,
                                            ALU.min, ALU.max))
                link(dve.tensor_copy(stat[:, 0:1], fw[:, F - 1:F]))
                link(dve.tensor_copy(stat[:, 2:3], bw[:, 0:1]))
                dve.wait_ge(s["bounce"], 32)
                link(dve.tensor_tensor_scan(run[:, 0, :], stat_h[:, :, 1], stat_h[:, :, 0], -BIG, ALU.min, ALU.max))
                link(dve.tensor_tensor_scan(run[:, 1, ::-1], stat_h[:, ::-1, 3], stat_h[:, ::-1, 2], -BIG,
                                            ALU.min, ALU.max))
                link(dve.memset(carry_h[:, 0, 0:1], -BIG))
                link(dve.memset(carry_h[:, NC - 1, 1:2], -BIG))
                link(dve.tensor_copy(carry_h[:, 1:NC, 0], run[:, 0, 0:NC - 1]))
                link(dve.tensor_copy(carry_h[:, 0:NC - 1, 1], run[:, 1, 1:NC]))
                dve.wait_ge(s["bounce"], 64)
                link(dve.tensor_tensor_scan(fw[:], lim[:, 0:F], lg[:], carry[:, 0:1], ALU.min, ALU.max))
                link(dve.tensor_tensor_scan(bw[:, ::-1], lim[:, 1:F + 1][:, ::-1], lg[:, ::-1],
                                            carry[:, 1:2], ALU.min, ALU.max))
                link(dve.tensor_tensor(fw[:], fw[:], bw[:], ALU.max))
                for x in range(NX):
                    c = slice(x * F // NX, (x + 1) * F // NX)
                    dve.tensor_tensor(lg[:, c], lg[:, c], fw[:, c], ALU.subtract).then_inc(s["less"], 1)
                for g in range(LG):
                    dve.wait_ge(s["turned"], 2 * g + 2)
                    dve.tensor_copy(place(lay.a_edge, g), bank(2 * g + 1, g)).then_inc(s["exp_copied"], 1)

            @block.scalar
            def _(act):
                act.activation(lin.rearrange("p t (c h) -> p t c h", h=H),
                               lay.lin_edge[:].rearrange("p (c t) h -> p t c h", c=NC), ACT.Copy).then_inc(s["lin_laid"], 1)
                for x in range(NX):
                    c = slice(x * F // NX, (x + 1) * F // NX)
                    act.wait_ge(s["less"], x + 1)
                    act.activation(lg[:, c], lg[:, c], ACT.Exp).then_inc(s["exp"], 1)
                act.wait_ge(s["lin_turned"], LG)
                for g in range(LG):
                    act.wait_ge(s["turned"], 2 * g + 1)
                    act.activation(place(lay.m_edge, g), bank(2 * g, g), ACT.Copy).then_inc(s["max_copied"], 1)

            @block.tensor
            def _(pe):
                pe.wait_ge(s["lin_laid"], 1)
                for g in range(LG):
                    if g >= 4:
                        pe.wait_ge(s["lin_added"], g - 3)
                    for q in range(min(GRP, TPC - g * GRP)):
                        ins = pe.transpose(ps[g % 4][0:CH, q * T:(q + 1) * T], lin[:, g * GRP + q, :],
                                           k.ident[0:T, 0:T])
                    ins.then_inc(s["lin_turned"], 1)
                pe.wait_ge(s["lin_added"], LG)
                pe.wait_ge(s["dve"], 16)
                for n in range(2 * LG):
                    g = n // 2
                    if n % 2:
                        pe.wait_ge(s["exp"], min(NX, -(-(g + 1) * GRP * T * NX // F)))
                    if n >= 4:
                        pe.wait_ge(s["exp_copied"] if n % 2 else s["max_copied"], g - 1)
                    for q in range(min(GRP, TPC - g * GRP)):
                        t = g * GRP + q
                        ins = pe.transpose(ps[n % 4][0:T, q * CH:(q + 1) * CH], (lg if n % 2 else fw)[:, t * T:(t + 1) * T],
                                           k.ident[0:CH, 0:CH])
                    ins.then_inc(s["turned"], 1)


def edge_sums(nc, k, lay):
    H = lay.H
    P = WN * H
    HV = P // 128
    VJ = 1
    OJ = Q // 2
    with ExitStack() as ctx:
        ph, nm = "b_", lay.nm + "b_"
        xs = [sbuf(nc, ctx, f"{nm}xs{r}", [T, Q, lay.XR]) for r in range(R)]
        oh = [sbuf(nc, ctx, f"{nm}oh{r}", [T, Q, WN]) for r in range(R)]
        p = [sbuf(nc, ctx, f"{nm}p{r}", [T, Q, P]) for r in range(R)]
        same = [sbuf(nc, ctx, f"{nm}same{r}", [128, Q]) for r in range(R)]
        dst = [sbuf(nc, ctx, f"{nm}dst{r}", [T, Q]) for r in range(R)]
        ae = [sbuf(nc, ctx, f"{nm}ae{r}", [T, Q, H]) for r in range(R)]
        acc = [sbuf(nc, ctx, f"{nm}acc{r}", [XW, Q, P]) for r in range(R)]
        rows = [sbuf(nc, ctx, f"{nm}rows{r}", [128, Q, HV * XW]) for r in range(R)]
        ps_v = [psum(nc, ctx, f"{nm}ps_v{j}") for j in range(Q)]
        ps_r = [psum(nc, ctx, f"{nm}ps_r{j}") for j in range(Q)]
        s = {n: semaphore(nc, k, ph + n) for n in (
            "zero", "oh_ready", "p_ready", "p_last", "staged", "v_ready", "chain", "turned", "copied", "pool_step", "pe_step")}
        s["max_stored"] = semaphore(nc, k, nm + "max_stored")
        s["max_gathered"] = semaphore(nc, k, nm + "max_gathered")
        load = [semaphore(nc, k, f"{ph}load{r}") for r in range(R)]
        store = [semaphore(nc, k, f"{ph}store{r}") for r in range(R)]

        def weights(eng, r, j):
            return eng.tensor_tensor(p[r][:, j, :].rearrange("p (n h) -> p n h", h=H),
                                     oh[r][:, j, :].unsqueeze(2).to_broadcast([T, WN, H]),
                                     ae[r][:, j, :].unsqueeze(1).to_broadcast([T, WN, H]), ALU.mult)

        with nc.Block() as block:
            @block.sync
            def _(sp):
                def body(i, first, last):
                    for r in range(R):
                        u = i * R + r
                        if not first:
                            sp.wait_ge(s["v_ready"], Q * (u - R + 1))
                        sp.dma_start(xs[r][:].rearrange("p j f -> p (j f)"),
                                     lay.xs_d[bass.ds(u, 1), :, :].rearrange("u p f -> (u p) f")).then_inc(load[r], 16)
                loop3(sp, body)

            @block.gpsimd
            def _(pool):
                pool.dma_start(lay.max_d.rearrange("(e u) h -> e (u h)", u=UT),
                               lay.m_edge[:].rearrange("e u h -> e (u h)")).then_inc(s["max_stored"], 16)

                def body(i, first, gathers):
                    for r in range(R):
                        u = i * R + r
                        if not first:
                            pool.wait_ge(s["v_ready"], Q * (u - R + 1))
                            pool.sem_inc(s["pool_step"], 1)
                        pool.wait_ge(s["oh_ready"], u + 1)
                        pool.sem_inc(s["pool_step"], 1)
                        for j in range(VJ, Q):
                            weights(pool, r, j).then_inc(s["p_last"], 1)
                        for t in gathers[r:r + 1]:
                            pool.indirect_dma_start(lay.node_max[:, t, :], None, lay.max_d,
                                                    bass.IndirectOffsetOnAxis(k.max_idx[:, t:t + 1], 0)).then_inc(s["max_gathered"], 16)

                body(0, True, [])
                pool.wait_ge(s["max_stored"], 16)
                rounds = -(-NT // R)
                for i in range(1, rounds + 1):
                    body(i, False, list(range(NT))[(i - 1) * R:i * R])
                with pool.Fori(rounds + 1, U // R) as i:
                    body(i, False, [])
                pool.wait_ge(s["max_gathered"], 16 * NT)

            @block.vector
            def _(dve):
                dve.memset(acc[R - 1][:, Q - 1, :], 0.0).then_inc(s["zero"], 1)

                def one_hot(u, r):
                    dve.wait_ge(s["staged"], 3 * u + 3)
                    dve.tensor_tensor(oh[r][:], dst[r][:].unsqueeze(2).to_broadcast([T, Q, WN]),
                                      k.node_in_window[:].unsqueeze(1).to_broadcast([T, Q, WN]),
                                      ALU.is_equal).then_inc(s["oh_ready"], 1)

                def weigh(u, r, j):
                    if j == 0:
                        dve.wait_ge(s["oh_ready"], u + 1)
                    weights(dve, r, j).then_inc(s["p_ready"], 1)

                def run(u, r, j, start):
                    if start:
                        dve.wait_ge(s["zero"], 1)
                    else:
                        dve.wait_ge(s["chain"], Q * u + j)
                    prev = acc[r][:, j - 1, :] if j else acc[(r + R - 1) % R][:, Q - 1, :]
                    dve.scalar_tensor_tensor(out=acc[r][:, j, :], in0=prev, scalar=same[r][0:XW, j:j + 1],
                                             in1=ps_v[j][0:XW, 0:P], op0=ALU.mult,
                                             op1=ALU.add).then_inc(s["chain"], 1)

                one_hot(0, 0)
                for j in range(VJ):
                    weigh(0, 0, j)
                one_hot(1, 1)
                dve.wait_ge(s["v_ready"], 1)

                def body(i, first, last):
                    for r in range(R):
                        u = i * R + r
                        if not first:
                            dve.wait_ge(s["turned"], Q * (u - R + 1))
                        for j in range(Q):
                            run(u, r, j, first and r == 0 and j == 0)
                            if not (last and r == R - 1 and j == Q - 1):
                                dve.wait_ge(s["v_ready"], Q * u + j + 2)
                            if j < VJ:
                                if not (last and r == R - 1):
                                    weigh(u + 1, (r + 1) % R, j)
                            if j == OJ and not (last and r >= R - 2):
                                one_hot(u + 2, (r + 2) % R)
                loop3(dve, body)

            @block.tensor
            def _(pe):
                def turn(u, r, j, free):
                    pe.wait_ge(s["chain"], Q * u + j + 1)
                    if free:
                        pe.wait_ge(s["copied"], Q * (u - 1) + j + 1)
                    pe.sem_inc(s["pe_step"], 1)
                    for v in range(HV):
                        ins = pe.transpose(ps_r[j][:, v * XW:(v + 1) * XW], acc[r][:, j, v * 128:(v + 1) * 128],
                                           k.ident[0:XW, 0:XW])
                    ins.then_inc(s["turned"], 1)

                def body(i, first, last):
                    for r in range(R):
                        u = i * R + r
                        pe.wait_ge(load[r], 16 * (i + 1))
                        for j in range(Q):
                            if j < VJ:
                                pe.wait_ge(s["p_ready"], VJ * u + j + 1)
                            else:
                                pe.wait_ge(s["p_last"], (Q - VJ) * u + j - VJ + 1)
                            if not (first and r == 0):
                                pe.wait_ge(s["chain"], Q * (u - 1) + j + 1)
                            pe.matmul(ps_v[j][0:XW, 0:P], xs[r][:, j, 0:XW], p[r][:, j, :],
                                      start=True, stop=True).then_inc(s["v_ready"], 1)
                            if not (first and r == 0):
                                turn(u - 1, (r + R - 1) % R, j, not (first and r == 1))
                loop3(pe, body)
                for j in range(Q):
                    turn(U - 1, R - 1, j, True)

            @block.scalar
            def _(act):
                def stage(u, r):
                    act.activation(same[r][:], k.same[:, bass.ds(u * Q, Q)], ACT.Copy).then_inc(s["staged"], 1)
                    act.activation(dst[r][:], k.dst_local[:, bass.ds(u * Q, Q)], ACT.Copy).then_inc(s["staged"], 1)
                    act.activation(ae[r][:], lay.a_edge[:, bass.ds(u * Q, Q), :], ACT.Copy).then_inc(s["staged"], 1)

                for r in range(R):
                    stage(r, r)

                def body(i, first, last):
                    for r in range(R):
                        u = i * R + r
                        if not first:
                            act.wait_ge(store[r], 16 * i)
                        for j in range(Q):
                            act.wait_ge(s["turned"], Q * u + j + 1)
                            act.activation(rows[r][:, j, :], ps_r[j][:, 0:HV * XW], ACT.Copy).then_inc(s["copied"], 1)
                        if not last:
                            stage(u + R, r)
                        act.wait_ge(s["copied"], Q * u + Q)
                        act.dma_start(bass.AP(lay.v_d.tensor, u * (Q * WN * H * XW),
                                              [[XW, 128], [WN * H * XW, Q], [128 * XW, HV], [1, XW]]),
                                      rows[r][:].rearrange("p j (v f) -> p j v f", v=HV)).then_inc(store[r], 16)
                loop3(act, body)
                for r in range(R):
                    act.wait_ge(store[r], 16 * (U // R))


def merge_nodes(nc, k, lay, finish):
    H = lay.H
    CK = H // 2
    TG = 5
    with ExitStack() as tmp:
        ph, nm = "n_", lay.nm + "n_"
        v = sbuf(nc, tmp, nm + "v", [T, NT, H * XW])
        m = lay.node_max
        den = sbuf(nc, tmp, nm + "den", [T, NT, H])
        me = sbuf(nc, tmp, nm + "me", [T, NT, H])
        be = sbuf(nc, tmp, nm + "be", [T, NT, H])
        ga = sbuf(nc, tmp, nm + "ga", [T, NT, H])
        agg = sbuf(nc, tmp, nm + "agg", [T, NT, H, D])
        selfx = [sbuf(nc, tmp, f"{nm}selfx{i}", [T, TG, H, D]) for i in range(2)]
        aggT = [sbuf(nc, tmp, f"{nm}aggT{i}", [128, CK * T]) for i in range(2)]
        wl = sbuf(nc, tmp, nm + "wl", [128, CK, D])
        bias = sbuf(nc, tmp, nm + "bias", [T, D])
        o = sbuf(nc, tmp, nm + "o", [T, NT, D])
        ps_t = [psum(nc, tmp, f"{nm}ps_t{i}") for i in range(2)]
        ps_o = [psum(nc, tmp, f"{nm}ps_o{i}") for i in range(2)]
        s = {n: semaphore(nc, k, ph + n) for n in (
            "load", "dve", "exp", "selfx", "agg", "turned", "copied", "proj", "out", "fin", "finb", "store")}
        s["gather"] = semaphore(nc, k, nm + "gather")
        with nc.Block() as block:
            @block.gpsimd
            def _(pool):
                for t in range(NT):
                    pool.indirect_dma_start(v[:, t, :], None, lay.v_d,
                                            bass.IndirectOffsetOnAxis(k.row_idx[:, t:t + 1], 0)).then_inc(s["gather"], 16)
                pool.wait_ge(s["gather"], 16 * NT)
                pool.wait_ge(s["dve"], 10)
                for g in range(NT // TG):
                    t = slice(g * TG, (g + 1) * TG)
                    if g >= 2:
                        pool.wait_ge(s["agg"], g - 1)
                    pool.tensor_tensor(selfx[g % 2][:], lay.x_node[:, t, :].unsqueeze(2).to_broadcast([T, TG, H, D]),
                                       ga[:, t, :].unsqueeze(3).to_broadcast([T, TG, H, D]), ALU.mult).then_inc(s["selfx"], 1)

            @block.sync
            def _(sp):
                ld = Dma(sp, s["load"])
                wsrc = lay.Wl.rearrange("d (c b f) -> b d c f", b=2, f=D)
                for b in range(2):
                    ld.start(wl[b * D:(b + 1) * D, :, :], wsrc[b])
                ld.start(bias[:], bass.AP(lay.bias.tensor, 0, [[0, T], [1, D]]))
                ld.wait()

            @block.vector
            def _(dve):
                link = Link(dve, s["dve"])
                flat = lambda x: x[:].rearrange("p t h -> p (t h)")
                one = v[:].rearrange("p t (h f) -> p (t h) f", f=XW)
                sums = one[:, :, D]
                dve.wait_ge(s["gather"], 16 * NT)
                link(dve.tensor_scalar(flat(me), sums, 0.5, -2 * BIG, ALU.is_lt, ALU.mult))
                link(dve.tensor_tensor(flat(me), flat(me), flat(m), ALU.add))
                link(dve.tensor_tensor(flat(m), flat(me), flat(lay.self_logit), ALU.max))
                link(dve.tensor_tensor(flat(be), flat(me), flat(m), ALU.subtract))
                link(dve.tensor_tensor(flat(ga), flat(lay.self_logit), flat(m), ALU.subtract))
                dve.wait_ge(s["exp"], 2)
                link(dve.tensor_tensor(flat(den), sums, flat(be), ALU.mult))
                link(dve.tensor_tensor(flat(den), flat(den), flat(ga), ALU.add))
                link(dve.reciprocal(flat(den), flat(den)))
                link(dve.tensor_tensor(flat(be), flat(be), flat(den), ALU.mult))
                link(dve.tensor_tensor(flat(ga), flat(ga), flat(den), ALU.mult))

                def leave(g):
                    for t in range(g * TG, (g + 1) * TG):
                        dve.wait_ge(s["proj"], t + 1)
                        dve.scalar_tensor_tensor(out=o[:, t, :], in0=ps_o[t % 2][0:T, 0:D], scalar=1.0 / H, in1=bias[:],
                                                 op0=ALU.mult, op1=ALU.add).then_inc(s["out"], 1)

                dve.wait_ge(s["load"], 48)
                for g in range(NT // TG):
                    th = slice(g * TG * H, (g + 1) * TG * H)
                    ag = agg[:].rearrange("p t h f -> p (t h) f")[:, th, :]
                    link(dve.tensor_tensor(ag, one[:, th, 0:D],
                                           flat(be)[:, th].unsqueeze(2).to_broadcast([T, TG * H, D]), ALU.mult))
                    dve.wait_ge(s["selfx"], g + 1)
                    dve.tensor_tensor(ag, ag, selfx[g % 2][:].rearrange("p t h f -> p (t h) f"), ALU.add).then_inc(s["agg"], 1)
                    if g:
                        leave(g - 1)
                leave(NT // TG - 1)

            @block.scalar
            def _(act):
                act.wait_ge(s["dve"], 4)
                act.activation(be[:], be[:], ACT.Exp).then_inc(s["exp"], 1)
                act.wait_ge(s["dve"], 5)
                act.activation(ga[:], ga[:], ACT.Exp).then_inc(s["exp"], 1)
                for t in range(NT):
                    act.wait_ge(s["turned"], t + 1)
                    if t >= 2:
                        act.wait_ge(s["proj"], t - 1)
                    act.activation(aggT[t % 2][:], ps_t[t % 2][:, 0:CK * T], ACT.Copy).then_inc(s["copied"], 1)

            @block.tensor
            def _(pe):
                pe.wait_ge(s["load"], 48)

                def turn(t):
                    pe.wait_ge(s["agg"], t // TG + 1)
                    if t >= 2:
                        pe.wait_ge(s["copied"], t - 1)
                    for c in range(CK):
                        ins = pe.transpose(ps_t[t % 2][:, c * T:(c + 1) * T],
                                           agg[:, t, 2 * c:2 * c + 2, :].rearrange("p h f -> p (h f)"), k.ident[0:T, 0:T])
                    ins.then_inc(s["turned"], 1)

                turn(0)
                for t in range(NT):
                    if t + 1 < NT:
                        turn(t + 1)
                    pe.wait_ge(s["copied"], t + 1)
                    if t >= 2:
                        pe.wait_ge(s["out"], t - 1)
                    for c in range(CK):
                        ins = pe.matmul(ps_o[t % 2][0:T, 0:D], aggT[t % 2][:, c * T:(c + 1) * T], wl[:, c, :],
                                        start=(c == 0), stop=(c == CK - 1))
                    ins.then_inc(s["proj"], 1)

        with nc.Block() as block:
            @block.vector
            def _(dve):
                finish(dve, Link(dve, s["fin"]), s["finb"], o)

            @block.scalar
            def _(act):
                if lay.norm:
                    act.wait_ge(s["fin"], 6)
                    act.activation(lay.std[:], lay.var[:], ACT.Sqrt).then_inc(s["finb"], 1)

            @block.sync
            def _(sp):
                sp.wait_ge(s["fin"], lay.fin_steps)
                sp.dma_start(lay.next_table.rearrange("(p t) d -> p t d", t=NT), lay.next_node[:]).then_inc(s["store"], 16)
                sp.wait_ge(s["store"], 16)


def layer_norm(dve, link, std_ready, x, y, sq, mean, var, std, out):
    bc = lambda v: v[:].unsqueeze(2).to_broadcast([T, NT, D])
    link(dve.tensor_tensor(out[:], x[:], y[:], ALU.add))
    link(dve.tensor_reduce(mean[:], out[:], AX.X, ALU.add))
    link(dve.tensor_scalar(mean[:], mean[:], 1.0 / D, None, ALU.mult))
    link(dve.tensor_tensor(out[:], out[:], bc(mean), ALU.subtract))
    dve.tensor_tensor(sq[:], out[:], out[:], ALU.mult).then_inc(std_ready, 1)
    dve.wait_ge(std_ready, 1)
    link(dve.tensor_reduce(var[:], sq[:], AX.X, ALU.add))
    link(dve.tensor_scalar(var[:], var[:], 1.0 / D, EPS, ALU.mult, ALU.add))
    dve.wait_ge(std_ready, 2)
    link(dve.reciprocal(std[:], std[:]))
    link(dve.tensor_tensor(out[:], out[:], bc(std), ALU.mult))


def neighbour_sums(nc, k, table):
    GT = GQ * T
    with ExitStack() as ctx:
        nm = "g_"
        idx = [sbuf(nc, ctx, f"{nm}idx{r}", [T, GQ], I32) for r in range(GR)]
        xs = [sbuf(nc, ctx, f"{nm}xs{r}", [T, GQ, D]) for r in range(GR)]
        keep = [sbuf(nc, ctx, f"{nm}keep{r}", [D, GT]) for r in range(GR)]
        run = [sbuf(nc, ctx, f"{nm}run{r}", [D, GT]) for r in range(GR)]
        rows = [sbuf(nc, ctx, f"{nm}rows{r}", [T, GQ, D]) for r in range(GR)]
        start = sbuf(nc, ctx, nm + "start", [D, 1])
        ps_x = [psum(nc, ctx, f"{nm}ps_x{r}") for r in range(GR)]
        ps_r = [psum(nc, ctx, f"{nm}ps_r{r}") for r in range(GR)]
        s = {n: semaphore(nc, k, nm + n) for n in (
            "idx_staged", "pool_step", "pe_step", "act_step", "zero", "x_turned", "run_ready", "run_turned", "rows_ready")}
        gath = [semaphore(nc, k, f"{nm}gath{r}") for r in range(GR)]
        kept = [semaphore(nc, k, f"{nm}kept{r}") for r in range(GR)]
        store = [semaphore(nc, k, f"{nm}store{r}") for r in range(GR)]
        GB = 16 * GQ
        loop = lambda eng, body: peeled(eng, GU // GR, body)

        with nc.Block() as block:
            @block.gpsimd
            def _(pool):
                def body(i, first, last):
                    for r in range(GR):
                        u = i * GR + r
                        if not first:
                            pool.wait_ge(s["x_turned"], u - GR + 1)
                            pool.sem_inc(s["pool_step"], 1)
                        pool.wait_ge(s["idx_staged"], u + 1)
                        pool.sem_inc(s["pool_step"], 1)
                        for j in range(GQ):
                            pool.indirect_dma_start(xs[r][:, j, :], None, table,
                                                    bass.IndirectOffsetOnAxis(idx[r][:, j:j + 1], 0)).then_inc(gath[r], 16)
                loop(pool, body)

            @block.sync
            def _(sp):
                def body(i, first, last):
                    for r in range(GR):
                        u = i * GR + r
                        if not first:
                            sp.wait_ge(s["run_ready"], u - GR + 1)
                        sp.dma_start(keep[r][:], bass.AP(k.same_d.tensor, u * GT, [[0, D], [1, GT]])).then_inc(kept[r], 16)
                loop(sp, body)

            @block.tensor
            def _(pe):
                def turn_back(u, r, free):
                    pe.wait_ge(s["run_ready"], u + 1)
                    if free:
                        pe.wait_ge(s["rows_ready"], u - GR + 1)
                    pe.sem_inc(s["pe_step"], 1)
                    for j in range(GQ):
                        ins = pe.transpose(ps_r[r][0:T, j * D:(j + 1) * D], run[r][:, j * T:(j + 1) * T], k.ident[0:D, 0:D])
                    ins.then_inc(s["run_turned"], 1)

                def body(i, first, last):
                    for r in range(GR):
                        u = i * GR + r
                        if not first:
                            pe.wait_ge(s["run_ready"], u - GR + 1)
                        pe.wait_ge(gath[r], GB * (i + 1))
                        pe.sem_inc(s["pe_step"], 1)
                        for j in range(GQ):
                            ins = pe.transpose(ps_x[r][0:D, j * T:(j + 1) * T], xs[r][:, j, :], k.ident[0:T, 0:T])
                        ins.then_inc(s["x_turned"], 1)
                        if r:
                            turn_back(u - 1, r - 1, not first)
                    turn_back(i * GR + GR - 1, GR - 1, not first)
                loop(pe, body)

            @block.vector
            def _(dve):
                dve.memset(start[:], 0.0).then_inc(s["zero"], 1)

                def body(i, first, last):
                    for r in range(GR):
                        u = i * GR + r
                        dve.wait_ge(s["x_turned"], u + 1)
                        dve.wait_ge(kept[r], 16 * (i + 1))
                        if not first:
                            dve.wait_ge(s["run_turned"], u - GR + 1)
                        if first and r == 0:
                            dve.wait_ge(s["zero"], 1)
                        else:
                            dve.wait_ge(s["run_ready"], u)
                        before = start[:] if first and r == 0 else run[(r + GR - 1) % GR][:, GT - 1:GT]
                        dve.tensor_tensor_scan(run[r][:], keep[r][:], ps_x[r][0:D, 0:GT], before,
                                               ALU.mult, ALU.add).then_inc(s["run_ready"], 1)
                loop(dve, body)

            @block.scalar
            def _(act):
                def stage(u, r):
                    act.activation(idx[r][:], k.src_tile[:, bass.ds(u * GQ, GQ)], ACT.Copy).then_inc(s["idx_staged"], 1)

                def leave(u, r, stored):
                    act.wait_ge(s["run_turned"], u + 1)
                    if stored is not None:
                        act.wait_ge(store[r], stored)
                    act.activation(rows[r][:].rearrange("e j f -> e (j f)"), ps_r[r][0:T, 0:GQ * D],
                                   ACT.Copy).then_inc(s["rows_ready"], 1)
                    act.wait_ge(s["rows_ready"], u + 1)
                    act.dma_start(k.sum_d.rearrange("(e g) f -> e g f", g=G)[:, bass.ds(u * GQ, GQ), :],
                                  rows[r][:]).then_inc(store[r], 16)

                for r in range(GR):
                    stage(r, r)

                def body(i, first, last):
                    for r in range(GR):
                        u = i * GR + r
                        if not last:
                            act.wait_ge(gath[r], GB * (i + 1))
                            act.sem_inc(s["act_step"], 1)
                            stage(u + GR, r)
                        if r:
                            leave(u - 1, r - 1, None if first else 16 * i)
                    leave(i * GR + GR - 1, GR - 1, None if first else 16 * i)
                loop(act, body)
                for r in range(GR):
                    act.wait_ge(store[r], 16 * (GU // GR))


def dense_layers(nc, k, a, out, x_node):
    KC = HID // 128
    BW = 500
    with ExitStack() as tmp:
        nm = "d_"
        agg = sbuf(nc, tmp, nm + "agg", [T, NT, D])
        hT = sbuf(nc, tmp, nm + "hT", [D, N])
        h1 = sbuf(nc, tmp, nm + "h1", [128, KC, N])
        h2 = sbuf(nc, tmp, nm + "h2", [128, KC, N])
        w1 = sbuf(nc, tmp, nm + "w1", [D, HID])
        w2 = sbuf(nc, tmp, nm + "w2", [128, KC, HID])
        w3 = sbuf(nc, tmp, nm + "w3", [128, KC, D])
        b1 = sbuf(nc, tmp, nm + "b1", [128, KC])
        b2 = sbuf(nc, tmp, nm + "b2", [128, KC])
        b3 = sbuf(nc, tmp, nm + "b3", [T, D])
        o = sbuf(nc, tmp, nm + "o", [T, NT, D])
        y = sbuf(nc, tmp, nm + "y", [T, NT, D])
        sq = sbuf(nc, tmp, nm + "sq", [T, NT, D])
        mean, var, std = (sbuf(nc, tmp, nm + n, [T, NT]) for n in ("mean", "var", "std"))
        ps = [psum(nc, tmp, f"{nm}ps{i}") for i in range(4)]
        ps_o = [psum(nc, tmp, f"{nm}ps_o{i}") for i in range(2)]
        s = {n: semaphore(nc, k, nm + n) for n in (
            "load", "gather", "dve", "turned", "copied", "mm1", "mm2", "mm3", "h1", "h2", "out", "fin", "finb", "store")}
        blocks = [(n0, min(BW, N - n0)) for n0 in range(0, N, BW)]
        NBK = len(blocks)
        with nc.Block() as block:
            @block.gpsimd
            def _(pool):
                for t in range(NT):
                    pool.indirect_dma_start(agg[:, t, :], None, k.sum_d,
                                            bass.IndirectOffsetOnAxis(k.edge_idx[:, t:t + 1], 0)).then_inc(s["gather"], 16)
                pool.wait_ge(s["gather"], 16 * NT)

            @block.sync
            def _(sp):
                ld = Dma(sp, s["load"])
                ld.start(w1[:], a["L1_gnn_W1"])
                ld.start(w2[:], a["L1_gnn_W2"].rearrange("(c p) f -> p c f", p=128))
                ld.start(w3[:], a["L1_gnn_W3"].rearrange("(c p) f -> p c f", p=128))
                ld.start(b1[:], a["L1_gnn_b1"].rearrange("(c p) -> p c", p=128), elements=True)
                ld.start(b2[:], a["L1_gnn_b2"].rearrange("(c p) -> p c", p=128), elements=True)
                ld.start(b3[:], bass.AP(a["L1_gnn_b3"].tensor, 0, [[0, T], [1, D]]))
                ld.wait()
                sp.wait_ge(s["fin"], 8)
                sp.dma_start(out.rearrange("(p t) d -> p t d", t=NT), y[:]).then_inc(s["store"], 16)
                sp.wait_ge(s["store"], 16)

            @block.vector
            def _(dve):
                dve.wait_ge(s["gather"], 16 * NT)
                dve.tensor_tensor(agg[:], agg[:], x_node[:], ALU.add).then_inc(s["dve"], 1)
                for t in range(NT):
                    dve.wait_ge(s["turned"], t + 1)
                    dve.tensor_copy(hT[:, t * T:(t + 1) * T], ps[t % 4][0:D, 0:T]).then_inc(s["copied"], 1)
                dve.wait_ge(s["load"], 96)
                for t in range(NT):
                    dve.wait_ge(s["mm3"], t + 1)
                    dve.tensor_tensor(o[:, t, :], ps_o[t % 2][0:T, 0:D], b3[:], ALU.add).then_inc(s["out"], 1)
                dve.wait_ge(s["out"], NT)
                layer_norm(dve, Link(dve, s["fin"]), s["finb"], x_node, o, sq, mean, var, std, y)

            @block.tensor
            def _(pe):
                pe.wait_ge(s["dve"], 1)
                for t in range(NT):
                    if t >= 4:
                        pe.wait_ge(s["copied"], t - 3)
                    pe.transpose(ps[t % 4][0:D, 0:T], agg[:, t, :], k.ident[0:T, 0:T]).then_inc(s["turned"], 1)
                pe.wait_ge(s["copied"], NT)
                pe.wait_ge(s["load"], 96)
                n = 0
                for n0, w in blocks:
                    for c in range(KC):
                        if n >= 4:
                            pe.wait_ge(s["h1"], n - 3)
                        pe.matmul(ps[n % 4][:, 0:w], w1[:, c * 128:(c + 1) * 128], hT[:, n0:n0 + w],
                                  start=True, stop=True).then_inc(s["mm1"], 1)
                        n += 1
                pe.wait_ge(s["h1"], KC * NBK)
                n = 0
                for n0, w in blocks:
                    for c in range(KC):
                        if n >= 4:
                            pe.wait_ge(s["h2"], n - 3)
                        for kc in range(KC):
                            ins = pe.matmul(ps[n % 4][:, 0:w], w2[:, kc, c * 128:(c + 1) * 128], h1[:, kc, n0:n0 + w],
                                            start=(kc == 0), stop=(kc == KC - 1))
                        ins.then_inc(s["mm2"], 1)
                        n += 1
                pe.wait_ge(s["h2"], KC * NBK)
                for t in range(NT):
                    if t >= 2:
                        pe.wait_ge(s["out"], t - 1)
                    for kc in range(KC):
                        ins = pe.matmul(ps_o[t % 2][0:T, 0:D], h2[:, kc, t * T:(t + 1) * T], w3[:, kc, :],
                                        start=(kc == 0), stop=(kc == KC - 1))
                    ins.then_inc(s["mm3"], 1)

            @block.scalar
            def _(act):
                act.wait_ge(s["load"], 96)
                for ready, done, h, bias in ((s["mm1"], s["h1"], h1, b1), (s["mm2"], s["h2"], h2, b2)):
                    n = 0
                    for n0, w in blocks:
                        for c in range(KC):
                            act.wait_ge(ready, n + 1)
                            act.activation(h[:, c, n0:n0 + w], ps[n % 4][:, 0:w], ACT.Relu,
                                           bias=bias[:, c:c + 1]).then_inc(done, 1)
                            n += 1
                act.wait_ge(s["fin"], 6)
                act.activation(std[:], var[:], ACT.Sqrt).then_inc(s["finb"], 1)


def build(nc, a, out):
    ctx = ExitStack()
    k = Program(ctx)

    def dram(name, shape, dt=F32):
        return nc.dram_tensor(name, shape, dt, kind="Internal").ap()

    with ctx:
        k.key_d = dram("key_d", [G])
        k.w_d = dram("w_d", [UT])
        k.keys_d = dram("keys_d", [SLOTS + 1])
        k.lim_d = dram("lim_d", [SLOTS + 1])
        k.row_d = dram("row_d", [NW * WN], I32)
        k.last_d = dram("last_d", [G])
        k.same_d = dram("same_d", [E])
        k.xw_d = dram("xw_d", [UT, WN * D])
        k.sum_d = dram("sum_d", [T * G, D])
        build_staircase(nc, k, a, ctx)

        x0 = sbuf(nc, ctx, "x0", [T, NT, D])
        x1 = sbuf(nc, ctx, "x1", [T, NT, D])
        load_x = semaphore(nc, k, "load_x")
        with nc.Block() as block:
            @block.sync
            def _(sp):
                sp.dma_start(x0[:], a["x"].rearrange("(p t) d -> p t d", t=NT)).then_inc(load_x, 16)
                sp.wait_ge(load_x, 16)

        x1_d = dram("x1_d", [N, D])
        nodes = [x0, x1, x1]
        for n, H in enumerate((a["L0_gnn_att1"].shape[0], a["L0_gnn_att2"].shape[0])):
            nm = f"L{n + 1}_"
            lay = Layer(nm=nm, H=H, Wl=a[f"L0_gnn_W{n + 1}l"], Wr=a[f"L0_gnn_W{n + 1}r"],
                                  att=a[f"L0_gnn_att{n + 1}"], bias=a[f"L0_gnn_b{n + 1}"],
                                  x_node=nodes[n], next_table=x1_d, next_node=nodes[n + 1],
                                  logit_d=dram(nm + "logit_d", [H, SLOTS]), norm=n == 1,
                                  v_d=dram(nm + "v_d", [UT * WN, H * XW]), max_d=dram(nm + "max_d", [T * UT, H]))
            if n == 0:
                before = set(k.sems)
            else:
                with nc.Block() as block:
                    @block.gpsimd
                    def _(pool):
                        for name in sorted(n for n in set(k.sems) - before if not n.startswith("L1_")):
                            pool.sem_clear(k.sems[name])
            with ExitStack() as lctx:
                if lay.norm:
                    lay.sq = sbuf(nc, lctx, nm + "sq", [T, NT, D])
                    lay.mean, lay.var, lay.std = (sbuf(nc, lctx, nm + v, [T, NT]) for v in ("mean", "var", "std"))
                    lay.fin_steps = 8

                    def finish(dve, link, finb, o, lay=lay):
                        layer_norm(dve, link, finb, x0, o, lay.sq, lay.mean, lay.var, lay.std, lay.next_node)
                else:
                    lay.fin_steps = 1

                    def finish(dve, link, finb, o, lay=lay):
                        link(dve.tensor_scalar(lay.next_node[:], o[:], 0.0, None, ALU.max))
                prepare_layer(nc, k, lctx, lay)
                lay.node_max = sbuf(nc, lctx, nm + "node_max", [T, NT, H])
                lay.xs_d = dram(nm + "xs_d", [U, T, Q * lay.XR])
                with ExitStack() as ectx:
                    lay.a_edge = sbuf(nc, ectx, nm + "a_edge", [T, UT, H])
                    lay.m_edge = sbuf(nc, ectx, nm + "m_edge", [T, UT, H])
                    lay.lin_edge = lay.a_edge
                    edge_logits(nc, k, lay)
                    edge_softmax(nc, k, lay)
                    edge_sums(nc, k, lay)
                merge_nodes(nc, k, lay, finish)
        neighbour_sums(nc, k, x1_d)
        dense_layers(nc, k, a, out, x1)


_INS = ["x", "src", "dst", "L0_gnn_W1l", "L0_gnn_W1r", "L0_gnn_att1", "L0_gnn_b1", "L0_gnn_W2l", "L0_gnn_W2r",
        "L0_gnn_att2", "L0_gnn_b2", "L1_gnn_W1", "L1_gnn_b1", "L1_gnn_W2", "L1_gnn_b2", "L1_gnn_W3", "L1_gnn_b3"]


def kernel(**inputs):
    import numpy as np
    import concourse.bacc as bacc
    from concourse import mybir as _mybir
    from concourse.bass_utils import run_bass_kernel_spmd

    nc = bacc.Bacc("TRN2", target_bir_lowering=False, num_devices=1)
    arrays, args = {}, {}
    for name in _INS:
        arr = np.ascontiguousarray(inputs[name])
        arrays[f"in_{name}_dram"] = arr
        args[name] = nc.dram_tensor(f"in_{name}_dram", arr.shape, _mybir.dt.from_np(arr.dtype),
                                    kind="ExternalInput").ap()
    out = nc.dram_tensor("out_dram", (N, D), _mybir.dt.float32, kind="ExternalOutput").ap()
    build(nc, args, out)
    r = run_bass_kernel_spmd(nc, [arrays], core_ids=[0])
    return r.results[0]["out_dram"]
```

```python
from contextlib import ExitStack

import concourse.bass as bass
from concourse import mybir

F32 = mybir.dt.float32
BF16 = mybir.dt.bfloat16
I32 = mybir.dt.int32
ALU = mybir.AluOpType
ACT = mybir.ActivationFunctionType
AX = mybir.AxisListType

N, D, E = 3125, 64, 100000
HID = 256
SLOPE = 0.2
EPS = 1e-5
T = 125
G = E // T
WN = 32
NW = -(-N // WN)
Q = 4
R = 3
U = -(-(G + NW - 1) // (Q * R)) * R
UT = U * Q
SLOTS = UT * T
QT = Q * T
NT = N // T
TG = 5
BG = 3
BLK = 100
NB = UT // BLK
GQ, GR = 4, 4
GU = G // GQ
KT = G // BLK
CH = 120
BIG = 1.5e38
XW = D + 1
PAD = NW * WN
assert UT % BLK == 0 and N % T == 0 and E % T == 0 and U % R == 0 and NT % TG == 0 and NB % BG == 0
assert G % BLK == 0 and GU % GR == 0


class Program:

    def __init__(self, ctx):
        self.ctx, self.sems = ctx, {}


class Layer:

    def __init__(self, nm, H, Wl, Wr, att, bias, x_node, x_pad, next_table, next_node, logit_d, v_d, max_d, norm):
        self.nm, self.H, self.Wl, self.Wr, self.att, self.bias = nm, H, Wl, Wr, att, bias
        self.x_node, self.x_pad, self.next_table, self.next_node = x_node, x_pad, next_table, next_node
        self.logit_d, self.v_d, self.max_d, self.norm = logit_d, v_d, max_d, norm
        self.XR = XW + H


class Link:

    def __init__(self, eng, sem):
        self.eng, self.sem, self.n = eng, sem, 0

    def __call__(self, ins):
        self.n += 1
        ins.then_inc(self.sem, 1)
        self.eng.wait_ge(self.sem, self.n)


class Dma:

    def __init__(self, eng, sem):
        self.eng, self.sem, self.n = eng, sem, 0

    def start(self, out, in_, elements=False):
        self.n += 16
        self.eng.dma_start(out, in_, allow_slow_non_contiguous=elements).then_inc(self.sem, 16)

    def wait(self):
        self.eng.wait_ge(self.sem, self.n)


def peeled(eng, count, body):
    body(0, True, False)
    with eng.Fori(1, count - 1) as i:
        body(i, False, False)
    body(count - 1, False, True)


def loop3(eng, body):
    peeled(eng, U // R, body)


def sbuf(nc, ctx, name, shape, dt=F32):
    return ctx.enter_context(nc.sbuf_tensor(name, shape, dt))


def psum(nc, ctx, name, shape=(128, 512)):
    return ctx.enter_context(nc.psum_tensor(name, list(shape), F32))


def semaphore(nc, k, name):
    if name not in k.sems:
        k.sems[name] = k.ctx.enter_context(nc.semaphore(name))
    return k.sems[name]


def build_staircase(nc, k, a, ctx0, x0):
    k.ident = sbuf(nc, ctx0, "ident", [128, 128])
    k.node_in_window = sbuf(nc, ctx0, "node_in_window", [T, WN])
    k.dst_local = sbuf(nc, ctx0, "dst_local", [T, UT])
    k.src_idx = sbuf(nc, ctx0, "src_idx", [T, UT], I32)
    k.win_idx = sbuf(nc, ctx0, "win_idx", [BLK, NB], I32)
    k.same = sbuf(nc, ctx0, "same", [128, UT])
    k.row_idx = sbuf(nc, ctx0, "row_idx", [T, NT], I32)
    k.max_idx = sbuf(nc, ctx0, "max_idx", [T, NT], I32)
    k.edge_idx = sbuf(nc, ctx0, "edge_idx", [T, NT], I32)
    k.src_tile = sbuf(nc, ctx0, "src_tile", [T, G], I32)
    k.pcol = sbuf(nc, ctx0, "pcol", [128, 1])

    with ExitStack() as ctx:
        dg = sbuf(nc, ctx, "dg", [BLK, G // BLK, T], I32)
        gnum_i = sbuf(nc, ctx, "gnum_i", [BLK, G // BLK], I32)
        ucol_i = sbuf(nc, ctx, "ucol_i", [BLK, NB], I32)
        pcol_i = sbuf(nc, ctx, "pcol_i", [128, 1], I32)
        niw_i = sbuf(nc, ctx, "niw_i", [T, WN], I32)
        lastw_i = sbuf(nc, ctx, "lastw_i", [BLK, G // BLK], I32)
        gnum = sbuf(nc, ctx, "gnum", [BLK, G // BLK])
        key = sbuf(nc, ctx, "key", [BLK, G // BLK])
        ucol = sbuf(nc, ctx, "ucol", [BLK, NB])
        key_all = sbuf(nc, ctx, "key_all", [BLK, G])
        cmp = sbuf(nc, ctx, "cmp", [128, UT])
        gcnt = sbuf(nc, ctx, "gcnt", [BLK, NB])
        gidx = sbuf(nc, ctx, "gidx", [BLK, NB], I32)
        wcol = sbuf(nc, ctx, "wcol", [BLK, NB])
        w32 = sbuf(nc, ctx, "w32", [BLK, NB])
        wrow = sbuf(nc, ctx, "wrow", [128, UT])
        win_f = sbuf(nc, ctx, "win_f", [BLK, NB])
        wcnt = sbuf(nc, ctx, "wcnt", [NW, 1])
        wl32 = sbuf(nc, ctx, "wl32", [NW, 1])
        rowf = sbuf(nc, ctx, "rowf", [NW, WN])
        rowi = sbuf(nc, ctx, "rowi", [NW, WN], I32)
        sg = sbuf(nc, ctx, "sg", [BLK, KT, T], I32)
        sgf = sbuf(nc, ctx, "sgf", [BLK, KT, T])
        dgf = sbuf(nc, ctx, "dgf", [BLK, KT * T])
        dprev_i = sbuf(nc, ctx, "dprev_i", [BLK, 1], I32)
        dprev = sbuf(nc, ctx, "dprev", [BLK, 1])
        same_edge = sbuf(nc, ctx, "same_edge", [BLK, KT * T])
        lastd = sbuf(nc, ctx, "lastd", [BLK, KT])
        last_all = sbuf(nc, ctx, "last_all", [T, G])
        node_i = sbuf(nc, ctx, "node_i", [T, NT], I32)
        nodew_i = sbuf(nc, ctx, "nodew_i", [T, NT], I32)
        node_half = sbuf(nc, ctx, "node_half", [T, NT])
        node_win = sbuf(nc, ctx, "node_win", [T, NT])
        side = sbuf(nc, ctx, "side", [T, G])
        side2 = sbuf(nc, ctx, "side2", [T, T])
        tiles_upto = sbuf(nc, ctx, "tiles_upto", [T, NT])
        tile_i = sbuf(nc, ctx, "tile_i", [T, NT], I32)
        dst_of = sbuf(nc, ctx, "dst_of", [T, NT, T], I32)
        edges_upto = sbuf(nc, ctx, "edges_upto", [T, NT])
        none = sbuf(nc, ctx, "none", [T, NT])
        place = sbuf(nc, ctx, "place", [T, NT])
        idxf = sbuf(nc, ctx, "idxf", [T, NT])
        srcu = sbuf(nc, ctx, "srcu", [BLK, NB * T], I32)
        dstu = sbuf(nc, ctx, "dstu", [BLK, NB * T], I32)
        srcf = sbuf(nc, ctx, "srcf", [BLK, NB * T])
        dstf = sbuf(nc, ctx, "dstf", [BLK, NB * T])
        dl = sbuf(nc, ctx, "dl", [BLK, NB * T])
        ge0 = sbuf(nc, ctx, "ge0", [BLK, NB * T])
        keyu = sbuf(nc, ctx, "keyu", [BLK, NB * T])
        keyp = sbuf(nc, ctx, "keyp", [BLK, NB * T])
        zero = sbuf(nc, ctx, "zero", [PAD - N, D])
        no_key = sbuf(nc, ctx, "no_key", [1, 1])
        no_more = sbuf(nc, ctx, "no_more", [1, 1])
        ps = [psum(nc, ctx, f"ps_setup{i}") for i in range(6)]
        s = {n: k.setup.enter_context(nc.semaphore("st_" + n)) for n in (
            "load", "iota", "ident0", "ident", "dve", "dve2", "dve3", "store", "transposed", "pad",
            "load2", "sides", "last", "upto2", "node", "keys", "lim", "x_pad")}
        k.setup_sems = dict(s)
        s["gather"] = semaphore(nc, k, "st_gather")
        gather2 = [semaphore(nc, k, f"st_gather2_{g}") for g in range(NT // TG)]

        with nc.Block() as block:
            @block.sync
            def _(sp):
                sp.dma_start(dg[:], a["dst"].rearrange("(p k e) -> p k e", k=KT, e=T)).then_inc(s["load"], 16)
                ld = Dma(sp, s["load2"])
                ld.start(x0[:], a["x"].rearrange("(p t) d -> p t d", t=NT))
                ld.start(sg[:], a["src"].rearrange("(p k e) -> p k e", k=KT, e=T))
                sp.wait_ge(s["pad"], 4)
                ld.start(dprev_i[1:BLK, :], bass.AP(a["dst"].tensor, KT * T - 1, [[KT * T, BLK - 1], [1, 1]]), elements=True)
                ld.wait()
                xs = Dma(sp, s["x_pad"])
                xs.start(k.x0_d[0:N, :].rearrange("(p t) d -> p t d", t=NT), x0[:])
                xs.start(k.x0_d[N:PAD, :], zero[:])
                xs.start(k.x1_d[N:PAD, :], zero[:])
                sp.wait_ge(s["dve"], 4)
                st = Dma(sp, s["store"])
                st.start(k.key_d.rearrange("(p k) -> p k", k=G // BLK), key[:])
                st.wait()
                st.start(key_all[:], bass.AP(k.key_d.tensor, 0, [[0, BLK], [1, G]]))
                sp.wait_ge(s["dve"], 8)
                la = Dma(sp, s["last"])
                la.start(k.last_d.rearrange("(p k) -> p k", k=KT), lastd[:])
                la.wait()
                la.start(last_all[:], bass.AP(k.last_d.tensor, 0, [[0, T], [1, G]]))
                sp.wait_ge(s["dve"], 15)
                la.start(k.same_d.rearrange("(p e) -> p e", p=BLK), same_edge[:])
                st.wait()
                la.wait()
                xs.wait()

            @block.gpsimd
            def _(pool):
                pool.iota(gnum_i[:], [[1, G // BLK]], base=0, channel_multiplier=G // BLK).then_inc(s["iota"], 1)
                pool.iota(ucol_i[:], [[BLK, NB]], base=0, channel_multiplier=1).then_inc(s["iota"], 1)
                pool.iota(pcol_i[:], [[0, 1]], base=0, channel_multiplier=1).then_inc(s["iota"], 1)
                pool.iota(niw_i[:], [[1, WN]], base=0, channel_multiplier=0).then_inc(s["iota"], 1)
                pool.memset(k.ident[:], 0.0).then_inc(s["ident0"], 1)
                pool.memset(no_key[:], -5.0).then_inc(s["pad"], 1)
                pool.memset(no_more[:], -BIG).then_inc(s["pad"], 1)
                pool.memset(dprev_i[:], -1).then_inc(s["pad"], 1)
                pool.memset(zero[:], 0.0).then_inc(s["pad"], 1)
                pool.iota(node_i[:], [[1, NT]], base=0, channel_multiplier=NT).then_inc(s["iota"], 1)
                pool.wait_ge(s["ident0"], 1)
                pool.affine_select(out=k.ident[:], in_=k.ident[:], compare_op=ALU.not_equal, fill=1.0,
                                   base=0, pattern=[[-1, 128]], channel_multiplier=1).then_inc(s["ident"], 1)

            @block.vector
            def _(dve):
                link = Link(dve, s["dve"])
                dve.wait_ge(s["load"], 16)
                dve.wait_ge(s["iota"], 5)
                link(dve.tensor_scalar(lastw_i[:], dg[:, :, T - 1], 5, None, ALU.arith_shift_right))
                link(dve.tensor_copy(key[:], lastw_i[:]))
                link(dve.tensor_copy(gnum[:], gnum_i[:]))
                link(dve.tensor_tensor(key[:], key[:], gnum[:], ALU.add))
                link(dve.tensor_copy(ucol[:], ucol_i[:]))
                link(dve.tensor_copy(k.pcol[:], pcol_i[:]))
                link(dve.tensor_copy(k.node_in_window[:], niw_i[:]))
                link(dve.tensor_copy(lastd[:], dg[:, :, T - 1]))
                link(dve.tensor_scalar(nodew_i[:], node_i[:], 5, None, ALU.arith_shift_right))
                link(dve.tensor_copy(node_win[:], nodew_i[:]))
                link(dve.tensor_scalar(node_half[:], node_i[:], 0.5, None, ALU.add))
                dve.wait_ge(s["load2"], 48)
                link(dve.tensor_copy(dgf[:], dg[:].rearrange("p k e -> p (k e)")))
                link(dve.tensor_copy(dprev[:], dprev_i[:]))
                link(dve.tensor_tensor(same_edge[:, 1:KT * T], dgf[:, 1:KT * T], dgf[:, 0:KT * T - 1], ALU.is_equal))
                link(dve.tensor_tensor(same_edge[:, 0:1], dgf[:, 0:1], dprev[:], ALU.is_equal))
                link(dve.tensor_copy(sgf[:], sg[:]))

        with nc.Block() as block:
            @block.vector
            def _(dve):
                link = Link(dve, s["dve2"])
                for b in range(NB):
                    link(dve.tensor_scalar(cmp[0:BLK, 0:G], key_all[:], ucol[:, b:b + 1], None, ALU.is_lt))
                    link(dve.tensor_reduce(gcnt[:, b:b + 1], cmp[0:BLK, 0:G], AX.X, ALU.add))
                link(dve.tensor_scalar(gcnt[:], gcnt[:], float(G - 1), None, ALU.min))
                link(dve.tensor_copy(gidx[:], gcnt[:]))
                link(dve.tensor_tensor(wcol[:], ucol[:], gcnt[:], ALU.subtract))
                link(dve.tensor_scalar(w32[:], wcol[:], float(WN), None, ALU.mult))

            @block.gpsimd
            def _(pool):
                pool.wait_ge(s["dve2"], 2 * NB + 2)
                for b in range(NB):
                    pool.indirect_dma_start(srcu[:, b * T:(b + 1) * T], None, a["src"].rearrange("(g e) -> g e", e=T),
                                            bass.IndirectOffsetOnAxis(gidx[:, b:b + 1], 0)).then_inc(s["gather"], 16)
                    pool.indirect_dma_start(dstu[:, b * T:(b + 1) * T], None, a["dst"].rearrange("(g e) -> g e", e=T),
                                            bass.IndirectOffsetOnAxis(gidx[:, b:b + 1], 0)).then_inc(s["gather"], 16)
                pool.wait_ge(s["gather"], 32 * NB)

            @block.sync
            def _(sp):
                st = Dma(sp, s["store"])
                st.n = 32
                sp.wait_ge(s["dve2"], 2 * NB + 3)
                st.start(k.w_d.rearrange("(b p) -> p b", p=BLK), wcol[:], elements=True)
                st.wait()
                st.start(wrow[:], bass.AP(k.w_d.tensor, 0, [[0, 128], [1, UT]]))
                st.wait()

            @block.scalar
            def _(act):
                for t in range(NT):
                    if t:
                        act.wait_ge(s["sides"], t)
                    act.activation(side[:], last_all[:], ACT.Sign, bias=node_half[:, t:t + 1], scale=-1.0,
                                   accum_out=tiles_upto[:, t:t + 1]).then_inc(s["sides"], 1)
                act.wait_ge(s["sides"], NT)

        with nc.Block() as block:
            @block.vector
            def _(dve):
                node = Link(dve, s["node"])
                node(dve.tensor_scalar(tiles_upto[:], tiles_upto[:], 0.5, G / 2, ALU.mult, ALU.add))
                node(dve.tensor_scalar(tiles_upto[:], tiles_upto[:], float(G - 1), None, ALU.min))
                node(dve.tensor_copy(tile_i[:], tiles_upto[:]))
                link = Link(dve, s["dve3"])
                link(dve.tensor_copy(srcf[:], srcu[:]))
                link(dve.tensor_copy(dstf[:], dstu[:]))
                for b in range(NB):
                    c = slice(b * T, (b + 1) * T)
                    link(dve.tensor_scalar(dl[:, c], dstf[:, c], w32[:, b:b + 1], None, ALU.subtract))
                link(dve.tensor_scalar(ge0[:], dl[:], 0.0, None, ALU.is_ge))
                link(dve.scalar_tensor_tensor(out=ge0[:], in0=dl[:], scalar=float(WN), in1=ge0[:],
                                              op0=ALU.is_lt, op1=ALU.mult))
                link(dve.scalar_tensor_tensor(out=keyu[:], in0=dstf[:], scalar=1.0, in1=ge0[:],
                                              op0=ALU.add, op1=ALU.mult))
                link(dve.tensor_scalar(keyu[:], keyu[:], -1.0, None, ALU.add))
                link(dve.tensor_scalar(win_f[:], wcol[:], float(NW - 1), None, ALU.min))
                link(dve.tensor_copy(k.win_idx[:], win_f[:]))
                link(dve.memset(k.same[:, 0:1], 0.0))
                link(dve.tensor_tensor(k.same[:, 1:UT], wrow[:, 1:UT], wrow[:, 0:UT - 1], ALU.is_equal))
                link(dve.tensor_scalar(cmp[0:NW, :], wrow[0:NW, :], k.pcol[0:NW, :], None, ALU.is_le))
                link(dve.tensor_reduce(wcnt[:], cmp[0:NW, :], AX.X, ALU.add))
                link(dve.tensor_scalar(wcnt[:], wcnt[:], -1.0, None, ALU.add))
                link(dve.tensor_scalar(wl32[:], wcnt[:], float(WN), None, ALU.mult))
                link(dve.tensor_scalar(rowf[:], k.node_in_window[0:NW, :], wl32[:], None, ALU.add))
                link(dve.tensor_copy(rowi[:], rowf[:]))
                dve.wait_ge(s["transposed"], 2 * NB + KT)
                link(dve.tensor_copy(k.src_idx[:, 0:5 * BLK], ps[0][0:T, 0:5 * BLK]))
                link(dve.tensor_copy(k.src_idx[:, 5 * BLK:UT], ps[1][0:T, 0:4 * BLK]))
                link(dve.tensor_copy(k.dst_local[:, 0:5 * BLK], ps[2][0:T, 0:5 * BLK]))
                link(dve.tensor_copy(k.dst_local[:, 5 * BLK:UT], ps[3][0:T, 0:4 * BLK]))
                for half in range(2):
                    link(dve.tensor_copy(k.src_tile[:].rearrange("e (p k) -> e k p", k=KT)[:, half * KT // 2:(half + 1) * KT // 2, :],
                                         ps[4 + half][0:T, 0:KT // 2 * BLK].rearrange("e (k p) -> e k p", p=BLK)))
                dve.wait_ge(s["keys"], 16 * (2 * NB + 1))
                dve.tensor_tensor(keyp[:], keyp[:], keyu[:], ALU.is_equal).then_inc(s["lim"], 1)
                dve.wait_ge(s["lim"], 1)
                dve.tensor_scalar(keyp[:], keyp[:], 2 * BIG, -BIG, ALU.mult, ALU.add).then_inc(s["lim"], 1)
                dve.wait_ge(s["upto2"], NT)
                node(dve.tensor_scalar(edges_upto[:], edges_upto[:], 0.5, T / 2, ALU.mult, ALU.add))
                node(dve.tensor_scalar(none[:], edges_upto[:], 0.5, None, ALU.is_lt))
                node(dve.scalar_tensor_tensor(out=place[:], in0=none[:], scalar=float(T), in1=edges_upto[:],
                                              op0=ALU.mult, op1=ALU.add))
                node(dve.tensor_scalar(place[:], place[:], -1.0, None, ALU.add))
                node(dve.tensor_tensor(tiles_upto[:], tiles_upto[:], none[:], ALU.subtract))
                node(dve.tensor_scalar(tiles_upto[:], tiles_upto[:], 0.0, None, ALU.max))
                node(dve.scalar_tensor_tensor(out=idxf[:], in0=place[:], scalar=float(G), in1=tiles_upto[:],
                                              op0=ALU.mult, op1=ALU.add))
                node(dve.tensor_copy(k.edge_idx[:], idxf[:]))
                node(dve.tensor_tensor(tiles_upto[:], tiles_upto[:], node_win[:], ALU.add))
                node(dve.scalar_tensor_tensor(out=idxf[:], in0=place[:], scalar=float(UT), in1=tiles_upto[:],
                                              op0=ALU.mult, op1=ALU.add))
                node(dve.tensor_copy(k.max_idx[:], idxf[:]))

            @block.gpsimd
            def _(pool):
                pool.wait_ge(s["node"], 3)
                for t in range(NT):
                    pool.indirect_dma_start(dst_of[:, t, :], None, a["dst"].rearrange("(g e) -> g e", e=T),
                                            bass.IndirectOffsetOnAxis(tile_i[:, t:t + 1], 0)).then_inc(gather2[t // TG], 16)
                for g in range(NT // TG):
                    pool.wait_ge(gather2[g], 16 * TG)

            @block.scalar
            def _(act):
                for t in range(NT):
                    if t % TG == 0:
                        act.wait_ge(gather2[t // TG], 16 * TG)
                    if t:
                        act.wait_ge(s["upto2"], t)
                    act.activation(side2[:], dst_of[:, t, :], ACT.Sign, bias=node_half[:, t:t + 1], scale=-1.0,
                                   accum_out=edges_upto[:, t:t + 1]).then_inc(s["upto2"], 1)

            @block.tensor
            def _(pe):
                pe.wait_ge(s["dve3"], NB + 2)
                for b in range(NB):
                    c = slice((b % 5) * BLK, (b % 5 + 1) * BLK)
                    pe.transpose(ps[b // 5][0:T, c], srcf[:, b * T:(b + 1) * T],
                                 k.ident[0:BLK, 0:BLK]).then_inc(s["transposed"], 1)
                    pe.transpose(ps[2 + b // 5][0:T, c], dl[:, b * T:(b + 1) * T],
                                 k.ident[0:BLK, 0:BLK]).then_inc(s["transposed"], 1)
                for c in range(KT):
                    h = KT // 2
                    pe.transpose(ps[4 + c // h][0:T, (c % h) * BLK:(c % h + 1) * BLK], sgf[:, c, :],
                                 k.ident[0:BLK, 0:BLK]).then_inc(s["transposed"], 1)

            @block.sync
            def _(sp):
                st = Dma(sp, s["store"])
                st.n = 64
                sp.wait_ge(s["dve3"], NB + 6)
                slots = lambda row, b, off: row[off + b * BLK * T:off + (b + 1) * BLK * T].rearrange("(p e) -> p e", e=T)
                ks = Dma(sp, s["keys"])
                ks.start(k.keys_d[0:1].unsqueeze(0), no_key[:])
                for b in range(NB):
                    ks.start(slots(k.keys_d, b, 1), keyu[:, b * T:(b + 1) * T])
                ks.wait()
                for b in range(NB):
                    ks.start(keyp[:, b * T:(b + 1) * T], slots(k.keys_d, b, 0))
                sp.wait_ge(s["dve3"], NB + 16)
                st.start(k.row_d.rearrange("(w n) -> w n", n=WN), rowi[:])
                st.wait()
                st.start(k.row_idx[:], k.row_d[0:N].rearrange("(p t) -> p t", t=NT))
                ks.wait()
                sp.wait_ge(s["lim"], 2)
                for b in range(NB):
                    st.start(slots(k.lim_d, b, 0), keyp[:, b * T:(b + 1) * T])
                st.start(k.lim_d[SLOTS:SLOTS + 1].unsqueeze(0), no_more[:])
                st.wait()


def prepare_layer(nc, k, ctx, wctx, lay):
    H = lay.H
    C = H * D // 128
    FR = 128 // H
    lay.C, lay.FR = C, FR
    lay.w_abs = sbuf(nc, ctx, lay.nm + "w_abs", [128, C * 128])
    lay.w_lin = sbuf(nc, ctx, lay.nm + "w_lin", [128, H])
    lay.sign = sbuf(nc, ctx, lay.nm + "sign", [128, C])
    lay.sign_sum = sbuf(nc, ctx, lay.nm + "sign_sum", [128, 128 // Q])
    lay.table = nc.dram_tensor(lay.nm + "table_d", [N, lay.XR], F32, kind="Internal").ap()
    lay.win = [sbuf(nc, wctx, f"{lay.nm}win{i}", [BLK, WN * D]) for i in range(2 * BG)]
    with ExitStack() as tmp:
        rows = sbuf(nc, tmp, lay.nm + "rows", [T, NT, lay.XR])
        w_raw = sbuf(nc, tmp, lay.nm + "w_raw", [128, H * D])
        att_row = sbuf(nc, tmp, lay.nm + "att_row", [128, H * D])
        att_abs = sbuf(nc, tmp, lay.nm + "att_abs", [128, H * D])
        w_att = sbuf(nc, tmp, lay.nm + "w_att", [128, H * D])
        sign_row = sbuf(nc, tmp, lay.nm + "sign_row", [128, H * D])
        att_col = sbuf(nc, tmp, lay.nm + "att_col", [128, C])
        head0_i = sbuf(nc, tmp, lay.nm + "head0_i", [128, H], I32)
        head0 = sbuf(nc, tmp, lay.nm + "head0", [128, H])
        in_head = sbuf(nc, tmp, lay.nm + "in_head", [128, H])
        xx = sbuf(nc, tmp, lay.nm + "xx", [T, NT, 2 * D])
        xxT = [sbuf(nc, tmp, f"{lay.nm}xxT{i}", [128, T]) for i in range(3)]
        rel = sbuf(nc, tmp, lay.nm + "rel", [T, 2, H * D])
        ps_t = [psum(nc, tmp, f"{lay.nm}ps_t{i}") for i in range(2)]
        ps_z = [psum(nc, tmp, f"{lay.nm}ps_z{i}") for i in range(2)]
        ps_l = psum(nc, tmp, lay.nm + "ps_l")
        s = {n: semaphore(nc, k, "p_" + n) for n in (
            "load", "dve", "iota", "xx", "xT", "xT_copied", "z", "relu", "used", "lin", "table", "rows")}
        lay.win_in = [semaphore(nc, k, f"{lay.nm}win_in{i}") for i in range(NB // BG)]
        lay.win_out = [semaphore(nc, k, f"p_win_out{i}") for i in range(NB // BG)]
        with nc.Block() as block:
            @block.sync
            def _(sp):
                ld = Dma(sp, s["load"])
                ld.start(w_raw[0:D, :], lay.Wl)
                ld.start(w_raw[D:128, :], lay.Wr)
                ld.start(att_row[:], bass.AP(lay.att.tensor, 0, [[0, 128], [1, H * D]]))
                for h in range(H):
                    ld.start(att_col[h * FR:(h + 1) * FR, :], lay.att[h, :].rearrange("(c r) -> r c", r=FR), elements=True)
                sp.wait_ge(lay.win_in[0], 16 * BG)
                for b in range(BG):
                    sp.dma_start(k.xw_d[b * BLK:(b + 1) * BLK, :], lay.win[b % (2 * BG)][:]).then_inc(lay.win_out[0], 16)
                ld.wait()
                F = SLOTS // (CH // H)
                ll = Dma(sp, lay.lim_loaded)
                for c in range(CH // H):
                    ll.start(lay.lim[c * H:(c + 1) * H, :], bass.AP(k.lim_d.tensor, c * F, [[0, H], [1, F + 1]]))

            @block.gpsimd
            def _(pool):
                pool.memset(rows[:, :, D:XW], 1.0).then_inc(s["rows"], 1)
                pool.iota(head0_i[:], [[-FR, H]], base=0, channel_multiplier=1).then_inc(s["iota"], 1)
                pool.wait_ge(s["load"], 16 * (3 + H))
                for b in range(NB):
                    if b >= 2 * BG and b % BG == 0:
                        pool.wait_ge(lay.win_out[b // BG - 2], 16 * BG)
                    pool.indirect_dma_start(lay.win[b % (2 * BG)][:], None, lay.x_pad.rearrange("(w n) d -> w (n d)", n=WN),
                                            bass.IndirectOffsetOnAxis(k.win_idx[:, b:b + 1], 0)).then_inc(lay.win_in[b // BG], 16)

            @block.vector
            def _(dve):
                link = Link(dve, s["dve"])
                link(dve.tensor_copy(xx[:, :, 0:D], lay.x_node[:, :, :]))
                dve.wait_ge(s["load"], 16 * (3 + H))
                link(dve.tensor_scalar(att_abs[:], att_row[:], -1.0, None, ALU.mult))
                link(dve.tensor_tensor(att_abs[:], att_abs[:], att_row[:], ALU.max))
                for c in range(C):
                    f = slice(c * FR, (c + 1) * FR)
                    link(dve.tensor_tensor(lay.w_abs[:, c * 128:(c + 1) * 128].rearrange("p (h r) -> p h r", h=H),
                                           w_raw[:].rearrange("p (h d) -> p h d", h=H)[:, :, f],
                                           att_abs[:].rearrange("p (h d) -> p h d", h=H)[:, :, f], ALU.mult))
                link(dve.tensor_tensor(w_att[:], w_raw[:], att_row[:], ALU.mult))
                link(dve.tensor_reduce(lay.w_lin[:], w_att[:].rearrange("p (h d) -> p h d", h=H), AX.X, ALU.add))
                link(dve.tensor_scalar(lay.w_lin[:], lay.w_lin[:], SLOPE, None, ALU.mult))
                for c in range(C):
                    f = slice(c * FR, (c + 1) * FR)
                    link(dve.tensor_scalar(sign_row[:, c * 128:(c + 1) * 128].rearrange("p (h r) -> p h r", h=H),
                                           att_row[:].rearrange("p (h d) -> p h d", h=H)[:, :, f], 0.0, 2.0,
                                           ALU.is_ge, ALU.mult))
                link(dve.tensor_scalar(sign_row[:], sign_row[:], -1.0, None, ALU.add))
                link(dve.tensor_scalar(att_col[:], att_col[:], 0.0, 2.0, ALU.is_ge, ALU.mult))
                link(dve.tensor_scalar(lay.sign[:], att_col[:], -1.0, None, ALU.add))
                dve.wait_ge(s["iota"], 1)
                link(dve.tensor_copy(head0[:], head0_i[:]))
                link(dve.tensor_scalar(in_head[:], head0[:], 0.0, None, ALU.is_ge))
                link(dve.scalar_tensor_tensor(out=in_head[:], in0=head0[:], scalar=float(FR), in1=in_head[:],
                                              op0=ALU.is_lt, op1=ALU.mult))
                link(dve.memset(lay.sign_sum[:], 0.0))
                link(dve.tensor_scalar(lay.sign_sum[:, 0:H], in_head[:], lay.sign[:, 0:1], None, ALU.mult))
                link(dve.tensor_scalar(lay.sign[:, 1:C], lay.sign[:, 1:C], lay.sign[:, 0:1], None, ALU.mult))

                def reduce(t):
                    dve.wait_ge(s["relu"], t + 1)
                    dve.tensor_tensor(rel[:, t % 2, :], rel[:, t % 2, :], sign_row[0:T, :],
                                      ALU.mult).then_inc(s["used"], 1)
                    dve.wait_ge(s["used"], 2 * t + 1)
                    dve.tensor_reduce(lay.self_logit[:, t, :],
                                      rel[:, t % 2, :].rearrange("p (c h r) -> p h c r", c=C, h=H),
                                      AX.XY, ALU.add).then_inc(s["used"], 1)

                for t in range(NT):
                    if t == NT - 1:
                        dve.wait_ge(s["lin"], NT)
                        dve.tensor_copy(rows[:, :, XW:lay.XR],
                                        ps_l[0:T, 0:NT * H].rearrange("p (t h) -> p t h", h=H)).then_inc(s["rows"], 1)
                    reduce(t)
                dve.wait_ge(s["used"], 2 * NT)
                dve.tensor_tensor(lay.self_logit[:].rearrange("p t h -> p (t h)"),
                                  lay.self_logit[:].rearrange("p t h -> p (t h)"),
                                  ps_l[0:T, 0:NT * H], ALU.add).then_inc(s["used"], 1)


            @block.tensor
            def _(pe):
                def turn(t):
                    if t >= 2:
                        pe.wait_ge(s["xT_copied"], t - 1)
                    pe.transpose(ps_t[t % 2][:, 0:T], xx[:, t, :], k.ident[0:T, 0:T]).then_inc(s["xT"], 1)

                pe.wait_ge(s["dve"], 1)
                pe.wait_ge(s["xx"], 1)
                turn(0)
                for t in range(NT):
                    if t + 1 < NT:
                        turn(t + 1)
                    pe.wait_ge(s["xT_copied"], t + 1)
                    if t == 0:
                        pe.wait_ge(s["dve"], C + 6)
                    if t >= 2:
                        pe.wait_ge(s["relu"], t - 1)
                    pe.matmul(ps_z[t % 2][0:T, 0:H * D], xxT[t % 3][:], lay.w_abs[:],
                              start=True, stop=True).then_inc(s["z"], 1)
                    pe.matmul(ps_l[0:T, t * H:(t + 1) * H], xxT[t % 3][0:D, :], lay.w_lin[0:D, :],
                              start=True, stop=True).then_inc(s["lin"], 1)

            @block.scalar
            def _(act):
                def copy_xT(t):
                    act.wait_ge(s["xT"], t + 1)
                    if t >= 3:
                        act.wait_ge(s["lin"], t - 2)
                    act.activation(xxT[t % 3][:], ps_t[t % 2][:, 0:T], ACT.Copy).then_inc(s["xT_copied"], 1)

                act.activation(xx[:, :, D:2 * D], lay.x_node[:], ACT.Copy).then_inc(s["xx"], 1)
                act.activation(rows[:, :, 0:D], lay.x_node[:], ACT.Copy).then_inc(s["rows"], 1)
                copy_xT(0)
                for t in range(NT):
                    if t + 1 < NT:
                        copy_xT(t + 1)
                    act.wait_ge(s["z"], t + 1)
                    if t >= 2:
                        act.wait_ge(s["used"], 2 * t - 2)
                    act.activation(rel[:, t % 2, :], ps_z[t % 2][0:T, 0:H * D], ACT.Relu,
                                   scale=1.0 - SLOPE).then_inc(s["relu"], 1)
                act.wait_ge(s["rows"], 3)
                act.dma_start(lay.table.rearrange("(p t) f -> p t f", t=NT), rows[:]).then_inc(s["table"], 16)
                act.wait_ge(s["table"], 16)


def edge_logits(nc, k, lay):
    H, C = lay.H, lay.C
    NE = 6
    with ExitStack() as ctx:
        ph, nm = "a_", lay.nm + "a_"
        idx = [sbuf(nc, ctx, f"{nm}idx{r}", [T, Q], I32) for r in range(R)]
        xs = [sbuf(nc, ctx, f"{nm}xs{r}", [T, Q, lay.XR]) for r in range(R)]
        xw = [sbuf(nc, ctx, f"{nm}xw{r}", [128, D]) for r in range(R)]
        ident = sbuf(nc, ctx, nm + "ident", [T, T], BF16)
        oh = [sbuf(nc, ctx, f"{nm}oh{r}", [T, Q, WN], BF16) for r in range(R)]
        ohT = [sbuf(nc, ctx, f"{nm}ohT{r}", [128, Q, T]) for r in range(R)]
        xT = [sbuf(nc, ctx, f"{nm}xT{r}", [128, QT]) for r in range(R)]
        rl = [sbuf(nc, ctx, f"{nm}rl{r}", [128, QT]) for r in range(NE)]
        f = [sbuf(nc, ctx, f"{nm}f{r}", [128, QT]) for r in range(R)]
        lg = [sbuf(nc, ctx, f"{nm}lg{r}", [128, T]) for r in range(R)]
        ps_oh = psum(nc, ctx, nm + "ps_oh")
        ps_x = [psum(nc, ctx, f"{nm}ps_x{r}") for r in range(R)]
        ps_z = [psum(nc, ctx, f"{nm}ps_z{r}") for r in range(R)]
        ps_l = psum(nc, ctx, nm + "ps_l")
        s = {n: semaphore(nc, k, ph + n) for n in (
            "zeros", "idx_staged", "pool_step", "act_step", "src_read", "lin_read", "oh_ready", "oh_turned", "ohT_ready", "x_ready",
            "xT_ready", "z_ready", "relu_done", "combined", "logit_ready", "logit_copied")}
        gath = [semaphore(nc, k, f"{nm}gath{r}") for r in range(R)]
        spill = [semaphore(nc, k, f"{ph}spill{r}") for r in range(R)]
        lgst = [semaphore(nc, k, f"{ph}lgst{r}") for r in range(R)]
        xwld = [semaphore(nc, k, f"{ph}xwld{r}") for r in range(R)]
        GB = 16 * Q
        LR = 128 // Q

        with nc.Block() as block:
            @block.gpsimd
            def _(pool):
                def body(i, first, last):
                    for r in range(R):
                        u = i * R + r
                        if not first:
                            pool.wait_ge(s["src_read"], u - R + 1)
                            pool.sem_inc(s["pool_step"], 1)
                            pool.wait_ge(s["lin_read"], u - R + 1)
                            pool.sem_inc(s["pool_step"], 1)
                            pool.wait_ge(spill[r], 16 * i)
                            pool.sem_inc(s["pool_step"], 1)
                        pool.wait_ge(s["idx_staged"], u + 1)
                        pool.sem_inc(s["pool_step"], 1)
                        for j in range(Q):
                            pool.indirect_dma_start(xs[r][:, j, :], None, lay.table,
                                                    bass.IndirectOffsetOnAxis(idx[r][:, j:j + 1], 0)).then_inc(gath[r], 16)
                loop3(pool, body)

            @block.sync
            def _(sp):
                def load_windows(u, r):
                    sp.dma_start(xw[r][:], k.xw_d[bass.ds(u * Q, Q), :].rearrange("w (n d) -> (w n) d", d=D)).then_inc(xwld[r], 16)

                def store_logits(u, r):
                    sp.wait_ge(s["logit_copied"], u + 1)
                    for j in range(Q):
                        sp.dma_start(lay.logit_d[:, bass.ds(u * QT + j * T, T)],
                                     lg[r][LR * j:LR * j + H, :]).then_inc(lgst[r], 16)

                sp.wait_ge(lay.win_out[0], 16 * BG)
                load_windows(0, 0)
                load_windows(1, 1)

                def body(i, first, last):
                    for r in range(R):
                        u = i * R + r
                        if not (last and r >= R - 2):
                            if not (first and r == 0):
                                sp.wait_ge(s["x_ready"], u)
                            load_windows(u + 2, (r + 2) % R)
                        sp.wait_ge(gath[r], GB * (i + 1))
                        sp.dma_start(lay.xs_d[bass.ds(u, 1), :, :].rearrange("u p f -> (u p) f"),
                                     xs[r][:].rearrange("p j f -> p (j f)")).then_inc(spill[r], 16)
                        if not (first and r < 2):
                            store_logits(u - 2, (r + R - 2) % R)
                        if first:
                            for b in range(BG + r, NB, R):
                                sp.wait_ge(lay.win_in[b // BG], 16 * BG)
                                sp.dma_start(k.xw_d[b * BLK:(b + 1) * BLK, :],
                                             lay.win[b % (2 * BG)][:]).then_inc(lay.win_out[b // BG], 16)
                    if not first:
                        for g in range(1, NB // BG):
                            sp.wait_ge(lay.win_out[g], 16 * BG)
                    if last:
                        store_logits(U - 2, R - 2)
                        store_logits(U - 1, R - 1)
                loop3(sp, body)
                for r in range(R):
                    sp.wait_ge(spill[r], 16 * (U // R))
                    sp.wait_ge(lgst[r], GB * (U // R))
                sp.wait_ge(lay.lim_loaded, 16 * (CH // H))

            @block.tensor
            def _(pe):
                def turn(u, r, uses, free):
                    pe.wait_ge(s["oh_ready"], u + 1)
                    if free:
                        pe.wait_ge(s["xT_ready"], u - R + 1)
                    if free is not None:
                        pe.wait_ge(s["ohT_ready"], u)
                    pe.wait_ge(gath[r], GB * uses)
                    pe.matmul(ps_oh[:, 0:T], oh[r][:].rearrange("p j n -> p (j n)"), ident[:],
                              start=True, stop=True).then_inc(s["oh_turned"], 1)
                    for j in range(Q):
                        ins = pe.transpose(ps_x[r][0:D, j * T:(j + 1) * T], xs[r][:, j, 0:D], k.ident[0:T, 0:T])
                    ins.then_inc(s["src_read"], 1)

                def spread(u, r, uses):
                    pe.wait_ge(s["ohT_ready"], u + 1)
                    pe.wait_ge(xwld[r], 16 * uses)
                    pe.matmul(ps_x[r][D:128, 0:QT], xw[r][:], ohT[r][:].rearrange("p j e -> p (j e)"),
                              start=True, stop=True).then_inc(s["x_ready"], 1)

                def project(i, r, first, cs):
                    u = i * R + r
                    for c in cs:
                        b = (C * r + c) % R
                        if c == 0:
                            pe.wait_ge(s["xT_ready"], u + 1)
                        if not (first and C * r + c < R):
                            pe.wait_ge(s["relu_done"], C * u + c - R + 1)
                        pe.matmul(ps_z[b][:, 0:QT], lay.w_abs[:, c * 128:(c + 1) * 128], xT[r][:],
                                  start=True, stop=True).then_inc(s["z_ready"], 1)

                def reduce(u, r, free):
                    if free:
                        pe.wait_ge(s["logit_copied"], u)
                    pe.wait_ge(s["combined"], (C - 1) * (u + 1))
                    for j in range(Q):
                        ins = pe.matmul(ps_l[LR * j:LR * j + LR, 0:T], lay.sign_sum[:], f[r][:, j * T:(j + 1) * T],
                                        start=True, stop=True)
                    ins.then_inc(s["logit_ready"], 1)

                pe.wait_ge(s["zeros"], R + 1)
                turn(0, 0, 1, None)
                spread(0, 0, 1)

                def body(i, first, last):
                    for r in range(R):
                        u = i * R + r
                        n = (r + 1) % R
                        more = not (last and r == R - 1)
                        if more:
                            turn(u + 1, n, i + 1 + (n == 0), not (first and n != 0))
                        project(i, r, first, range(0, C - 1))
                        if more:
                            spread(u + 1, n, i + 1 + (n == 0))
                        project(i, r, first, range(C - 1, C))
                        if not (first and r == 0):
                            reduce(u - 1, (r + R - 1) % R, not (first and r == 1))
                loop3(pe, body)
                reduce(U - 1, R - 1, True)

            @block.scalar
            def _(act):
                def copy_logit(u, r, i, free):
                    act.wait_ge(s["logit_ready"], u + 1)
                    if free:
                        act.wait_ge(lgst[r], GB * i)
                    act.activation(lg[r][:], ps_l[:, 0:T], ACT.Copy).then_inc(s["logit_copied"], 1)

                def stage(u, r):
                    act.activation(idx[r][:], k.src_idx[:, bass.ds(u * Q, Q)], ACT.Copy).then_inc(s["idx_staged"], 1)

                for r in range(R):
                    stage(r, r)

                def body(i, first, second, last=False):
                    for r in range(R):
                        u = i * R + r
                        act.wait_ge(gath[r], GB * (i + 1))
                        act.sem_inc(s["act_step"], 1)
                        if not last:
                            stage(u + R, r)
                        act.activation(lay.lin_edge[:, bass.ds(u * Q, Q), :], xs[r][:, :, XW:lay.XR],
                                       ACT.Copy).then_inc(s["lin_read"], 1)
                        for c in range(C):
                            m = C * r + c
                            act.wait_ge(s["z_ready"], C * u + c + 1)
                            back = m - NE
                            br, bc = back // C, back % C
                            if not (first and back < 0):
                                act.wait_ge(s["combined"], (C - 1) * (i * R + br) + max(bc, 1))
                            act.activation(rl[m % NE][:], ps_z[m % R][:, 0:QT], ACT.Relu,
                                           scale=1.0 - SLOPE).then_inc(s["relu_done"], 1)
                        if not (first and r == 0):
                            copy_logit(u - 1, (r + R - 1) % R, i - (r == 0), not (first or second and r == 0))
                body(0, True, False)
                body(1, False, True)
                with act.Fori(2, U // R - 1) as i:
                    body(i, False, False)
                body(U // R - 1, False, False, True)
                copy_logit(U - 1, R - 1, U // R - 1, True)

            @block.vector
            def _(dve):
                def one_hot(u, r, free):
                    if free:
                        dve.wait_ge(s["oh_turned"], u - R + 1)
                    dve.tensor_tensor(oh[r][:], k.dst_local[:, bass.ds(u * Q, Q)].unsqueeze(2).to_broadcast([T, Q, WN]),
                                      k.node_in_window[:].unsqueeze(1).to_broadcast([T, Q, WN]),
                                      ALU.is_equal).then_inc(s["oh_ready"], 1)

                def copy_ohT(u, r, free):
                    dve.wait_ge(s["oh_turned"], u + 1)
                    if free:
                        dve.wait_ge(s["x_ready"], u - R + 1)
                    for j in range(Q):
                        p = slice(WN * j, WN * j + WN)
                        ins = dve.tensor_copy(ohT[r][p, j, :], ps_oh[p, 0:T])
                    ins.then_inc(s["ohT_ready"], 1)

                def copy_xT(u, r, free):
                    dve.wait_ge(s["x_ready"], u + 1)
                    if free:
                        dve.wait_ge(s["z_ready"], C * (u - R + 1))
                    dve.tensor_copy(xT[r][:], ps_x[r][:, 0:QT]).then_inc(s["xT_ready"], 1)

                def combine(i, r, first, c):
                    u = i * R + r
                    dve.wait_ge(s["relu_done"], C * u + c + 1)
                    if c == 1 and not first:
                        dve.wait_ge(s["logit_ready"], u - R + 1)
                    if c > 1:
                        dve.wait_ge(s["combined"], (C - 1) * u + c - 1)
                    dve.scalar_tensor_tensor(out=f[r][:], in0=rl[(C * r + c) % NE][:], scalar=lay.sign[:, c:c + 1],
                                             in1=rl[(C * r) % NE][:] if c == 1 else f[r][:],
                                             op0=ALU.mult, op1=ALU.add).then_inc(s["combined"], 1)

                for r in range(R):
                    dve.memset(ohT[r][:], 0.0).then_inc(s["zeros"], 1)
                dve.tensor_copy(ident[:], k.ident[0:T, 0:T]).then_inc(s["zeros"], 1)
                dve.wait_ge(s["zeros"], R + 1)
                one_hot(0, 0, False)
                one_hot(1, 1, False)
                copy_ohT(0, 0, False)
                copy_xT(0, 0, False)

                def body(i, first, last):
                    for r in range(R):
                        u = i * R + r
                        more = not (last and r == R - 1)
                        free = not (first and r + 1 < R)
                        if more:
                            copy_ohT(u + 1, (r + 1) % R, free)
                        if not (last and r >= R - 2):
                            one_hot(u + 2, (r + 2) % R, not (first and r + 2 < R))
                        combine(i, r, first, 1)
                        if more:
                            copy_xT(u + 1, (r + 1) % R, free)
                        for c in range(2, C):
                            combine(i, r, first, c)
                loop3(dve, body)


def edge_softmax(nc, k, lay):
    H = lay.H
    NC = CH // H
    F = SLOTS // NC
    TPC = F // T
    lay.stat_d = nc.dram_tensor(lay.nm + "stat_d", [NC, H, 4], F32, kind="Internal").ap()
    lay.carry_d = nc.dram_tensor(lay.nm + "carry_d", [NC, H, 2], F32, kind="Internal").ap()
    with ExitStack() as tmp:
        ph, nm = "s_", lay.nm + "s_"
        lim = lay.lim
        lg = sbuf(nc, tmp, nm + "lg", [CH, F])
        fw = sbuf(nc, tmp, nm + "fw", [CH, F])
        bw = sbuf(nc, tmp, nm + "bw", [CH, F])
        stat = sbuf(nc, tmp, nm + "stat", [CH, 4])
        stat_h = sbuf(nc, tmp, nm + "stat_h", [H, NC, 4])
        run = sbuf(nc, tmp, nm + "run", [H, 2, NC])
        carry_h = sbuf(nc, tmp, nm + "carry_h", [H, NC, 2])
        carry = sbuf(nc, tmp, nm + "carry", [CH, 2])
        ps = [psum(nc, tmp, f"{nm}ps{i}") for i in range(4)]
        s = {n: semaphore(nc, k, ph + n) for n in (
            "load_lg", "bounce", "dve", "exp", "lin_laid", "lin_turned", "lin_added", "less", "turned", "act_copied", "dve_copied")}
        lin = lay.m_edge[:].rearrange("p s h -> p (s h)").rearrange("p (t v) -> p t v", v=CH)
        GRP = 4
        LG = -(-TPC // GRP)
        CUT = LG // 2
        order = [*range(CUT, LG), *range(CUT)]
        EARLY = 2 * (LG - CUT)
        cut = CUT * GRP * T
        halves = [(cut, F), (0, cut)]
        parts = [(a + y * (b - a) // 2, a + (y + 1) * (b - a) // 2) for a, b in halves for y in range(2)]

        def place(edge, g):
            return edge[:].rearrange("p (c t) h -> p t c h", c=NC)[:, g * GRP:min((g + 1) * GRP, TPC), :, :]

        def bank(n, g):
            return ps[n % 4][0:T, 0:min(GRP, TPC - g * GRP) * CH].rearrange("p (q c h) -> p q c h", c=NC, h=H)

        with nc.Block() as block:
            @block.sync
            def _(sp):
                ld = Dma(sp, s["load_lg"])
                for c in range(NC):
                    ld.start(lg[c * H:(c + 1) * H, :], lay.logit_d[:, c * F:(c + 1) * F])
                bo = Dma(sp, s["bounce"])
                sp.wait_ge(s["dve"], 7)
                bo.start(lay.stat_d.rearrange("c h v -> (c h) v"), stat[:])
                bo.wait()
                bo.start(stat_h[:], lay.stat_d.rearrange("c h v -> h c v"))
                bo.wait()
                sp.wait_ge(s["dve"], 13)
                bo.start(lay.carry_d.rearrange("c h v -> h c v"), carry_h[:])
                bo.wait()
                bo.start(carry[:], lay.carry_d.rearrange("c h v -> (c h) v"))
                bo.wait()

            @block.vector
            def _(dve):
                link = Link(dve, s["dve"])
                link(dve.tensor_reduce(stat[:, 3:4], lim[:, 1:F], AX.X, ALU.min))
                link(dve.tensor_tensor(stat[:, 1:2], stat[:, 3:4], lim[:, 0:1], ALU.min))
                link(dve.tensor_tensor(stat[:, 3:4], stat[:, 3:4], lim[:, F:F + 1], ALU.min))
                dve.wait_ge(s["load_lg"], 16 * NC)
                for g in range(LG):
                    c = slice(g * GRP * T, min((g + 1) * GRP, TPC) * T)
                    dve.wait_ge(s["lin_turned"], g + 1)
                    dve.tensor_tensor(lg[:, c], lg[:, c], ps[g % 4][0:CH, 0:c.stop - c.start],
                                      ALU.add).then_inc(s["lin_added"], 1)
                dve.wait_ge(s["lin_added"], LG)
                link(dve.tensor_tensor_scan(fw[:], lim[:, 0:F], lg[:], -BIG, ALU.min, ALU.max))
                link(dve.tensor_tensor_scan(bw[:, ::-1], lim[:, 1:F + 1][:, ::-1], lg[:, ::-1], -BIG,
                                            ALU.min, ALU.max))
                link(dve.tensor_copy(stat[:, 0:1], fw[:, F - 1:F]))
                link(dve.tensor_copy(stat[:, 2:3], bw[:, 0:1]))
                dve.wait_ge(s["bounce"], 32)
                link(dve.tensor_tensor_scan(run[:, 0, :], stat_h[:, :, 1], stat_h[:, :, 0], -BIG, ALU.min, ALU.max))
                link(dve.tensor_tensor_scan(run[:, 1, ::-1], stat_h[:, ::-1, 3], stat_h[:, ::-1, 2], -BIG,
                                            ALU.min, ALU.max))
                link(dve.memset(carry_h[:, 0, 0:1], -BIG))
                link(dve.memset(carry_h[:, NC - 1, 1:2], -BIG))
                link(dve.tensor_copy(carry_h[:, 1:NC, 0], run[:, 0, 0:NC - 1]))
                link(dve.tensor_copy(carry_h[:, 0:NC - 1, 1], run[:, 1, 1:NC]))
                dve.wait_ge(s["bounce"], 64)
                link(dve.tensor_tensor_scan(fw[:], lim[:, 0:F], lg[:], carry[:, 0:1], ALU.min, ALU.max))
                for n, (a, b) in enumerate(halves):
                    link(dve.tensor_tensor_scan(bw[:, a:b][:, ::-1], lim[:, a + 1:b + 1][:, ::-1], fw[:, a:b][:, ::-1],
                                                carry[:, 1:2] if n == 0 else bw[:, cut:cut + 1], ALU.min, ALU.max))
                    for c0, c1 in parts[2 * n:2 * n + 2]:
                        dve.tensor_tensor(lg[:, c0:c1], lg[:, c0:c1], bw[:, c0:c1], ALU.subtract).then_inc(s["less"], 1)
                for n in range(EARLY + 1, 2 * LG, 2):
                    dve.wait_ge(s["turned"], n + 1)
                    dve.tensor_copy(place(lay.a_edge, order[n // 2]), bank(n, order[n // 2])).then_inc(s["dve_copied"], 1)

            @block.scalar
            def _(act):
                act.activation(lin.rearrange("p t (c h) -> p t c h", h=H),
                               lay.lin_edge[:].rearrange("p (c t) h -> p t c h", c=NC), ACT.Copy).then_inc(s["lin_laid"], 1)

                def exponentials(x):
                    c0, c1 = parts[x]
                    act.wait_ge(s["less"], x + 1)
                    act.activation(lg[:, c0:c1], lg[:, c0:c1], ACT.Exp).then_inc(s["exp"], 1)

                def leave(n):
                    act.wait_ge(s["turned"], n + 1)
                    act.activation(place(lay.a_edge if n % 2 else lay.m_edge, order[n // 2]), bank(n, order[n // 2]),
                                   ACT.Copy).then_inc(s["act_copied"], 1)

                act.wait_ge(s["lin_turned"], LG)
                exponentials(0)
                exponentials(1)
                for n in range(EARLY):
                    leave(n)
                exponentials(2)
                exponentials(3)
                for n in range(EARLY, 2 * LG, 2):
                    leave(n)

            @block.tensor
            def _(pe):
                pe.wait_ge(s["lin_laid"], 1)
                for g in range(LG):
                    if g >= 4:
                        pe.wait_ge(s["lin_added"], g - 3)
                    for q in range(min(GRP, TPC - g * GRP)):
                        ins = pe.transpose(ps[g % 4][0:CH, q * T:(q + 1) * T], lin[:, g * GRP + q, :],
                                           k.ident[0:T, 0:T])
                    ins.then_inc(s["lin_turned"], 1)
                pe.wait_ge(s["lin_added"], LG)
                for n in range(2 * LG):
                    g = order[n // 2]
                    if n in (0, EARLY):
                        pe.wait_ge(s["dve"], 15 + n // EARLY)
                    if n % 2:
                        end = min((g + 1) * GRP * T, F)
                        x = 0 if n < EARLY else 2
                        pe.wait_ge(s["exp"], x + (1 if end <= parts[x][1] else 2))
                    if n >= 4:
                        m = n - 4
                        if m < EARLY:
                            pe.wait_ge(s["act_copied"], m + 1)
                        elif m % 2 == 0:
                            pe.wait_ge(s["act_copied"], EARLY + (m - EARLY) // 2 + 1)
                        else:
                            pe.wait_ge(s["dve_copied"], (m - EARLY) // 2 + 1)
                    for q in range(min(GRP, TPC - g * GRP)):
                        t = g * GRP + q
                        ins = pe.transpose(ps[n % 4][0:T, q * CH:(q + 1) * CH], (lg if n % 2 else bw)[:, t * T:(t + 1) * T],
                                           k.ident[0:CH, 0:CH])
                    ins.then_inc(s["turned"], 1)


def edge_sums(nc, k, lay):
    H = lay.H
    P = WN * H
    HV = P // 128
    VJ = 1
    OJ = Q // 2
    with ExitStack() as ctx:
        ph, nm = "b_", lay.nm + "b_"
        xs = [sbuf(nc, ctx, f"{nm}xs{r}", [T, Q, lay.XR]) for r in range(R)]
        oh = [sbuf(nc, ctx, f"{nm}oh{r}", [T, Q, WN]) for r in range(R)]
        p = [sbuf(nc, ctx, f"{nm}p{r}", [T, Q, P]) for r in range(R)]
        same = [sbuf(nc, ctx, f"{nm}same{r}", [128, Q]) for r in range(R)]
        dst = [sbuf(nc, ctx, f"{nm}dst{r}", [T, Q]) for r in range(R)]
        ae = [sbuf(nc, ctx, f"{nm}ae{r}", [T, Q, H]) for r in range(R)]
        acc = [sbuf(nc, ctx, f"{nm}acc{r}", [XW, Q, P]) for r in range(R)]
        rows = [sbuf(nc, ctx, f"{nm}rows{r}", [128, Q, HV * XW]) for r in range(R)]
        ps_v = [psum(nc, ctx, f"{nm}ps_v{j}") for j in range(Q)]
        ps_r = [psum(nc, ctx, f"{nm}ps_r{j}") for j in range(Q)]
        s = {n: semaphore(nc, k, ph + n) for n in (
            "zero", "oh_ready", "p_ready", "p_last", "staged", "v_ready", "chain", "turned", "copied", "pool_step", "pe_step")}
        s["max_stored"] = semaphore(nc, k, nm + "max_stored")
        s["max_gathered"] = semaphore(nc, k, nm + "max_gathered")
        load = [semaphore(nc, k, f"{ph}load{r}") for r in range(R)]
        store = [semaphore(nc, k, f"{ph}store{r}") for r in range(R)]

        def weights(eng, r, j):
            return eng.tensor_tensor(p[r][:, j, :].rearrange("p (n h) -> p n h", h=H),
                                     oh[r][:, j, :].unsqueeze(2).to_broadcast([T, WN, H]),
                                     ae[r][:, j, :].unsqueeze(1).to_broadcast([T, WN, H]), ALU.mult)

        with nc.Block() as block:
            @block.sync
            def _(sp):
                def body(i, first, last):
                    for r in range(R):
                        u = i * R + r
                        if not first:
                            sp.wait_ge(s["v_ready"], Q * (u - R + 1))
                        sp.dma_start(xs[r][:].rearrange("p j f -> p (j f)"),
                                     lay.xs_d[bass.ds(u, 1), :, :].rearrange("u p f -> (u p) f")).then_inc(load[r], 16)
                loop3(sp, body)

            @block.gpsimd
            def _(pool):
                pool.dma_start(lay.max_d.rearrange("(e u) h -> e (u h)", u=UT),
                               lay.m_edge[:].rearrange("e u h -> e (u h)")).then_inc(s["max_stored"], 16)

                def body(i, first, gathers):
                    for r in range(R):
                        u = i * R + r
                        if not first:
                            pool.wait_ge(s["v_ready"], Q * (u - R + 1))
                            pool.sem_inc(s["pool_step"], 1)
                        pool.wait_ge(s["oh_ready"], u + 1)
                        pool.sem_inc(s["pool_step"], 1)
                        for j in range(VJ, Q):
                            weights(pool, r, j).then_inc(s["p_last"], 1)
                        for t in gathers[r:r + 1]:
                            pool.indirect_dma_start(lay.node_max[:, t, :], None, lay.max_d,
                                                    bass.IndirectOffsetOnAxis(k.max_idx[:, t:t + 1], 0)).then_inc(s["max_gathered"], 16)

                body(0, True, [])
                pool.wait_ge(s["max_stored"], 16)
                rounds = -(-NT // R)
                for i in range(1, rounds + 1):
                    body(i, False, list(range(NT))[(i - 1) * R:i * R])
                with pool.Fori(rounds + 1, U // R) as i:
                    body(i, False, [])
                pool.wait_ge(s["max_gathered"], 16 * NT)

            @block.vector
            def _(dve):
                dve.memset(acc[R - 1][:, Q - 1, :], 0.0).then_inc(s["zero"], 1)

                def one_hot(u, r):
                    dve.wait_ge(s["staged"], 3 * u + 3)
                    dve.tensor_tensor(oh[r][:], dst[r][:].unsqueeze(2).to_broadcast([T, Q, WN]),
                                      k.node_in_window[:].unsqueeze(1).to_broadcast([T, Q, WN]),
                                      ALU.is_equal).then_inc(s["oh_ready"], 1)

                def weigh(u, r, j):
                    if j == 0:
                        dve.wait_ge(s["oh_ready"], u + 1)
                    weights(dve, r, j).then_inc(s["p_ready"], 1)

                def run(u, r, j, start):
                    if start:
                        dve.wait_ge(s["zero"], 1)
                    else:
                        dve.wait_ge(s["chain"], Q * u + j)
                    prev = acc[r][:, j - 1, :] if j else acc[(r + R - 1) % R][:, Q - 1, :]
                    dve.scalar_tensor_tensor(out=acc[r][:, j, :], in0=prev, scalar=same[r][0:XW, j:j + 1],
                                             in1=ps_v[j][0:XW, 0:P], op0=ALU.mult,
                                             op1=ALU.add).then_inc(s["chain"], 1)

                one_hot(0, 0)
                for j in range(VJ):
                    weigh(0, 0, j)
                one_hot(1, 1)
                dve.wait_ge(s["v_ready"], 1)

                def body(i, first, last):
                    for r in range(R):
                        u = i * R + r
                        if not first:
                            dve.wait_ge(s["turned"], Q * (u - R + 1))
                        for j in range(Q):
                            run(u, r, j, first and r == 0 and j == 0)
                            if not (last and r == R - 1 and j == Q - 1):
                                dve.wait_ge(s["v_ready"], Q * u + j + 2)
                            if j < VJ:
                                if not (last and r == R - 1):
                                    weigh(u + 1, (r + 1) % R, j)
                            if j == OJ and not (last and r >= R - 2):
                                one_hot(u + 2, (r + 2) % R)
                loop3(dve, body)

            @block.tensor
            def _(pe):
                def turn(u, r, j, free):
                    pe.wait_ge(s["chain"], Q * u + j + 1)
                    if free:
                        pe.wait_ge(s["copied"], Q * (u - 1) + j + 1)
                    pe.sem_inc(s["pe_step"], 1)
                    for v in range(HV):
                        ins = pe.transpose(ps_r[j][:, v * XW:(v + 1) * XW], acc[r][:, j, v * 128:(v + 1) * 128],
                                           k.ident[0:XW, 0:XW])
                    ins.then_inc(s["turned"], 1)

                def body(i, first, last):
                    for r in range(R):
                        u = i * R + r
                        pe.wait_ge(load[r], 16 * (i + 1))
                        for j in range(Q):
                            if j < VJ:
                                pe.wait_ge(s["p_ready"], VJ * u + j + 1)
                            else:
                                pe.wait_ge(s["p_last"], (Q - VJ) * u + j - VJ + 1)
                            if not (first and r == 0):
                                pe.wait_ge(s["chain"], Q * (u - 1) + j + 1)
                            pe.matmul(ps_v[j][0:XW, 0:P], xs[r][:, j, 0:XW], p[r][:, j, :],
                                      start=True, stop=True).then_inc(s["v_ready"], 1)
                            if not (first and r == 0):
                                turn(u - 1, (r + R - 1) % R, j, not (first and r == 1))
                loop3(pe, body)
                for j in range(Q):
                    turn(U - 1, R - 1, j, True)

            @block.scalar
            def _(act):
                def stage(u, r):
                    act.activation(same[r][:], k.same[:, bass.ds(u * Q, Q)], ACT.Copy).then_inc(s["staged"], 1)
                    act.activation(dst[r][:], k.dst_local[:, bass.ds(u * Q, Q)], ACT.Copy).then_inc(s["staged"], 1)
                    act.activation(ae[r][:], lay.a_edge[:, bass.ds(u * Q, Q), :], ACT.Copy).then_inc(s["staged"], 1)

                for r in range(R):
                    stage(r, r)

                def body(i, first, last):
                    for r in range(R):
                        u = i * R + r
                        if not first:
                            act.wait_ge(store[r], 16 * i)
                        for j in range(Q):
                            act.wait_ge(s["turned"], Q * u + j + 1)
                            act.activation(rows[r][:, j, :], ps_r[j][:, 0:HV * XW], ACT.Copy).then_inc(s["copied"], 1)
                        if not last:
                            stage(u + R, r)
                        act.wait_ge(s["copied"], Q * u + Q)
                        act.dma_start(bass.AP(lay.v_d.tensor, u * (Q * WN * H * XW),
                                              [[XW, 128], [WN * H * XW, Q], [128 * XW, HV], [1, XW]]),
                                      rows[r][:].rearrange("p j (v f) -> p j v f", v=HV)).then_inc(store[r], 16)
                loop3(act, body)
                for r in range(R):
                    act.wait_ge(store[r], 16 * (U // R))


def merge_nodes(nc, k, lay, finish):
    H = lay.H
    CK = H // 2
    with ExitStack() as tmp:
        ph, nm = "n_", lay.nm + "n_"
        v = sbuf(nc, tmp, nm + "v", [T, NT, H * XW])
        m = lay.node_max
        den = sbuf(nc, tmp, nm + "den", [T, NT, H])
        me = sbuf(nc, tmp, nm + "me", [T, NT, H])
        be = sbuf(nc, tmp, nm + "be", [T, NT, H])
        ga = sbuf(nc, tmp, nm + "ga", [T, NT, H])
        agg = sbuf(nc, tmp, nm + "agg", [T, NT, H, D])
        selfx = [sbuf(nc, tmp, f"{nm}selfx{i}", [T, TG, H, D]) for i in range(2)]
        aggT = [sbuf(nc, tmp, f"{nm}aggT{i}", [128, CK * T]) for i in range(2)]
        wl = sbuf(nc, tmp, nm + "wl", [128, CK, D])
        bias = sbuf(nc, tmp, nm + "bias", [D, 1])
        oT = [sbuf(nc, tmp, f"{nm}oT{i}", [D, T]) for i in range(2)]
        o = sbuf(nc, tmp, nm + "o", [T, NT, D])
        ps_t = [psum(nc, tmp, f"{nm}ps_t{i}") for i in range(2)]
        ps_o = [psum(nc, tmp, f"{nm}ps_o{i}") for i in range(2)]
        ps_b = [psum(nc, tmp, f"{nm}ps_b{i}") for i in range(2)]
        s = {n: semaphore(nc, k, ph + n) for n in (
            "load", "coef", "weighted", "exp", "selfx", "agg", "turned", "copied", "proj", "mean", "back", "out", "fin", "finb", "store")}
        gather = [semaphore(nc, k, f"{nm}gather{g}") for g in range(NT // TG)]
        COEF = 10
        with nc.Block() as block:
            @block.gpsimd
            def _(pool):
                def rows_of(g):
                    for t in range(g * TG, (g + 1) * TG):
                        pool.indirect_dma_start(v[:, t, :], None, lay.v_d,
                                                bass.IndirectOffsetOnAxis(k.row_idx[:, t:t + 1], 0)).then_inc(gather[g], 16)

                rows_of(0)
                for g in range(NT // TG):
                    if g + 1 < NT // TG:
                        rows_of(g + 1)
                    t = slice(g * TG, (g + 1) * TG)
                    pool.wait_ge(s["coef"], COEF * (g + 1))
                    if g >= 2:
                        pool.wait_ge(s["agg"], g - 1)
                    pool.tensor_tensor(selfx[g % 2][:], lay.x_node[:, t, :].unsqueeze(2).to_broadcast([T, TG, H, D]),
                                       ga[:, t, :].unsqueeze(3).to_broadcast([T, TG, H, D]), ALU.mult).then_inc(s["selfx"], 1)
                for g in range(NT // TG):
                    pool.wait_ge(gather[g], 16 * TG)

            @block.sync
            def _(sp):
                ld = Dma(sp, s["load"])
                wsrc = lay.Wl.rearrange("d (c b f) -> b d c f", b=2, f=D)
                for b in range(2):
                    ld.start(wl[b * D:(b + 1) * D, :, :], wsrc[b])
                ld.start(bias[:], lay.bias.unsqueeze(1), elements=True)
                ld.wait()

            @block.vector
            def _(dve):
                coef = Link(dve, s["coef"])
                weighted = Link(dve, s["weighted"])
                one = v[:].rearrange("p t (h f) -> p (t h) f", f=XW)
                th = lambda g: slice(g * TG * H, (g + 1) * TG * H)
                flat = lambda x, g: x[:].rearrange("p t h -> p (t h)")[:, th(g)]

                def maxima(g):
                    dve.wait_ge(gather[g], 16 * TG)
                    coef(dve.tensor_scalar(flat(me, g), one[:, th(g), D], 0.5, -2 * BIG, ALU.is_lt, ALU.mult))
                    coef(dve.tensor_tensor(flat(me, g), flat(me, g), flat(m, g), ALU.add))
                    coef(dve.tensor_tensor(flat(m, g), flat(me, g), flat(lay.self_logit, g), ALU.max))
                    coef(dve.tensor_tensor(flat(be, g), flat(me, g), flat(m, g), ALU.subtract))
                    coef(dve.tensor_tensor(flat(ga, g), flat(lay.self_logit, g), flat(m, g), ALU.subtract))

                def coefficients(g):
                    dve.wait_ge(s["exp"], 2 * g + 2)
                    coef(dve.tensor_tensor(flat(den, g), one[:, th(g), D], flat(be, g), ALU.mult))
                    coef(dve.tensor_tensor(flat(den, g), flat(den, g), flat(ga, g), ALU.add))
                    coef(dve.reciprocal(flat(den, g), flat(den, g)))
                    coef(dve.tensor_tensor(flat(be, g), flat(be, g), flat(den, g), ALU.mult))
                    coef(dve.tensor_tensor(flat(ga, g), flat(ga, g), flat(den, g), ALU.mult))

                def leave(g):
                    dve.wait_ge(s["back"], TG * (g + 1))
                    dve.tensor_copy(o[:, g * TG:(g + 1) * TG, :].rearrange("p t d -> p (t d)"),
                                    ps_b[g % 2][0:T, 0:TG * D]).then_inc(s["out"], 1)

                maxima(0)
                coefficients(0)
                for g in range(NT // TG):
                    ag = agg[:].rearrange("p t h f -> p (t h) f")[:, th(g), :]
                    weighted(dve.tensor_tensor(ag, one[:, th(g), 0:D],
                                               flat(be, g).unsqueeze(2).to_broadcast([T, TG * H, D]), ALU.mult))
                    if g + 1 < NT // TG:
                        maxima(g + 1)
                    dve.wait_ge(s["selfx"], g + 1)
                    dve.tensor_tensor(ag, ag, selfx[g % 2][:].rearrange("p t h f -> p (t h) f"), ALU.add).then_inc(s["agg"], 1)
                    if g + 1 < NT // TG:
                        coefficients(g + 1)
                    if g:
                        leave(g - 1)
                leave(NT // TG - 1)

            @block.scalar
            def _(act):
                def exponentials(g):
                    t = slice(g * TG, (g + 1) * TG)
                    act.wait_ge(s["coef"], COEF * g + 4)
                    act.activation(be[:, t, :], be[:, t, :], ACT.Exp).then_inc(s["exp"], 1)
                    act.wait_ge(s["coef"], COEF * g + 5)
                    act.activation(ga[:, t, :], ga[:, t, :], ACT.Exp).then_inc(s["exp"], 1)

                def mean(t):
                    act.wait_ge(s["proj"], t + 1)
                    if t >= 2:
                        act.wait_ge(s["back"], t - 1)
                    act.activation(oT[t % 2][:], ps_o[t % 2][0:D, 0:T], ACT.Identity, bias=bias[:, 0:1],
                                   scale=1.0 / H).then_inc(s["mean"], 1)

                act.wait_ge(s["load"], 48)
                exponentials(0)
                for t in range(NT):
                    if t % TG == 0 and t + TG < NT:
                        exponentials(t // TG + 1)
                    act.wait_ge(s["turned"], t + 1)
                    if t >= 2:
                        act.wait_ge(s["proj"], t - 1)
                    act.activation(aggT[t % 2][:], ps_t[t % 2][:, 0:CK * T], ACT.Copy).then_inc(s["copied"], 1)
                    if t:
                        mean(t - 1)
                mean(NT - 1)

            @block.tensor
            def _(pe):
                pe.wait_ge(s["load"], 48)

                def turn(t):
                    pe.wait_ge(s["agg"], t // TG + 1)
                    if t >= 2:
                        pe.wait_ge(s["copied"], t - 1)
                    for c in range(CK):
                        ins = pe.transpose(ps_t[t % 2][:, c * T:(c + 1) * T],
                                           agg[:, t, 2 * c:2 * c + 2, :].rearrange("p h f -> p (h f)"), k.ident[0:T, 0:T])
                    ins.then_inc(s["turned"], 1)

                def turn_back(t):
                    pe.wait_ge(s["mean"], t + 1)
                    g, i = t // TG, t % TG
                    if g >= 2:
                        pe.wait_ge(s["out"], g - 1)
                    pe.transpose(ps_b[g % 2][0:T, i * D:(i + 1) * D], oT[t % 2][:], k.ident[0:D, 0:D]).then_inc(s["back"], 1)

                turn(0)
                for t in range(NT):
                    if t + 1 < NT:
                        turn(t + 1)
                    pe.wait_ge(s["copied"], t + 1)
                    if t >= 2:
                        pe.wait_ge(s["mean"], t - 1)
                    for c in range(CK):
                        ins = pe.matmul(ps_o[t % 2][0:D, 0:T], wl[:, c, :], aggT[t % 2][:, c * T:(c + 1) * T],
                                        start=(c == 0), stop=(c == CK - 1))
                    ins.then_inc(s["proj"], 1)
                    if t:
                        turn_back(t - 1)
                turn_back(NT - 1)

        with nc.Block() as block:
            @block.vector
            def _(dve):
                finish(dve, Link(dve, s["fin"]), s["finb"], o)

            @block.scalar
            def _(act):
                if lay.norm:
                    act.wait_ge(s["fin"], 6)
                    act.activation(lay.std[:], lay.var[:], ACT.Sqrt).then_inc(s["finb"], 1)

            @block.sync
            def _(sp):
                sp.wait_ge(s["fin"], lay.fin_steps)
                sp.dma_start(lay.next_table.rearrange("(p t) d -> p t d", t=NT), lay.next_node[:]).then_inc(s["store"], 16)
                sp.wait_ge(s["store"], 16)


def layer_norm(dve, link, std_ready, n, x, y, sq, mean, var, std, out):
    bc = lambda v: v.unsqueeze(2).to_broadcast([T, out.shape[1], D])
    link(dve.tensor_tensor(out, x, y, ALU.add))
    link(dve.tensor_reduce(mean, out, AX.X, ALU.add))
    link(dve.tensor_scalar(mean, mean, 1.0 / D, None, ALU.mult))
    link(dve.tensor_tensor(out, out, bc(mean), ALU.subtract))
    dve.tensor_tensor(sq, out, out, ALU.mult).then_inc(std_ready, 1)
    dve.wait_ge(std_ready, 2 * n + 1)
    link(dve.tensor_reduce(var, sq, AX.X, ALU.add))
    link(dve.tensor_scalar(var, var, 1.0 / D, EPS, ALU.mult, ALU.add))
    dve.wait_ge(std_ready, 2 * n + 2)
    link(dve.reciprocal(std, std))
    link(dve.tensor_tensor(out, out, bc(std), ALU.mult))


def neighbour_sums(nc, k, table):
    GT = GQ * T
    with ExitStack() as ctx:
        nm = "g_"
        idx = [sbuf(nc, ctx, f"{nm}idx{r}", [T, GQ], I32) for r in range(GR)]
        xs = [sbuf(nc, ctx, f"{nm}xs{r}", [T, GQ, D]) for r in range(GR)]
        keep = [sbuf(nc, ctx, f"{nm}keep{r}", [D, GT]) for r in range(GR)]
        run = [sbuf(nc, ctx, f"{nm}run{r}", [D, GT]) for r in range(GR)]
        rows = [sbuf(nc, ctx, f"{nm}rows{r}", [T, GQ, D]) for r in range(GR)]
        start = sbuf(nc, ctx, nm + "start", [D, 1])
        ps_x = [psum(nc, ctx, f"{nm}ps_x{r}") for r in range(GR)]
        ps_r = [psum(nc, ctx, f"{nm}ps_r{r}") for r in range(GR)]
        s = {n: semaphore(nc, k, nm + n) for n in (
            "idx_staged", "pool_step", "pe_step", "act_step", "zero", "x_turned", "run_ready", "run_turned", "rows_ready")}
        gath = [semaphore(nc, k, f"{nm}gath{r}") for r in range(GR)]
        kept = [semaphore(nc, k, f"{nm}kept{r}") for r in range(GR)]
        store = [semaphore(nc, k, f"{nm}store{r}") for r in range(GR)]
        GB = 16 * GQ
        loop = lambda eng, body: peeled(eng, GU // GR, body)

        with nc.Block() as block:
            @block.gpsimd
            def _(pool):
                def body(i, first, last):
                    for r in range(GR):
                        u = i * GR + r
                        if not first:
                            pool.wait_ge(s["x_turned"], u - GR + 1)
                            pool.sem_inc(s["pool_step"], 1)
                        pool.wait_ge(s["idx_staged"], u + 1)
                        pool.sem_inc(s["pool_step"], 1)
                        for j in range(GQ):
                            pool.indirect_dma_start(xs[r][:, j, :], None, table,
                                                    bass.IndirectOffsetOnAxis(idx[r][:, j:j + 1], 0)).then_inc(gath[r], 16)
                loop(pool, body)

            @block.sync
            def _(sp):
                def body(i, first, last):
                    for r in range(GR):
                        u = i * GR + r
                        if not first:
                            sp.wait_ge(s["run_ready"], u - GR + 1)
                        sp.dma_start(keep[r][:], bass.AP(k.same_d.tensor, u * GT, [[0, D], [1, GT]])).then_inc(kept[r], 16)
                loop(sp, body)

            @block.tensor
            def _(pe):
                def turn_back(u, r, free):
                    pe.wait_ge(s["run_ready"], u + 1)
                    if free:
                        pe.wait_ge(s["rows_ready"], u - GR + 1)
                    pe.sem_inc(s["pe_step"], 1)
                    for j in range(GQ):
                        ins = pe.transpose(ps_r[r][0:T, j * D:(j + 1) * D], run[r][:, j * T:(j + 1) * T], k.ident[0:D, 0:D])
                    ins.then_inc(s["run_turned"], 1)

                def body(i, first, last):
                    for r in range(GR):
                        u = i * GR + r
                        if not first:
                            pe.wait_ge(s["run_ready"], u - GR + 1)
                        pe.wait_ge(gath[r], GB * (i + 1))
                        pe.sem_inc(s["pe_step"], 1)
                        for j in range(GQ):
                            ins = pe.transpose(ps_x[r][0:D, j * T:(j + 1) * T], xs[r][:, j, :], k.ident[0:T, 0:T])
                        ins.then_inc(s["x_turned"], 1)
                        if r:
                            turn_back(u - 1, r - 1, not first)
                    turn_back(i * GR + GR - 1, GR - 1, not first)
                loop(pe, body)

            @block.vector
            def _(dve):
                dve.memset(start[:], 0.0).then_inc(s["zero"], 1)

                def body(i, first, last):
                    for r in range(GR):
                        u = i * GR + r
                        dve.wait_ge(s["x_turned"], u + 1)
                        dve.wait_ge(kept[r], 16 * (i + 1))
                        if not first:
                            dve.wait_ge(s["run_turned"], u - GR + 1)
                        if first and r == 0:
                            dve.wait_ge(s["zero"], 1)
                        else:
                            dve.wait_ge(s["run_ready"], u)
                        before = start[:] if first and r == 0 else run[(r + GR - 1) % GR][:, GT - 1:GT]
                        dve.tensor_tensor_scan(run[r][:], keep[r][:], ps_x[r][0:D, 0:GT], before,
                                               ALU.mult, ALU.add).then_inc(s["run_ready"], 1)
                loop(dve, body)

            @block.scalar
            def _(act):
                def stage(u, r):
                    act.activation(idx[r][:], k.src_tile[:, bass.ds(u * GQ, GQ)], ACT.Copy).then_inc(s["idx_staged"], 1)

                def leave(u, r, stored):
                    act.wait_ge(s["run_turned"], u + 1)
                    if stored is not None:
                        act.wait_ge(store[r], stored)
                    act.activation(rows[r][:].rearrange("e j f -> e (j f)"), ps_r[r][0:T, 0:GQ * D],
                                   ACT.Copy).then_inc(s["rows_ready"], 1)
                    act.wait_ge(s["rows_ready"], u + 1)
                    act.dma_start(k.sum_d.rearrange("(e g) f -> e g f", g=G)[:, bass.ds(u * GQ, GQ), :],
                                  rows[r][:]).then_inc(store[r], 16)

                for r in range(GR):
                    stage(r, r)

                def body(i, first, last):
                    for r in range(GR):
                        u = i * GR + r
                        if not last:
                            act.wait_ge(gath[r], GB * (i + 1))
                            act.sem_inc(s["act_step"], 1)
                            stage(u + GR, r)
                        if r:
                            leave(u - 1, r - 1, None if first else 16 * i)
                    leave(i * GR + GR - 1, GR - 1, None if first else 16 * i)
                loop(act, body)
                for r in range(GR):
                    act.wait_ge(store[r], 16 * (GU // GR))


def dense_layers(nc, k, a, out, x_node):
    KC = HID // 128
    BW = 500
    with ExitStack() as tmp:
        nm = "d_"
        agg = sbuf(nc, tmp, nm + "agg", [T, NT, D])
        hT = sbuf(nc, tmp, nm + "hT", [D, N])
        h1 = sbuf(nc, tmp, nm + "h1", [128, KC, N])
        h2 = sbuf(nc, tmp, nm + "h2", [128, KC, N])
        w1 = sbuf(nc, tmp, nm + "w1", [D, HID])
        w2 = sbuf(nc, tmp, nm + "w2", [128, KC, HID])
        w3 = sbuf(nc, tmp, nm + "w3", [128, KC, D])
        b1 = sbuf(nc, tmp, nm + "b1", [128, KC])
        b2 = sbuf(nc, tmp, nm + "b2", [128, KC])
        b3 = sbuf(nc, tmp, nm + "b3", [T, D])
        o = sbuf(nc, tmp, nm + "o", [T, NT, D])
        y = sbuf(nc, tmp, nm + "y", [T, NT, D])
        sq = sbuf(nc, tmp, nm + "sq", [T, NT, D])
        mean, var, std = (sbuf(nc, tmp, nm + n, [T, NT]) for n in ("mean", "var", "std"))
        ps_t = [psum(nc, tmp, f"{nm}ps_t{i}") for i in range(2)]
        ps = [psum(nc, tmp, f"{nm}ps{i}") for i in range(4)]
        ps_o = [psum(nc, tmp, f"{nm}ps_o{i}") for i in range(2)]
        s = {n: semaphore(nc, k, nm + n) for n in (
            "load", "added", "turned", "copied", "product", "relu", "mm3", "out", "fin", "finb", "store")}
        gather = [semaphore(nc, k, f"{nm}gather{g}") for g in range(NT // TG)]
        blocks = [(n0, min(BW, N - n0)) for n0 in range(0, N, BW)]
        NBK = len(blocks)
        steps = [(1, 0)] + [st for b in range(1, NBK) for st in ((1, b), (2, b - 1))] + [(2, NBK - 1)]
        relus = lambda layer, b: KC * (steps.index((layer, b)) + 1)
        with nc.Block() as block:
            @block.gpsimd
            def _(pool):
                for t in range(NT):
                    pool.indirect_dma_start(agg[:, t, :], None, k.sum_d,
                                            bass.IndirectOffsetOnAxis(k.edge_idx[:, t:t + 1], 0)).then_inc(gather[t // TG], 16)
                for g in range(NT // TG):
                    pool.wait_ge(gather[g], 16 * TG)

            @block.sync
            def _(sp):
                ld = Dma(sp, s["load"])
                ld.start(w1[:], a["L1_gnn_W1"])
                ld.start(w2[:], a["L1_gnn_W2"].rearrange("(c p) f -> p c f", p=128))
                ld.start(w3[:], a["L1_gnn_W3"].rearrange("(c p) f -> p c f", p=128))
                ld.start(b1[:], a["L1_gnn_b1"].rearrange("(c p) -> p c", p=128), elements=True)
                ld.start(b2[:], a["L1_gnn_b2"].rearrange("(c p) -> p c", p=128), elements=True)
                ld.start(b3[:], bass.AP(a["L1_gnn_b3"].tensor, 0, [[0, T], [1, D]]))
                ld.wait()
                st = Dma(sp, s["store"])
                for g in range(NT // TG):
                    t = slice(g * TG, (g + 1) * TG)
                    sp.wait_ge(s["fin"], 8 * (g + 1))
                    st.start(out.rearrange("(p t) d -> p t d", t=NT)[:, t, :], y[:, t, :])
                st.wait()

            @block.vector
            def _(dve):
                for g in range(NT // TG):
                    t = slice(g * TG, (g + 1) * TG)
                    dve.wait_ge(gather[g], 16 * TG)
                    dve.tensor_tensor(agg[:, t, :], agg[:, t, :], x_node[:, t, :], ALU.add).then_inc(s["added"], 1)
                    for i in range(g * TG, (g + 1) * TG):
                        dve.wait_ge(s["turned"], i + 1)
                        dve.tensor_copy(hT[:, i * T:(i + 1) * T], ps_t[i % 2][0:D, 0:T]).then_inc(s["copied"], 1)
                dve.wait_ge(s["load"], 96)
                link = Link(dve, s["fin"])
                for g in range(NT // TG):
                    t = slice(g * TG, (g + 1) * TG)
                    dve.wait_ge(s["mm3"], TG * (g + 1))
                    dve.tensor_tensor(o[:, t, :], ps_o[g % 2][0:T, 0:TG * D].rearrange("p (t d) -> p t d", d=D),
                                      b3[:].unsqueeze(1).to_broadcast([T, TG, D]), ALU.add).then_inc(s["out"], 1)
                    dve.wait_ge(s["out"], g + 1)
                    layer_norm(dve, link, s["finb"], g, x_node[:, t, :], o[:, t, :], sq[:, t, :],
                               mean[:, t], var[:, t], std[:, t], y[:, t, :])

            @block.tensor
            def _(pe):
                def turn(t):
                    pe.wait_ge(s["added"], t // TG + 1)
                    if t >= 2:
                        pe.wait_ge(s["copied"], t - 1)
                    pe.transpose(ps_t[t % 2][0:D, 0:T], agg[:, t, :], k.ident[0:T, 0:T]).then_inc(s["turned"], 1)

                pe.wait_ge(s["load"], 96)
                turned, n = 0, 0
                for layer, b in steps:
                    n0, w = blocks[b]
                    if layer == 1:
                        while turned * T < n0 + w:
                            turn(turned)
                            turned += 1
                        pe.wait_ge(s["copied"], turned)
                    else:
                        pe.wait_ge(s["relu"], relus(1, b))
                    for c in range(KC):
                        if n >= 4:
                            pe.wait_ge(s["relu"], n - 3)
                        cols = slice(c * 128, (c + 1) * 128)
                        if layer == 1:
                            ins = pe.matmul(ps[n % 4][:, 0:w], w1[:, cols], hT[:, n0:n0 + w], start=True, stop=True)
                        else:
                            for kc in range(KC):
                                ins = pe.matmul(ps[n % 4][:, 0:w], w2[:, kc, cols], h1[:, kc, n0:n0 + w],
                                                start=(kc == 0), stop=(kc == KC - 1))
                        ins.then_inc(s["product"], 1)
                        n += 1
                pe.wait_ge(s["relu"], n)
                for t in range(NT):
                    g, i = t // TG, t % TG
                    if g >= 2:
                        pe.wait_ge(s["out"], g - 1)
                    for kc in range(KC):
                        ins = pe.matmul(ps_o[g % 2][0:T, i * D:(i + 1) * D], h2[:, kc, t * T:(t + 1) * T], w3[:, kc, :],
                                        start=(kc == 0), stop=(kc == KC - 1))
                    ins.then_inc(s["mm3"], 1)

            @block.scalar
            def _(act):
                act.wait_ge(s["load"], 96)
                n = 0
                for layer, b in steps:
                    n0, w = blocks[b]
                    h, bias = (h1, b1) if layer == 1 else (h2, b2)
                    for c in range(KC):
                        act.wait_ge(s["product"], n + 1)
                        act.activation(h[:, c, n0:n0 + w], ps[n % 4][:, 0:w], ACT.Relu,
                                       bias=bias[:, c:c + 1]).then_inc(s["relu"], 1)
                        n += 1
                for g in range(NT // TG):
                    t = slice(g * TG, (g + 1) * TG)
                    act.wait_ge(s["fin"], 8 * g + 6)
                    act.activation(std[:, t], var[:, t], ACT.Sqrt).then_inc(s["finb"], 1)


def build(nc, a, out):
    ctx = ExitStack()
    k = Program(ctx)
    k.setup = ExitStack()

    def dram(name, shape, dt=F32):
        return nc.dram_tensor(name, shape, dt, kind="Internal").ap()

    with ctx:
        k.key_d = dram("key_d", [G])
        k.w_d = dram("w_d", [UT])
        k.keys_d = dram("keys_d", [SLOTS + 1])
        k.lim_d = dram("lim_d", [SLOTS + 1])
        k.row_d = dram("row_d", [NW * WN], I32)
        k.last_d = dram("last_d", [G])
        k.same_d = dram("same_d", [E])
        k.xw_d = dram("xw_d", [UT, WN * D])
        k.sum_d = dram("sum_d", [T * G, D])
        k.x0_d, k.x1_d = dram("x0_d", [PAD, D]), dram("x1_d", [PAD, D])
        x0 = sbuf(nc, ctx, "x0", [T, NT, D])
        build_staircase(nc, k, a, ctx, x0)

        x1 = sbuf(nc, ctx, "x1", [T, NT, D])
        x1_d = k.x1_d[0:N, :]
        nodes = [x0, x1, x1]
        for n, H in enumerate((a["L0_gnn_att1"].shape[0], a["L0_gnn_att2"].shape[0])):
            nm = f"L{n + 1}_"
            lay = Layer(nm=nm, H=H, Wl=a[f"L0_gnn_W{n + 1}l"], Wr=a[f"L0_gnn_W{n + 1}r"],
                                  att=a[f"L0_gnn_att{n + 1}"], bias=a[f"L0_gnn_b{n + 1}"],
                                  x_node=nodes[n], x_pad=(k.x0_d, k.x1_d)[n], next_table=x1_d, next_node=nodes[n + 1],
                                  logit_d=dram(nm + "logit_d", [H, SLOTS]), norm=n == 1,
                                  v_d=dram(nm + "v_d", [UT * WN, H * XW]), max_d=dram(nm + "max_d", [T * UT, H]))
            if n == 0:
                before = set(k.sems)
            else:
                with nc.Block() as block:
                    old = [k.sems[name] for name in sorted(set(k.sems) - before) if not name.startswith("L1_")]
                    old += k.setup_sems.values()

                    @block.gpsimd
                    def _(pool):
                        for sem in old[0::4]:
                            pool.sem_clear(sem)

                    @block.vector
                    def _(dve):
                        for sem in old[1::4]:
                            dve.sem_clear(sem)

                    @block.scalar
                    def _(act):
                        for sem in old[2::4]:
                            act.sem_clear(sem)

                    @block.sync
                    def _(sp):
                        for sem in old[3::4]:
                            sp.sem_clear(sem)
                k.setup.close()
            with ExitStack() as lctx:
                if lay.norm:
                    lay.sq = sbuf(nc, lctx, nm + "sq", [T, NT, D])
                    lay.mean, lay.var, lay.std = (sbuf(nc, lctx, nm + v, [T, NT]) for v in ("mean", "var", "std"))
                    lay.fin_steps = 8

                    def finish(dve, link, finb, o, lay=lay):
                        layer_norm(dve, link, finb, 0, x0[:], o[:], lay.sq[:], lay.mean[:], lay.var[:], lay.std[:],
                                   lay.next_node[:])
                else:
                    lay.fin_steps = 1

                    def finish(dve, link, finb, o, lay=lay):
                        link(dve.tensor_scalar(lay.next_node[:], o[:], 0.0, None, ALU.max))
                lay.node_max = sbuf(nc, lctx, nm + "node_max", [T, NT, H])
                lay.self_logit = sbuf(nc, lctx, nm + "self_logit", [T, NT, H])
                lay.xs_d = dram(nm + "xs_d", [U, T, Q * lay.XR])
                with ExitStack() as ectx:
                    lay.a_edge = sbuf(nc, ectx, nm + "a_edge", [T, UT, H])
                    lay.m_edge = sbuf(nc, ectx, nm + "m_edge", [T, UT, H])
                    lay.lin_edge = lay.a_edge
                    lay.lim = sbuf(nc, ectx, nm + "lim", [CH, SLOTS // (CH // H) + 1])
                    lay.lim_loaded = semaphore(nc, k, "lim_loaded")
                    with ExitStack() as wctx:
                        prepare_layer(nc, k, ectx, wctx, lay)
                        edge_logits(nc, k, lay)
                    edge_softmax(nc, k, lay)
                    edge_sums(nc, k, lay)
                merge_nodes(nc, k, lay, finish)
        neighbour_sums(nc, k, x1_d)
        dense_layers(nc, k, a, out, x1)


_INS = ["x", "src", "dst", "L0_gnn_W1l", "L0_gnn_W1r", "L0_gnn_att1", "L0_gnn_b1", "L0_gnn_W2l", "L0_gnn_W2r",
        "L0_gnn_att2", "L0_gnn_b2", "L1_gnn_W1", "L1_gnn_b1", "L1_gnn_W2", "L1_gnn_b2", "L1_gnn_W3", "L1_gnn_b3"]


def kernel(**inputs):
    import numpy as np
    import concourse.bacc as bacc
    from concourse import mybir as _mybir
    from concourse.bass_utils import run_bass_kernel_spmd

    nc = bacc.Bacc("TRN2", target_bir_lowering=False, num_devices=1)
    arrays, args = {}, {}
    for name in _INS:
        arr = np.ascontiguousarray(inputs[name])
        arrays[f"in_{name}_dram"] = arr
        args[name] = nc.dram_tensor(f"in_{name}_dram", arr.shape, _mybir.dt.from_np(arr.dtype),
                                    kind="ExternalInput").ap()
    out = nc.dram_tensor("out_dram", (N, D), _mybir.dt.float32, kind="ExternalOutput").ap()
    build(nc, args, out)
    r = run_bass_kernel_spmd(nc, [arrays], core_ids=[0])
    return r.results[0]["out_dram"]
```
